# Optimizing a Trainium2 kernel written in Bass

```python
import numpy as np
import jax
import jax.numpy as jnp

def _softmax(x, axis=-1):
    return jax.nn.softmax(x, axis=axis)

def _gelu(x):
    return jax.nn.gelu(x, approximate=True)

def _silu(x):
    return jax.nn.silu(x)

def _sigmoid(x):
    return jax.nn.sigmoid(x)

def _layernorm(x, axis=-1, eps=1e-05):
    m = jnp.mean(x, axis=axis, keepdims=True)
    v = jnp.var(x, axis=axis, keepdims=True)
    return (x - m) / jnp.sqrt(v + eps)

def _scatter_add(tgt, idx, src, axis=0):
    return tgt.at[idx].add(src)

def _segment_sum(src, seg, n):
    return jax.ops.segment_sum(src, seg, n)
kernel_name = 'mk_gnn_preln_d2_gnn_r64_0e9eaa'

def setup_inputs(seed: int=0):
    np.random.seed(seed)
    _w = jnp.asarray

    def _rec_inputs():
        import jax
        import jax.numpy as jnp
        _gk = jax.random.key(seed)
        x = -0.000202 + 1 * jax.random.normal(jax.random.fold_in(_gk, 1), (100000, 128), jnp.float32)
        src = jax.random.randint(jax.random.fold_in(_gk, 2), (50000,), 0, 100000, jnp.int32)
        dst = jnp.minimum((100000 * jax.random.uniform(jax.random.fold_in(_gk, 3), (50000,)) ** 2.0).astype(jnp.int32), 99999)
        _o = jnp.argsort(dst, stable=True)
        src = src[_o]
        dst = dst[_o]
        edge_attr_4 = 0.000714719 + 1.00021 * jax.random.normal(jax.random.fold_in(_gk, 11), (50000, 4), jnp.float32)
        return (x, src, dst, edge_attr_4)
    x, src, dst, edge_attr_4 = _rec_inputs()

    def _L0_gnn_setup():
        import jax, jax.numpy as jnp
        import numpy as np
        N = 50000
        E = 12500
        IN_C = 128
        OUT_C = 128
        HEADS = 8
        BASES = 4
        N_AGG = 4
        HEAD_D = OUT_C // HEADS

        def _egc_forward(x, edge_index, bases_W, comb_W, comb_b, bias):
            n = x.shape[0]
            row, col = (edge_index[0], edge_index[1])
            bases = jnp.einsum('nc,bcd->nbd', x, bases_W).reshape(n, BASES * HEAD_D)
            msgs = bases[row]
            ones_e = jnp.ones((row.shape[0],), dtype=x.dtype)
            cnt = jax.ops.segment_sum(ones_e, col, num_segments=n)
            cnt_c = jnp.maximum(cnt, 1.0)[:, None]
            loops = jnp.arange(n, dtype=row.dtype)
            row_sl = jnp.concatenate([row, loops])
            col_sl = jnp.concatenate([col, loops])
            deg = jax.ops.segment_sum(jnp.ones((row_sl.shape[0],), dtype=x.dtype), col_sl, num_segments=n)
            dinv = jnp.where(deg > 0, jax.lax.rsqrt(deg), 0.0)
            norm = dinv[row_sl] * dinv[col_sl]
            symadd = jax.ops.segment_sum(norm[:, None] * bases[row_sl], col_sl, num_segments=n)
            s = jax.ops.segment_sum(msgs, col, num_segments=n)
            mean = s / cnt_c
            mx = jax.ops.segment_max(msgs, col, num_segments=n)
            mx = jnp.where(cnt[:, None] > 0, mx, 0.0)
            mean_sq = jax.ops.segment_sum(msgs * msgs, col, num_segments=n) / cnt_c
            var = mean_sq - mean * mean
            std = jnp.sqrt(jax.nn.relu(var) + 1e-05)
            aggs = jnp.stack([a.reshape(n, BASES, HEAD_D) for a in (symadd, mean, mx, std)], axis=2)
            w = x @ comb_W + comb_b
            w = jax.nn.softmax(w.reshape(n, HEADS, BASES * N_AGG), axis=-1)
            w = w.reshape(n, HEADS, BASES, N_AGG)
            z = jnp.einsum('nhba,nbad->nhd', w, aggs).reshape(n, OUT_C)
            return z + bias
        key = jax.random.key(seed)
        k1, k2, k3, k4, k5 = jax.random.split(key, 5)
        x = jax.random.normal(k1, (N, IN_C), dtype=jnp.float32)
        edge_index = jax.random.randint(k2, (2, E), 0, N, dtype=jnp.int64)
        glorot_scale = np.sqrt(6.0 / (IN_C + HEAD_D))
        bases_W = jax.random.uniform(k3, (BASES, IN_C, HEAD_D), dtype=jnp.float32, minval=-glorot_scale, maxval=glorot_scale)
        fan = IN_C
        lim = np.sqrt(1.0 / fan)
        comb_W = jax.random.uniform(k4, (IN_C, HEADS * BASES * N_AGG), dtype=jnp.float32, minval=-lim, maxval=lim)
        comb_b = jax.random.uniform(k5, (HEADS * BASES * N_AGG,), dtype=jnp.float32, minval=-lim, maxval=lim)
        bias = jnp.zeros((OUT_C,), dtype=jnp.float32)
        return {'x': x, 'edge_index': edge_index, 'bases_W': bases_W, 'comb_W': comb_W, 'comb_b': comb_b, 'bias': bias}
    _L0_gnn_all = _L0_gnn_setup()
    _L0_gnn_in = {k: v for k, v in _L0_gnn_all.items() if k in ('bases_W', 'comb_W', 'comb_b', 'bias')}
    del _L0_gnn_all

    def _L1_gnn_setup():
        import jax, jax.numpy as jnp
        import numpy as np
        N_NODES = 50000
        N_EDGES = 12500
        HIDDEN = 128
        HEADS = 4
        HEAD_DIM = HIDDEN // HEADS
        EDGE_DIM = 4
        LN_EPS = 1e-05

        def _layer_norm(x, g, b):
            mu = jnp.mean(x, axis=-1, keepdims=True)
            var = jnp.mean(jnp.square(x - mu), axis=-1, keepdims=True)
            return (x - mu) * jax.lax.rsqrt(var + LN_EPS) * g + b
        key = jax.random.key(seed)
        ks = jax.random.split(key, 20)
        s = 0.02

        def w(k, shape):
            return jax.random.normal(k, shape, dtype=jnp.float32) * s
        return {'x': jax.random.normal(ks[0], (N_NODES, HIDDEN), dtype=jnp.float32), 'edge_index': jax.random.randint(ks[1], (2, N_EDGES), 0, N_NODES, dtype=jnp.int32), 'edge_attr': jax.random.normal(ks[2], (N_EDGES, EDGE_DIM), dtype=jnp.float32), 'ln1_g': jnp.ones((HIDDEN,), jnp.float32), 'ln1_b': jnp.zeros((HIDDEN,), jnp.float32), 'Wq': w(ks[3], (HIDDEN, HIDDEN)), 'bq': jnp.zeros((HIDDEN,), jnp.float32), 'Wk': w(ks[4], (HIDDEN, HIDDEN)), 'bk': jnp.zeros((HIDDEN,), jnp.float32), 'Wv': w(ks[5], (HIDDEN, HIDDEN)), 'bv': jnp.zeros((HIDDEN,), jnp.float32), 'We': w(ks[6], (EDGE_DIM, HIDDEN)), 'Wskip': w(ks[7], (HIDDEN, HIDDEN)), 'bskip': jnp.zeros((HIDDEN,), jnp.float32), 'Wbeta': w(ks[8], (3 * HIDDEN, 1)), 'ln2_g': jnp.ones((HIDDEN,), jnp.float32), 'ln2_b': jnp.zeros((HIDDEN,), jnp.float32), 'W1': w(ks[9], (HIDDEN, 4 * HIDDEN)), 'b1': jnp.zeros((4 * HIDDEN,), jnp.float32), 'W2': w(ks[10], (4 * HIDDEN, HIDDEN)), 'b2': jnp.zeros((HIDDEN,), jnp.float32)}
    _L1_gnn_all = _L1_gnn_setup()
    _L1_gnn_in = {k: v for k, v in _L1_gnn_all.items() if k in ('ln1_g', 'ln1_b', 'Wq', 'bq', 'Wk', 'bk', 'Wv', 'bv', 'We', 'Wskip', 'bskip', 'Wbeta', 'ln2_g', 'ln2_b', 'W1', 'b1', 'W2', 'b2')}
    del _L1_gnn_all
    return {'x': x, 'src': src, 'dst': dst, 'edge_attr_4': edge_attr_4, 'L0_gnn_bases_W': _L0_gnn_in['bases_W'], 'L0_gnn_comb_W': _L0_gnn_in['comb_W'], 'L0_gnn_comb_b': _L0_gnn_in['comb_b'], 'L0_gnn_bias': _L0_gnn_in['bias'], 'L1_gnn_ln1_g': _L1_gnn_in['ln1_g'], 'L1_gnn_ln1_b': _L1_gnn_in['ln1_b'], 'L1_gnn_Wq': _L1_gnn_in['Wq'], 'L1_gnn_bq': _L1_gnn_in['bq'], 'L1_gnn_Wk': _L1_gnn_in['Wk'], 'L1_gnn_bk': _L1_gnn_in['bk'], 'L1_gnn_Wv': _L1_gnn_in['Wv'], 'L1_gnn_bv': _L1_gnn_in['bv'], 'L1_gnn_We': _L1_gnn_in['We'], 'L1_gnn_Wskip': _L1_gnn_in['Wskip'], 'L1_gnn_bskip': _L1_gnn_in['bskip'], 'L1_gnn_Wbeta': _L1_gnn_in['Wbeta'], 'L1_gnn_ln2_g': _L1_gnn_in['ln2_g'], 'L1_gnn_ln2_b': _L1_gnn_in['ln2_b'], 'L1_gnn_W1': _L1_gnn_in['W1'], 'L1_gnn_b1': _L1_gnn_in['b1'], 'L1_gnn_W2': _L1_gnn_in['W2'], 'L1_gnn_b2': _L1_gnn_in['b2']}

def reference(x, src, dst, edge_attr_4, L0_gnn_bases_W, L0_gnn_comb_W, L0_gnn_comb_b, L0_gnn_bias, L1_gnn_ln1_g, L1_gnn_ln1_b, L1_gnn_Wq, L1_gnn_bq, L1_gnn_Wk, L1_gnn_bk, L1_gnn_Wv, L1_gnn_bv, L1_gnn_We, L1_gnn_Wskip, L1_gnn_bskip, L1_gnn_Wbeta, L1_gnn_ln2_g, L1_gnn_ln2_b, L1_gnn_W1, L1_gnn_b1, L1_gnn_W2, L1_gnn_b2):
    import jax
    import jax.numpy as jnp

    def _L0_gnn_ref(x, edge_index, bases_W, comb_W, comb_b, bias):
        import jax, jax.numpy as jnp
        import numpy as np
        N = 50000
        E = 12500
        IN_C = 128
        OUT_C = 128
        HEADS = 8
        BASES = 4
        N_AGG = 4
        HEAD_D = OUT_C // HEADS

        def _egc_forward(x, edge_index, bases_W, comb_W, comb_b, bias):
            n = x.shape[0]
            row, col = (edge_index[0], edge_index[1])
            bases = jnp.einsum('nc,bcd->nbd', x, bases_W).reshape(n, BASES * HEAD_D)
            msgs = bases[row]
            ones_e = jnp.ones((row.shape[0],), dtype=x.dtype)
            cnt = jax.ops.segment_sum(ones_e, col, num_segments=n)
            cnt_c = jnp.maximum(cnt, 1.0)[:, None]
            loops = jnp.arange(n, dtype=row.dtype)
            row_sl = jnp.concatenate([row, loops])
            col_sl = jnp.concatenate([col, loops])
            deg = jax.ops.segment_sum(jnp.ones((row_sl.shape[0],), dtype=x.dtype), col_sl, num_segments=n)
            dinv = jnp.where(deg > 0, jax.lax.rsqrt(deg), 0.0)
            norm = dinv[row_sl] * dinv[col_sl]
            symadd = jax.ops.segment_sum(norm[:, None] * bases[row_sl], col_sl, num_segments=n)
            s = jax.ops.segment_sum(msgs, col, num_segments=n)
            mean = s / cnt_c
            mx = jax.ops.segment_max(msgs, col, num_segments=n)
            mx = jnp.where(cnt[:, None] > 0, mx, 0.0)
            mean_sq = jax.ops.segment_sum(msgs * msgs, col, num_segments=n) / cnt_c
            var = mean_sq - mean * mean
            std = jnp.sqrt(jax.nn.relu(var) + 1e-05)
            aggs = jnp.stack([a.reshape(n, BASES, HEAD_D) for a in (symadd, mean, mx, std)], axis=2)
            w = x @ comb_W + comb_b
            w = jax.nn.softmax(w.reshape(n, HEADS, BASES * N_AGG), axis=-1)
            w = w.reshape(n, HEADS, BASES, N_AGG)
            z = jnp.einsum('nhba,nbad->nhd', w, aggs).reshape(n, OUT_C)
            return z + bias
        return _egc_forward(x, edge_index, bases_W, comb_W, comb_b, bias)

    def _L1_gnn_ref(x, edge_index, edge_attr, ln1_g, ln1_b, Wq, bq, Wk, bk, Wv, bv, We, Wskip, bskip, Wbeta, ln2_g, ln2_b, W1, b1, W2, b2):
        import jax, jax.numpy as jnp
        import numpy as np
        N_NODES = 50000
        N_EDGES = 12500
        HIDDEN = 128
        HEADS = 4
        HEAD_DIM = HIDDEN // HEADS
        EDGE_DIM = 4
        LN_EPS = 1e-05

        def _layer_norm(x, g, b):
            mu = jnp.mean(x, axis=-1, keepdims=True)
            var = jnp.mean(jnp.square(x - mu), axis=-1, keepdims=True)
            return (x - mu) * jax.lax.rsqrt(var + LN_EPS) * g + b
        N, Hd = x.shape
        heads, d = (HEADS, Hd // HEADS)
        src, dst = (edge_index[0], edge_index[1])
        xn = _layer_norm(x, ln1_g, ln1_b)
        q = (xn @ Wq + bq).reshape(N, heads, d)
        k = (xn @ Wk + bk).reshape(N, heads, d)
        v = (xn @ Wv + bv).reshape(N, heads, d)
        e = (edge_attr @ We).reshape(-1, heads, d)
        kj = k[src] + e
        vj = v[src] + e
        alpha = jnp.sum(q[dst] * kj, axis=-1) * (1.0 / np.sqrt(d))
        m = jax.ops.segment_max(alpha, dst, num_segments=N)
        p = jnp.exp(alpha - m[dst])
        denom = jax.ops.segment_sum(p, dst, num_segments=N)
        attn = p / (denom[dst] + 1e-16)
        out = jax.ops.segment_sum(attn[..., None] * vj, dst, num_segments=N)
        out = out.reshape(N, Hd)
        x_r = xn @ Wskip + bskip
        beta = jax.nn.sigmoid(jnp.concatenate([out, x_r, out - x_r], axis=-1) @ Wbeta)
        h = beta * x_r + (1.0 - beta) * out
        x = x + h
        x2 = _layer_norm(x, ln2_g, ln2_b)
        h2 = jax.nn.relu(x2 @ W1 + b1) @ W2 + b2
        return x + h2
    edge_index = jnp.stack([src, dst])
    h = jnp.maximum(_layernorm(x, axis=-1), 0.0)
    x = x + _L0_gnn_ref(h, edge_index, L0_gnn_bases_W, L0_gnn_comb_W, L0_gnn_comb_b, L0_gnn_bias)
    h = jnp.maximum(_layernorm(x, axis=-1), 0.0)
    x = x + _L1_gnn_ref(h, edge_index, edge_attr_4, L1_gnn_ln1_g, L1_gnn_ln1_b, L1_gnn_Wq, L1_gnn_bq, L1_gnn_Wk, L1_gnn_bk, L1_gnn_Wv, L1_gnn_bv, L1_gnn_We, L1_gnn_Wskip, L1_gnn_bskip, L1_gnn_Wbeta, L1_gnn_ln2_g, L1_gnn_ln2_b, L1_gnn_W1, L1_gnn_b1, L1_gnn_W2, L1_gnn_b2)
    return x

_drawn_inputs = setup_inputs


def setup_inputs(seed=0):
    import zlib

    import numpy as np

    out = dict(_drawn_inputs(seed))
    spreads = {'L0_gnn_bias': (0.0, 0.1),
     'L1_gnn_ln1_g': (1.0, 0.6),
     'L1_gnn_ln1_b': (0.0, 0.8),
     'L1_gnn_bq': (0.0, 0.8),
     'L1_gnn_bk': (0.0, 0.8),
     'L1_gnn_bv': (0.0, 0.442),
     'L1_gnn_bskip': (0.0, 0.282),
     'L1_gnn_ln2_g': (1.0, 0.6),
     'L1_gnn_ln2_b': (0.0, 0.8),
     'L1_gnn_b1': (0.0, 0.422),
     'L1_gnn_b2': (0.0, 0.1)}
    factors = {'edge_attr_4': 7.796,
     'L0_gnn_comb_b': 7.679,
     'L1_gnn_Wq': 8.0,
     'L1_gnn_Wk': 8.0,
     'L1_gnn_We': 7.888,
     'L1_gnn_Wbeta': 8.0}
    for name, (base, spread) in spreads.items():
        noise = np.random.default_rng([zlib.crc32(name.encode()), seed]).standard_normal(out[name].shape)
        drawn = base * np.exp(spread * noise) if base else spread * noise
        out[name] = jnp.asarray(drawn.astype(out[name].dtype))
    for name, factor in factors.items():
        out[name] = (out[name] * factor).astype(out[name].dtype)
    return out
```

```python
from contextlib import ExitStack

import concourse.bass as bass
from concourse import mybir

ALU = mybir.AluOpType
ACT = mybir.ActivationFunctionType
F32 = mybir.dt.float32
F16 = mybir.dt.float16
BF16 = mybir.dt.bfloat16
I32 = mybir.dt.int32
AX_X = mybir.AxisListType.X

P = 128
TILES = 4
GROUP = P * TILES
C = 128
EPS = 1e-5
NOWHERE = 1 << 20
HUGE = 3.0e38

HEADS0, BASES, AGGS = 8, 4, 4
D0 = C // HEADS0
BD = BASES * D0
MIX = BASES * AGGS
AGG_ORDER = (1, 0, 3, 2)
HEADS1 = 4
D1 = C // HEADS1
EDGE_C = 4
HID = 4 * C


def after(g, n):
    return not isinstance(g, int) or g >= n


def skewed(eng, count, *stages, peel=0):
    deepest = max(lag for _, lag in stages)
    head = 2 * ((deepest + 3) // 2)
    for t in range(head):
        for stage, lag in stages:
            if 0 <= t - lag < count:
                stage(t - lag, (t - lag) % 2, (t - lag) // 2)
    pairs = max(0, (count - peel - head) // 2)
    if pairs:
        with eng.Fori(0, pairs) as k:
            for u in range(2):
                for stage, lag in stages:
                    slot = (u - lag) % 2
                    turn = k + (head + u - lag - slot) // 2
                    stage(turn * 2 + slot, slot, turn)
    for t in range(head + 2 * pairs, count + deepest):
        for stage, lag in stages:
            if 0 <= t - lag < count:
                stage(t - lag, (t - lag) % 2, (t - lag) // 2)


def row_of(vec):
    return vec.rearrange("(o n) -> o n", o=1).to_broadcast([P, vec.shape[0]])


def fold(ap):
    return ap.rearrange("p a b -> p (a b)")


def spread(ap, n):
    return ap.rearrange("p (a o) -> p a o", o=1).to_broadcast([ap.shape[0], ap.shape[1], n])


def over(ap, n):
    return ap.rearrange("p (o a) -> p o a", o=1).to_broadcast([ap.shape[0], n, ap.shape[1]])


class Scope:

    def __init__(self, nc, ctx, tag):
        self.nc, self.ctx, self.tag = nc, ctx, tag
        self.sems = []

    def sb(self, name, shape, dt=F32):
        return self.ctx.enter_context(self.nc.sbuf_tensor(f"{self.tag}_{name}", list(shape), dt))

    def ps(self, name, shape, dt=F32):
        return self.ctx.enter_context(self.nc.psum_tensor(f"{self.tag}_ps_{name}", list(shape), dt))

    def sem(self, name):
        self.sems.append(self.ctx.enter_context(self.nc.semaphore(f"{self.tag}_{name}")))
        return self.sems[-1]

    def clear(self):
        for sem in self.sems:
            self.nc.sync.sem_clear(sem)

    def block(self):
        self.ctx.callback(self.clear)
        return self.ctx.enter_context(self.nc.Block())


def prepare(nc, shape, keep, dram, src, dst):
    N, E, GE, GN = shape
    HB = GN // 2
    with ExitStack() as ctx:
        m = Scope(nc, ctx, "pre")
        dst_i = m.sb("dst_i", [GE, GROUP], I32)
        src_i = m.sb("src_i", [GE, GROUP], I32)
        part_i = m.sb("part_i", [GE, 2, GROUP], I32)
        edge_i = m.sb("edge_i", [GE, 2], I32)
        edge_f = m.sb("edge_f", [GE, 2])
        dst_f = m.sb("dst_f", [GE, GROUP])
        same = m.sb("same", [GE, GROUP])
        same_next = m.sb("same_next", [GE, 1])
        cols = m.sb("cols", [GE, 5, GROUP])
        place_i = m.sb("place_i", [GE, GROUP], I32)
        place = m.sb("place", [GE, GROUP])
        begin = m.sb("begin", [GE, GROUP])
        zero_row = m.sb("zero_row", [GE, GROUP])
        begin_row = m.sb("begin_row", [1, GE + 1])
        factor = m.sb("factor", [GE, 2, GROUP])
        parts = m.sb("parts", [P, 2, TILES * GE])
        zeros = m.sb("zeros", [P, 3584])
        count_i = m.sb("count_i", [P, GROUP], I32)
        ramp = m.sb("ramp", [P, GROUP], F16)
        hot = m.sb("hot", [P, 2, TILES, GROUP + GN], BF16)
        counts = m.sb("counts", [HB, 2, GROUP])
        degree = m.sb("degree", [HB, 2, GROUP])
        dinv = m.sb("dinv", [HB, 2, GROUP])
        turned = [m.ps(f"turned{i}", [P, TILES * GE]) for i in range(5)]
        hist = [m.ps(f"hist{i}", [HB, GROUP]) for i in range(2)]
        s_blank, s_load, s_zero, s_fill = m.sem("blank"), m.sem("load"), m.sem("zero"), m.sem("fill")
        s_id, s_iota, s_ramp, s_chain = m.sem("id"), m.sem("iota"), m.sem("ramp"), m.sem("chain")
        s_last, s_carry, s_runs, s_runroot = m.sem("last"), m.sem("carry"), m.sem("runs"), m.sem("runroot")
        s_same, s_cols, s_turned, s_parts = m.sem("same"), m.sem("cols"), m.sem("turned"), m.sem("parts")
        s_hot, s_hist, s_counts, s_root = m.sem("hot"), m.sem("hist"), m.sem("counts"), m.sem("root")
        s_dinv, s_store, s_node, s_taken = m.sem("dinv"), m.sem("store"), m.sem("node"), m.sem("taken")
        full = (GE - 1) * GROUP
        table = GN * GROUP * C // P
        fills = []
        at = 0
        while at < table:
            fills.append((at, min(3584, table - at)))
            at += 3584
        block = m.block()

        @block.sync
        def _(sp):
            sp.wait_ge(s_blank, 3)
            sp.dma_start(dst_i[0:GE - 1, :], dst[0:full].rearrange("(g c) -> g c", c=GROUP)).then_inc(s_load, 16)
            sp.dma_start(dst_i[GE - 1:GE, 0:E - full], dst[full:E].rearrange("(o c) -> o c", o=1)).then_inc(s_load, 16)
            sp.dma_start(src_i[0:GE - 1, :], src[0:full].rearrange("(g c) -> g c", c=GROUP)).then_inc(s_load, 16)
            sp.dma_start(src_i[GE - 1:GE, 0:E - full], src[full:E].rearrange("(o c) -> o c", o=1)).then_inc(s_load, 16)
            sp.dma_start(edge_i[1:GE, 0:1], dst[0:full].rearrange("(g c) -> g c", c=GROUP)[:, GROUP - 1:GROUP], allow_slow_non_contiguous=True).then_inc(s_load, 16)
            sp.dma_start(edge_i[0:GE - 2, 1:2], dst[GROUP:full].rearrange("(g c) -> g c", c=GROUP)[:, 0:1], allow_slow_non_contiguous=True).then_inc(s_load, 16)
            sp.dma_start(edge_i[GE - 2:GE - 1, 1:2], dst[full:full + 1].rearrange("(o c) -> o c", o=1)).then_inc(s_load, 16)
            sp.wait_ge(s_zero, 1)
            for name in ("mixed", "attended"):
                rows = dram[name].rearrange("(p r) c -> p (r c)", p=P)
                for a, n in fills:
                    sp.dma_start(rows[:, a:a + n], zeros[:, 0:n]).then_inc(s_fill, 16)
            sp.wait_ge(s_same, 1)
            sp.dma_start(dram["same"], same[:, :]).then_inc(s_store, 16)
            sp.wait_ge(s_runs, 3)
            sp.dma_start(dram["factor"].rearrange("g k c -> g (k c)"), factor[:, :, :].rearrange("g k c -> g (k c)")).then_inc(s_store, 16)
            sp.wait_ge(s_dinv, 1)
            sp.dma_start(dram["dinv"].rearrange("(b g c) o -> g b (c o)", b=2, c=GROUP), dinv[:, :, :]).then_inc(s_store, 16)
            sp.wait_ge(s_store, 48)
            sp.wait_ge(s_fill, 16 * 2 * len(fills))

        @block.gpsimd
        def _(pool):
            pool.iota(count_i[:, :], pattern=[[1, GROUP]], base=0, channel_multiplier=0).then_inc(s_iota, 1)
            pool.iota(place_i[:, :], pattern=[[1, GROUP]], base=0, channel_multiplier=GROUP).then_inc(s_iota, 1)
            pool.memset(keep["ident"][:, :], 0.0).then_inc(s_id, 1)
            pool.wait_ge(s_id, 1)
            pool.affine_select(out=keep["ident"][:, :], in_=keep["ident"][:, :], compare_op=ALU.not_equal, fill=1.0,
                               base=0, pattern=[[-1, P]], channel_multiplier=1).then_inc(s_id, 1)

        @block.scalar
        def _(act):
            act.wait_ge(s_runs, 1)
            act.activation(factor[:, 1, :], factor[:, 0, :], ACT.Sqrt, bias=keep["one"][0:GE, :]).then_inc(s_runroot, 1)
            act.wait_ge(s_counts, 2)
            act.activation(dinv[:, :, :], degree[:, :, :], ACT.Sqrt).then_inc(s_root, 1)

        @block.vector
        def _(v):
            done = [0]

            def chain(instruction):
                done[0] += 1
                instruction.then_inc(s_chain, 1)
                v.wait_ge(s_chain, done[0])

            v.memset(dst_i[:, :], NOWHERE).then_inc(s_blank, 1)
            v.memset(src_i[:, :], 0).then_inc(s_blank, 1)
            v.memset(edge_i[:, 0:1], -1)
            v.memset(edge_i[:, 1:2], NOWHERE).then_inc(s_blank, 1)
            v.memset(zeros[:, :], 0.0).then_inc(s_zero, 1)
            v.memset(keep["eps"][:, :], EPS)
            v.memset(keep["one"][:, :], 1.0)
            v.memset(zero_row[:, :], 0.0)
            v.wait_ge(s_iota, 2)
            v.tensor_copy(ramp[:, :], count_i[:, :]).then_inc(s_ramp, 1)
            v.wait_ge(s_load, 16 * 7)
            v.tensor_copy(edge_f[:, :], edge_i[:, :])
            v.tensor_copy(cols[:, 0, :], src_i[:, :])
            v.tensor_scalar(part_i[:, 0, :], dst_i[:, :], 9, None, ALU.logical_shift_right)
            v.tensor_scalar(part_i[:, 1, :], dst_i[:, :], GROUP - 1, None, ALU.bitwise_and)
            chain(v.tensor_copy(dst_f[:, :], dst_i[:, :]))
            v.tensor_copy(cols[:, 3:5, :], part_i[:, :, :])
            v.tensor_scalar(cols[:, 1, :], dst_f[:, :], float(N - 1), None, ALU.min)
            v.tensor_tensor(same[:, 1:GROUP], dst_f[:, 1:GROUP], dst_f[:, 0:GROUP - 1], ALU.is_equal)
            v.tensor_tensor(same[:, 0:1], dst_f[:, 0:1], edge_f[:, 0:1], ALU.is_equal).then_inc(s_same, 1)
            chain(v.tensor_tensor(same_next[:, :], dst_f[:, GROUP - 1:GROUP], edge_f[:, 1:2], ALU.is_equal))
            v.scalar_tensor_tensor(out=cols[:, 2, 0:GROUP - 1], in0=same[:, 1:GROUP], scalar=float(NOWHERE),
                                   in1=dst_f[:, 0:GROUP - 1], op0=ALU.mult, op1=ALU.max)
            v.scalar_tensor_tensor(out=cols[:, 2, GROUP - 1:GROUP], in0=same_next[:, :], scalar=float(NOWHERE),
                                   in1=dst_f[:, GROUP - 1:GROUP], op0=ALU.mult, op1=ALU.max).then_inc(s_cols, 1)
            chain(v.tensor_scalar(begin[:, :], same[:, :], -1.0, 1.0, ALU.mult, ALU.add))
            chain(v.tensor_copy(place[:, :], place_i[:, :]))
            chain(v.tensor_tensor(begin[:, :], begin[:, :], place[:, :], ALU.mult))
            v.tensor_tensor_scan(begin[:, :], zero_row[:, :], begin[:, :], 0.0, ALU.add, ALU.max).then_inc(s_last, 1)
            v.wait_ge(s_carry, 1)
            v.memset(begin_row[:, 0:1], 0.0)
            v.tensor_tensor_scan(begin_row[:, 1:GE + 1], zero_row[0:1, 0:GE], turned[0][0:1, 0:GE], 0.0, ALU.add, ALU.max).then_inc(s_last, 1)
            v.wait_ge(s_carry, 2)
            chain(v.tensor_scalar(begin[:, :], begin[:, :], turned[1][0:GE, 0:1], None, ALU.max))
            chain(v.tensor_tensor(factor[:, 0, :], place[:, :], begin[:, :], ALU.subtract))
            v.tensor_scalar(factor[:, 0, :], factor[:, 0, :], 1.0, None, ALU.add).then_inc(s_runs, 1)
            v.wait_ge(s_runroot, 1)
            v.reciprocal(factor[:, :, :], factor[:, :, :]).then_inc(s_runs, 2)
            for i in range(3):
                v.wait_ge(s_turned, i + 1)
                v.tensor_copy(keep["index"][:, i, :], turned[i][:, :])
            for i in range(2):
                v.wait_ge(s_turned, i + 4)
                last = v.tensor_copy(parts[:, i, :], turned[3 + i][:, :])
            last.then_inc(s_parts, 1)
            v.wait_ge(s_parts, 1)
            v.wait_ge(s_ramp, 1)

            def one_hot(g, slot, turn):
                if after(g, 2):
                    v.wait_ge(s_hist, g - 1)
                for j in range(TILES):
                    v.tensor_scalar(hot[:, slot, j, 0:GROUP], ramp[:, :], parts[:, 1, bass.ds(g + j * GE, 1)], None, ALU.is_equal)
                    last = v.tensor_scalar(hot[:, slot, j, GROUP:GROUP + GN], ramp[:, 0:GN],
                                           parts[:, 0, bass.ds(g + j * GE, 1)], None, ALU.is_equal)
                last.then_inc(s_hot, 1)

            skewed(v, GE, (one_hot, 0))
            v.wait_ge(s_hist, GE)
            for b in range(2):
                v.tensor_copy(counts[:, b, :], hist[b][:, :])
                last = v.tensor_scalar(degree[:, b, :], hist[b][:, :], 1.0, None, ALU.add)
            last.then_inc(s_counts, 2)
            v.wait_ge(s_root, 1)
            v.reciprocal(dinv[:, :, :], dinv[:, :, :]).then_inc(s_dinv, 1)
            for j in range(TILES):
                v.wait_ge(s_node, j + 1)
                taken = turned[j][:, 0:GN]
                chain(v.tensor_scalar(keep["selfw"][:, j, :], taken, 1.0, None, ALU.add))
                v.reciprocal(keep["selfw"][:, j, :], keep["selfw"][:, j, :])
                v.tensor_scalar(keep["lonew"][:, j, :], taken, 0.0, float(EPS) ** 0.5, ALU.is_equal, ALU.mult).then_inc(s_taken, 1)

        @block.tensor
        def _(pe):
            ident = keep["ident"]
            pe.wait_ge(s_id, 2)
            pe.wait_ge(s_last, 1)
            pe.transpose(turned[0][0:1, 0:GE], begin[:, GROUP - 1:GROUP], ident[0:GE, 0:GE]).then_inc(s_carry, 1)
            pe.wait_ge(s_last, 2)
            pe.transpose(turned[1][0:GE, 0:1], begin_row[:, 0:GE], ident[0:1, 0:1]).then_inc(s_carry, 1)
            pe.wait_ge(s_runs, 1)
            pe.wait_ge(s_cols, 1)
            for i in range(5):
                for j in range(TILES):
                    last = pe.transpose(turned[i][:, j * GE:(j + 1) * GE], cols[:, i, j * P:(j + 1) * P], ident[0:GE, 0:GE])
                last.then_inc(s_turned, 1)

            def histogram(g, slot, turn):
                pe.wait_ge(s_hot, g + 1)
                for j in range(TILES):
                    first = isinstance(g, int) and g == 0 and j == 0
                    final = isinstance(g, int) and g == GE - 1 and j == TILES - 1
                    for b in range(2):
                        last = pe.matmul(hist[b][:, :], hot[:, slot, j, GROUP + b * HB:GROUP + (b + 1) * HB],
                                         hot[:, slot, j, 0:GROUP], start=first, stop=final)
                last.then_inc(s_hist, 1)

            skewed(pe, GE, (histogram, 1))
            pe.wait_ge(s_counts, 2)
            pe.wait_ge(s_parts, 1)
            for j in range(TILES):
                for b in range(2):
                    last = pe.transpose(turned[j][:, b * HB:(b + 1) * HB], counts[:, b, j:GROUP:TILES], ident[0:HB, 0:HB])
                last.then_inc(s_node, 1)


class Chain:

    def __init__(self, eng, sem, steps):
        self.eng, self.sem, self.steps = eng, sem, steps

    def start(self, g):
        self.at = g * self.steps

    def __call__(self, instruction):
        instruction.then_inc(self.sem, 1)
        self.at = self.at + 1
        self.eng.wait_ge(self.sem, self.at)


def moments(v, chain, rows, stats, tmp, mean, var):
    for k in range(rows.shape[1]):
        last = v.bn_stats(stats[:, k, :], rows[:, k, :])
    chain(last)
    v.tensor_tensor(tmp[:, 0, :], stats[:, :, 1], stats[:, :, 4], ALU.add)
    v.tensor_tensor(tmp[:, 1, :], stats[:, :, 1], stats[:, :, 4], ALU.subtract)
    chain(v.tensor_tensor(tmp[:, 2, :], stats[:, :, 2], stats[:, :, 5], ALU.add))
    v.tensor_scalar(mean, tmp[:, 0, :], 0.5, None, ALU.mult)
    chain(v.scalar_tensor_tensor(out=tmp[:, 3, :], in0=tmp[:, 1, :], scalar=0.25, in1=tmp[:, 1, :],
                                 op0=ALU.mult, op1=ALU.mult))
    return v.scalar_tensor_tensor(out=var, in0=tmp[:, 2, :], scalar=1.0 / C, in1=tmp[:, 3, :],
                                  op0=ALU.mult, op1=ALU.add)


def index_of(keep, GE, kinds, g):
    a, b = kinds
    return keep["index"][:, a:b, :].rearrange("p k (j g) -> p (k j) g", g=GE)[:, :, bass.ds(g, 1)]


def edges0(nc, shape, keep, dram, x, bases_W, comb_W, comb_b):
    N, E, GE, GN = shape
    with ExitStack() as ctx:
        m = Scope(nc, ctx, "e0")
        w_bases = m.sb("w_bases", [C, 2 * BD])
        w_raw = m.sb("w_raw", [C, HEADS0 * MIX])
        w_mix = m.sb("w_mix", [C, HEADS0 * MIX])
        b_raw = m.sb("b_raw", [1, HEADS0 * MIX])
        b_mix = m.sb("b_mix", [1, TILES, HEADS0 * MIX])
        ones = m.sb("ones", [1, P])
        gidx = m.sb("gidx", [P, 2, 2 * TILES], I32)
        sidx = m.sb("sidx", [P, 2, TILES], I32)
        rows = m.sb("rows", [P, 2, 2 * TILES, C])
        scale = m.sb("scale", [P, 2, TILES])
        same = m.sb("same", [P, 2, GROUP])
        barrier = m.sb("barrier", [P, 2, GROUP])
        stats = m.sb("stats", [P, 2 * TILES, 6])
        tmp = m.sb("tmp", [P, 4, 2 * TILES])
        mean = m.sb("mean", [P, 2, 2 * TILES])
        var = m.sb("var", [P, 2, 2 * TILES])
        root = m.sb("root", [P, 2, 2 * TILES])
        rstd = m.sb("rstd", [P, 2 * TILES])
        normed = m.sb("normed", [P, 2, 2 * TILES, C])
        hT = m.sb("hT", [P, 2, 2, GROUP])
        wide = m.sb("wide", [P, 2, TILES, P])
        twin = m.sb("twin", [P, 2, GROUP])
        square = m.sb("square", [BD, 2, GROUP])
        value = m.sb("value", [P, GROUP])
        factor = m.sb("factor", [P, 2, GROUP])
        total = m.sb("total", [P, 2, GROUP])
        total_sq = m.sb("total_sq", [BD, 2, GROUP])
        aggs = m.sb("aggs", [P, 2, 2, GROUP])
        msq = m.sb("msq", [BD, GROUP])
        mean_sq = m.sb("mean_sq", [BD, GROUP])
        top = m.sb("top", [P, TILES * HEADS0])
        mix = m.sb("mix", [P, 2, TILES, HEADS0 * MIX])
        mixsum = m.sb("mixsum", [P, TILES * HEADS0])
        prod = m.sb("prod", [P, TILES, MIX, C])
        outrow = m.sb("outrow", [P, 2, TILES, C])
        p_turn = m.ps("turn", [P, 2, GROUP])
        p_twin = m.ps("twin", [P, GROUP])
        p_wide = m.ps("wide", [P, GROUP])
        p_mix = m.ps("mix", [P, TILES, HEADS0 * MIX])
        p_aggs = m.ps("aggs", [P, TILES, 2 * P])
        p_out = m.ps("out", [P, TILES, C])
        s_weights, s_ready = m.sem("weights"), m.sem("ready")
        s_gidx, s_sidx, s_issue = m.sem("gidx"), m.sem("sidx"), m.sem("issue")
        s_rows = [m.sem(f"rows{i}") for i in range(2)]
        s_dinv = [m.sem(f"dinv{i}") for i in range(2)]
        s_same = [m.sem(f"same{i}") for i in range(2)]
        s_scatter = [m.sem(f"scatter{i}") for i in range(2)]
        s_moment, s_var, s_root, s_rstd, s_norm = (m.sem(n) for n in ("moment", "var", "root", "rstd", "norm"))
        s_turn, s_hT, s_wide, s_bases, s_scales, s_mix = (m.sem(n) for n in ("turn", "hT", "wide", "bases", "scales", "mix"))
        s_twin, s_top, s_sub, s_exp, s_barrier = (m.sem(n) for n in ("twin", "top", "sub", "exp", "barrier"))
        s_factor = [m.sem(f"factor{i}") for i in range(2)]
        s_scan, s_mean, s_meansq, s_varb, s_std = (m.sem(n) for n in ("scan", "mean", "meansq", "varb", "std"))
        s_aggs, s_sum, s_prod, s_reduced, s_mixsum, s_out = (m.sem(n) for n in ("aggs", "sum", "prod", "reduced", "mixsum", "out"))
        s_go = m.sem("go")
        block = m.block()

        @block.sync
        def _(sp):
            sp.dma_start(w_bases[:, 0:BD].rearrange("c (b d) -> c b d", b=BASES), bases_W.rearrange("b c d -> c b d")).then_inc(s_weights, 16)
            sp.dma_start(w_bases[:, BD:2 * BD].rearrange("c (b d) -> c b d", b=BASES), bases_W.rearrange("b c d -> c b d")).then_inc(s_weights, 16)
            sp.dma_start(w_raw[:, :], comb_W).then_inc(s_weights, 16)
            sp.dma_start(b_raw[:, :], comb_b.rearrange("(o n) -> o n", o=1)).then_inc(s_weights, 16)

            def load_same(g, slot, turn):
                if after(g, 2):
                    sp.wait_ge(s_scan, 2 * (g - 1))
                    sp.wait_ge(s_barrier, g - 1)
                    sp.sem_inc(s_go, 1)
                sp.dma_start(same[:, slot, :], dram["same"][bass.ds(g, 1), :].to_broadcast([P, GROUP])).then_inc(s_same[slot], 16)

            def load_factor(g, slot, turn):
                if after(g, 2):
                    sp.wait_ge(s_varb, g - 1)
                    sp.sem_inc(s_go, 1)
                for i in range(2):
                    sp.dma_start(factor[i * BD:(i + 1) * BD, slot, :],
                                 dram["factor"][bass.ds(g, 1), i, :].to_broadcast([BD, GROUP])).then_inc(s_factor[slot], 16)

            skewed(sp, GE, (load_same, 0), (load_factor, 0))

        @block.gpsimd
        def _(pool):
            def gather(g, slot, turn):
                if after(g, 2):
                    pool.wait_ge(s_norm, g - 1)
                    pool.wait_ge(s_wide, g - 1)
                    pool.sem_inc(s_issue, 1)
                pool.tensor_copy(gidx[:, slot, :].rearrange("p (k o) -> p k o", o=1), index_of(keep, GE, (0, 2), g)).then_inc(s_gidx, 1)
                pool.wait_ge(s_gidx, g + 1)
                pool.sem_inc(s_issue, 1)
                for k in range(2 * TILES):
                    pool.indirect_dma_start(rows[:, slot, k, :], None, x, bass.IndirectOffsetOnAxis(ap=gidx[:, slot, k:k + 1], axis=0)).then_inc(s_rows[slot], 16)
                for k in range(TILES):
                    pool.indirect_dma_start(scale[:, slot, k:k + 1], None, dram["dinv"],
                                            bass.IndirectOffsetOnAxis(ap=gidx[:, slot, k:k + 1], axis=0)).then_inc(s_dinv[slot], 16)

            def scatter(g, slot, turn):
                if after(g, 2):
                    pool.wait_ge(s_scatter[slot], 64 * turn)
                    pool.sem_inc(s_issue, 1)
                pool.tensor_copy(sidx[:, slot, :].rearrange("p (k o) -> p k o", o=1), index_of(keep, GE, (2, 3), g)).then_inc(s_sidx, 1)
                pool.wait_ge(s_sidx, g + 1)
                pool.wait_ge(s_out, g + 1)
                pool.sem_inc(s_issue, 1)
                for k in range(TILES):
                    pool.indirect_dma_start(dram["mixed"], bass.IndirectOffsetOnAxis(ap=sidx[:, slot, k:k + 1], axis=0), outrow[:, slot, k, :], None,
                                            bounds_check=N - 1, oob_is_err=False).then_inc(s_scatter[slot], 16)

            skewed(pool, GE, (gather, 0), (scatter, 2))
            for i in range(2):
                pool.wait_ge(s_scatter[i], 64 * (GE // 2))

        @block.scalar
        def _(act):
            def roots(g, slot, turn):
                act.wait_ge(s_var, g + 1)
                act.activation(root[:, slot, :], var[:, slot, :], ACT.Sqrt, bias=keep["eps"][:, :]).then_inc(s_root, 1)

            def columns(g, slot, turn):
                if after(g, 2):
                    act.wait_ge(s_mix, g - 1)
                act.wait_ge(s_dinv[slot], 64 * (turn + 1))
                act.activation(wide[:, slot, :, BD:P], scale[:, slot, :].rearrange("p (j o) -> p j o", o=1).to_broadcast([P, TILES, P - BD]),
                               ACT.Copy).then_inc(s_wide, 1)
                act.wait_ge(s_turn, g + 1)
                act.activation(hT[:, slot, :, :], p_turn[:, :, :], ACT.Relu).then_inc(s_hT, 1)

            def twins(g, slot, turn):
                act.wait_ge(s_bases, g + 1)
                if after(g, 2):
                    act.wait_ge(s_scan, 2 * (g - 1))
                act.activation(twin[:, slot, :], p_twin[:, :], ACT.Copy)
                act.activation(square[:, slot, :], p_twin[0:BD, :], ACT.Square).then_inc(s_twin, 1)
                act.wait_ge(s_same[slot], 16 * (turn + 1))
                act.activation(barrier[BD:P, slot, :], same[BD:P, slot, :], ACT.Copy, scale=HUGE, bias=-HUGE).then_inc(s_barrier, 1)

            def exponent(g, slot, turn):
                act.wait_ge(s_sub, g + 1)
                act.activation(fold(mix[:, slot, :, :]), fold(mix[:, slot, :, :]), ACT.Exp).then_inc(s_exp, 1)

            def deviation(g, slot, turn):
                act.wait_ge(s_mean, g + 1)
                act.activation(mean_sq[:, :], aggs[0:BD, slot, 0, :], ACT.Square).then_inc(s_meansq, 1)
                act.wait_ge(s_varb, g + 1)
                act.activation(aggs[0:BD, slot, 1, :], msq[:, :], ACT.Sqrt).then_inc(s_std, 1)

            act.wait_ge(s_ready, 1)
            skewed(act, GE, (roots, 0), (columns, 0), (twins, 0), (exponent, 0), (deviation, 0))

        @block.vector
        def _(v):
            v.memset(ones[:, :], 1.0)
            v.memset(wide[:, 0, :, 0:BD], 1.0)
            v.memset(wide[:, 1, :, 0:BD], 1.0)
            v.wait_ge(s_weights, 64)
            for i, a in enumerate(AGG_ORDER):
                v.tensor_copy(w_mix[:, :].rearrange("c (h q b) -> c h q b", h=HEADS0, q=AGGS)[:, :, i, :],
                              w_raw[:, :].rearrange("c (h b q) -> c h b q", h=HEADS0, q=AGGS)[:, :, :, a])
                for j in range(TILES):
                    last = v.tensor_copy(b_mix[:, j, :].rearrange("c (h q b) -> c h q b", h=HEADS0, q=AGGS)[:, :, i, :],
                                         b_raw[:, :].rearrange("c (h b q) -> c h b q", h=HEADS0, q=AGGS)[:, :, :, a])
            last.then_inc(s_ready, 1)
            moment, scan = Chain(v, s_moment, 3), Chain(v, s_scan, 2)

            def row_moments(g, slot, turn):
                moment.start(g)
                v.wait_ge(s_rows[slot], 128 * (turn + 1))
                moments(v, moment, rows[:, slot], stats, tmp, mean[:, slot, :], var[:, slot, :]).then_inc(s_var, 1)

            def normalise(g, slot, turn):
                v.wait_ge(s_root, g + 1)
                v.reciprocal(rstd[:, :], root[:, slot, :]).then_inc(s_rstd, 1)
                if after(g, 2):
                    v.wait_ge(s_turn, g - 1)
                v.wait_ge(s_rstd, g + 1)
                for k in range(2 * TILES):
                    last = v.tensor_scalar(normed[:, slot, k, :], rows[:, slot, k, :], mean[:, slot, k:k + 1], rstd[:, k:k + 1],
                                           ALU.subtract, ALU.mult)
                last.then_inc(s_norm, 1)

            def soften(g, slot, turn):
                v.wait_ge(s_mix, g + 1)
                v.tensor_reduce(top[:, :], p_mix[:, :, :].rearrange("p j (h k) -> p (j h) k", k=MIX), AX_X, ALU.max).then_inc(s_top, 1)
                v.wait_ge(s_top, g + 1)
                v.tensor_tensor(mix[:, slot, :, :].rearrange("p j (h k) -> p (j h) k", k=MIX),
                                p_mix[:, :, :].rearrange("p j (h k) -> p (j h) k", k=MIX), spread(top[:, :], MIX), ALU.subtract).then_inc(s_sub, 1)

            def scans(g, slot, turn):
                first = isinstance(g, int) and g == 0

                def carry(tile):
                    return 0.0 if first else tile[:, GROUP - 1:GROUP]

                scan.start(g)
                v.wait_ge(s_same[slot], 16 * (turn + 1))
                v.wait_ge(s_twin, g + 1)
                v.wait_ge(s_scales, g + 1)
                scan(v.tensor_tensor(value[:, :], p_wide[:, :], twin[:, slot, :], ALU.mult))
                v.tensor_tensor_scan(total[:, slot, :], same[:, slot, :], value[:, :], carry(total[:, 1 - slot, :]), ALU.mult, ALU.add)
                v.tensor_tensor_scan(total_sq[:, slot, :], same[0:BD, slot, :], square[:, slot, :],
                                     carry(total_sq[:, 1 - slot, :]), ALU.mult, ALU.add)
                v.wait_ge(s_barrier, g + 1)
                scan(v.tensor_tensor_scan(aggs[BD:P, slot, 1, :], barrier[BD:P, slot, :], twin[BD:P, slot, :],
                                          carry(aggs[BD:P, 1 - slot, 1, :]), ALU.add, ALU.max))
                v.wait_ge(s_factor[slot], 32 * (turn + 1))
                v.tensor_tensor(aggs[:, slot, 0, :], total[:, slot, :], factor[:, slot, :], ALU.mult).then_inc(s_mean, 1)
                v.tensor_tensor(msq[:, :], total_sq[:, slot, :], factor[0:BD, slot, :], ALU.mult).then_inc(s_sum, 1)
                v.wait_ge(s_sum, 3 * g + 1)
                v.wait_ge(s_meansq, g + 1)
                v.tensor_tensor(msq[:, :], msq[:, :], mean_sq[:, :], ALU.subtract).then_inc(s_sum, 1)
                v.wait_ge(s_sum, 3 * g + 2)
                v.tensor_scalar(msq[:, :], msq[:, :], 0.0, EPS, ALU.max, ALU.add).then_inc(s_varb, 1)

            def products(g, slot, turn):
                v.wait_ge(s_exp, g + 1)
                v.tensor_reduce(mixsum[:, :], mix[:, slot, :, :].rearrange("p j (h k) -> p (j h) k", k=MIX), AX_X, ALU.add).then_inc(s_sum, 1)
                v.wait_ge(s_aggs, g + 1)
                for j in range(TILES):
                    if after(g, 1):
                        v.wait_ge(s_reduced, 4 * g - 3 + j)
                    v.tensor_tensor(prod[:, j, :, :].rearrange("p k (h d) -> p k h d", h=HEADS0),
                                    mix[:, slot, j, :].rearrange("p (h k o) -> p k h o", k=MIX, o=1).to_broadcast([P, MIX, HEADS0, D0]),
                                    p_aggs[:, j, :].rearrange("p (k o d) -> p k o d", k=MIX, o=1).to_broadcast([P, MIX, HEADS0, D0]),
                                    ALU.mult).then_inc(s_prod, 1)

            def finish(g, slot, turn):
                v.wait_ge(s_sum, 3 * g + 3)
                v.reciprocal(mixsum[:, :], mixsum[:, :]).then_inc(s_mixsum, 1)
                v.wait_ge(s_mixsum, g + 1)
                v.wait_ge(s_reduced, 4 * (g + 1))
                if after(g, 2):
                    v.wait_ge(s_scatter[slot], 64 * turn)
                v.tensor_tensor(outrow[:, slot, :, :].rearrange("p j (h d) -> p (j h) d", h=HEADS0),
                                p_out[:, :, :].rearrange("p j (h d) -> p (j h) d", h=HEADS0), spread(mixsum[:, :], D0),
                                ALU.mult).then_inc(s_out, 1)

            skewed(v, GE, (row_moments, 0), (products, 1), (normalise, 0), (finish, 1), (soften, 0), (scans, 0))

        @block.tensor
        def _(pe):
            ident = keep["ident"]
            pe.wait_ge(s_ready, 1)

            def turns(g, slot, turn):
                pe.wait_ge(s_norm, g + 1)
                if after(g, 1):
                    pe.wait_ge(s_hT, g)
                for k in range(2 * TILES):
                    last = pe.transpose(p_turn[:, k // TILES, (k % TILES) * P:(k % TILES + 1) * P], normed[:, slot, k, :], ident[:, :])
                last.then_inc(s_turn, 1)

            def project(g, slot, turn):
                pe.wait_ge(s_hT, g + 1)
                if after(g, 1):
                    pe.wait_ge(s_twin, g)
                pe.matmul(p_twin[:, :], w_bases[:, :], hT[:, slot, 0, :], start=True, stop=True).then_inc(s_bases, 1)
                pe.wait_ge(s_wide, g + 1)
                if after(g, 1):
                    pe.wait_ge(s_scan, 2 * g - 1)
                for j in range(TILES):
                    last = pe.transpose(p_wide[:, j * P:(j + 1) * P], wide[:, slot, j, :], ident[:, :])
                last.then_inc(s_scales, 1)
                if after(g, 1):
                    pe.wait_ge(s_sub, g)
                pe.matmul(fold(p_mix[:, :, :]), ones[:, :], fold(b_mix[:, :, :]), start=True, stop=False)
                for j in range(TILES):
                    last = pe.matmul(p_mix[:, j, :], hT[:, slot, 1, j * P:(j + 1) * P], w_mix[:, :], start=False, stop=(j == TILES - 1))
                last.then_inc(s_mix, 1)

            def turn_back(g, slot, turn):
                pe.wait_ge(s_std, g + 1)
                pe.wait_ge(s_mean, g + 1)
                if after(g, 1):
                    pe.wait_ge(s_prod, 4 * g)
                for j in range(TILES):
                    for i in range(2):
                        last = pe.transpose(p_aggs[:, j, i * P:(i + 1) * P], aggs[:, slot, i, j * P:(j + 1) * P], ident[:, :])
                last.then_inc(s_aggs, 1)

            def reduce(g, slot, turn):
                if after(g, 1):
                    pe.wait_ge(s_out, g)
                for j in range(TILES):
                    pe.wait_ge(s_prod, 4 * g + j + 1)
                    for k in range(MIX):
                        last = pe.matmul(p_out[:, j, :], ident[:, :], prod[:, j, k, :], start=(k == 0), stop=(k == MIX - 1))
                    last.then_inc(s_reduced, 1)

            skewed(pe, GE, (reduce, 1), (turns, 0), (project, 0), (turn_back, 0))


def node_rows(table, N, g):
    if not isinstance(g, int):
        return table[bass.ds(g * GROUP, GROUP), :].rearrange("(p j) c -> p j c", j=TILES), P
    n = min(GROUP, N - g * GROUP) // TILES
    return table[g * GROUP:g * GROUP + n * TILES, :].rearrange("(p j) c -> p j c", j=TILES), n


def nodes0(nc, shape, keep, dram, x, bases_W, comb_W, comb_b, bias):
    N, E, GE, GN = shape
    JH = TILES * HEADS0
    with ExitStack() as ctx:
        m = Scope(nc, ctx, "n0")
        w_bases = m.sb("w_bases", [C, BD])
        w_raw = m.sb("w_raw", [C, HEADS0 * MIX])
        w_mix = m.sb("w_mix", [C, HEADS0 * MIX])
        b_raw = m.sb("b_raw", [1, HEADS0 * MIX])
        b_mix = m.sb("b_mix", [1, TILES, HEADS0 * MIX])
        b_out = m.sb("b_out", [P, C])
        ones = m.sb("ones", [1, P])
        rows = m.sb("rows", [P, 2, TILES, C])
        mixed = m.sb("mixed", [P, 2, TILES, C])
        stats = m.sb("stats", [P, TILES, 6])
        tmp = m.sb("tmp", [P, 4, TILES])
        mean = m.sb("mean", [P, 2, TILES])
        var = m.sb("var", [P, 2, TILES])
        root = m.sb("root", [P, 2, TILES])
        rstd = m.sb("rstd", [P, TILES])
        normed = m.sb("normed", [P, 2, TILES, C])
        hT = m.sb("hT", [P, 2, GROUP])
        top = m.sb("top", [P, JH])
        mix = m.sb("mix", [P, 2, TILES, HEADS0 * MIX])
        mixsum = m.sb("mixsum", [P, JH])
        lone = m.sb("lone", [P, JH])
        selfs = m.sb("selfs", [P, JH])
        prod = m.sb("prod", [P, BASES, TILES, C])
        residual = m.sb("residual", [P, 2, TILES, C])
        part = m.sb("part", [P, TILES, C])
        x1 = m.sb("x1", [P, 2, TILES, C])
        p_turn = m.ps("turn", [P, GROUP])
        p_mix = m.ps("mix", [P, TILES, HEADS0 * MIX])
        p_bases = m.ps("bases", [P, TILES, BD])
        p_out = m.ps("out", [P, TILES, C])
        s_weights, s_ready = m.sem("weights"), m.sem("ready")
        s_rows = [m.sem(f"rows{i}") for i in range(2)]
        s_mixed = [m.sem(f"mixed{i}") for i in range(2)]
        s_store = [m.sem(f"store{i}") for i in range(2)]
        s_moment, s_var, s_root, s_rstd, s_norm = (m.sem(n) for n in ("moment", "var", "root", "rstd", "norm"))
        s_turn, s_hT, s_mix, s_top, s_sub, s_exp = (m.sem(n) for n in ("turn", "hT", "mix", "top", "sub", "exp"))
        s_sum, s_prod, s_reduced, s_small, s_part, s_x1 = (m.sem(n) for n in ("sum", "prod", "reduced", "small", "part", "x1"))
        s_added, s_residual = m.sem("added"), m.sem("residual")
        s_go = m.sem("go")
        block = m.block()

        @block.sync
        def _(sp):
            sp.dma_start(w_bases[:, :].rearrange("c (b d) -> c b d", b=BASES), bases_W.rearrange("b c d -> c b d")).then_inc(s_weights, 16)
            sp.dma_start(w_raw[:, :], comb_W).then_inc(s_weights, 16)
            sp.dma_start(b_raw[:, :], comb_b.rearrange("(o n) -> o n", o=1)).then_inc(s_weights, 16)
            sp.dma_start(b_out[:, :], row_of(bias)).then_inc(s_weights, 16)

            def load(g, slot, turn):
                if after(g, 2):
                    sp.wait_ge(s_norm, g - 1)
                    sp.wait_ge(s_added, g - 1)
                    sp.sem_inc(s_go, 1)
                source, n = node_rows(x, N, g)
                sp.dma_start(rows[0:n, slot, :, :], source).then_inc(s_rows[slot], 16)
                source, n = node_rows(dram["mixed"], GN * GROUP, g)
                sp.dma_start(mixed[:, slot, :, :], source).then_inc(s_mixed[slot], 16)

            def store(g, slot, turn):
                sp.wait_ge(s_x1, g + 1)
                sp.sem_inc(s_go, 1)
                sp.dma_start(node_rows(dram["x1"], GN * GROUP, g)[0], x1[:, slot, :, :]).then_inc(s_store[slot], 16)

            skewed(sp, GN, (load, 0), (store, 2), peel=2)
            for i in range(2):
                sp.wait_ge(s_store[i], 16 * (GN // 2))

        @block.gpsimd
        def _(pool):
            pool.wait_ge(s_weights, 64)

            def add(g, slot, turn):
                if after(g, 2):
                    pool.wait_ge(s_x1, g - 1)
                pool.wait_ge(s_mixed[slot], 16 * (turn + 1))
                pool.wait_ge(s_rows[slot], 16 * (turn + 1))
                pool.tensor_tensor(residual[:, slot, :, :], rows[:, slot, :, :], mixed[:, slot, :, :], ALU.add).then_inc(s_added, 1)
                pool.wait_ge(s_added, g + 1)
                pool.tensor_tensor(residual[:, slot, :, :], residual[:, slot, :, :], over(b_out[:, :], TILES), ALU.add).then_inc(s_residual, 1)

            skewed(pool, GN, (add, 0))

        @block.scalar
        def _(act):
            def roots(g, slot, turn):
                act.wait_ge(s_var, g + 1)
                act.activation(root[:, slot, :], var[:, slot, :], ACT.Sqrt, bias=keep["eps"][:, :]).then_inc(s_root, 1)

            def columns(g, slot, turn):
                if after(g, 2):
                    act.wait_ge(s_mix, g - 1)
                act.wait_ge(s_turn, g + 1)
                act.activation(hT[:, slot, :], p_turn[:, :], ACT.Relu).then_inc(s_hT, 1)

            def exponent(g, slot, turn):
                act.wait_ge(s_sub, g + 1)
                act.activation(fold(mix[:, slot, :, :]), fold(mix[:, slot, :, :]), ACT.Exp).then_inc(s_exp, 1)

            skewed(act, GN, (roots, 0), (columns, 0), (exponent, 0))

        @block.vector
        def _(v):
            v.memset(ones[:, :], 1.0)
            v.wait_ge(s_weights, 64)
            for i, a in enumerate(AGG_ORDER):
                v.tensor_copy(w_mix[:, :].rearrange("c (h q b) -> c h q b", h=HEADS0, q=AGGS)[:, :, i, :],
                              w_raw[:, :].rearrange("c (h b q) -> c h b q", h=HEADS0, q=AGGS)[:, :, :, a])
                for j in range(TILES):
                    last = v.tensor_copy(b_mix[:, j, :].rearrange("c (h q b) -> c h q b", h=HEADS0, q=AGGS)[:, :, i, :],
                                         b_raw[:, :].rearrange("c (h b q) -> c h b q", h=HEADS0, q=AGGS)[:, :, :, a])
            last.then_inc(s_ready, 1)
            moment, small = Chain(v, s_moment, 3), Chain(v, s_small, 2)

            def row_moments(g, slot, turn):
                moment.start(g)
                v.wait_ge(s_rows[slot], 16 * (turn + 1))
                moments(v, moment, rows[:, slot], stats, tmp, mean[:, slot, :], var[:, slot, :]).then_inc(s_var, 1)

            def normalise(g, slot, turn):
                v.wait_ge(s_root, g + 1)
                v.reciprocal(rstd[:, :], root[:, slot, :]).then_inc(s_rstd, 1)
                if after(g, 2):
                    v.wait_ge(s_turn, g - 1)
                v.wait_ge(s_rstd, g + 1)
                for k in range(TILES):
                    last = v.tensor_scalar(normed[:, slot, k, :], rows[:, slot, k, :], mean[:, slot, k:k + 1], rstd[:, k:k + 1],
                                           ALU.subtract, ALU.mult)
                last.then_inc(s_norm, 1)

            def soften(g, slot, turn):
                v.wait_ge(s_mix, g + 1)
                v.tensor_reduce(top[:, :], p_mix[:, :, :].rearrange("p j (h k) -> p (j h) k", k=MIX), AX_X, ALU.max).then_inc(s_top, 1)
                v.wait_ge(s_top, g + 1)
                v.tensor_tensor(mix[:, slot, :, :].rearrange("p j (h k) -> p (j h) k", k=MIX),
                                p_mix[:, :, :].rearrange("p j (h k) -> p (j h) k", k=MIX), spread(top[:, :], MIX), ALU.subtract).then_inc(s_sub, 1)

            def products(g, slot, turn):
                v.wait_ge(s_exp, g + 1)
                v.tensor_reduce(mixsum[:, :], mix[:, slot, :, :].rearrange("p j (h k) -> p (j h) k", k=MIX), AX_X, ALU.add)
                v.tensor_reduce(lone[:, :], mix[:, slot, :, :].rearrange("p j (h q b) -> p (j h) q b", q=AGGS, b=BASES)[:, :, 2, :],
                                AX_X, ALU.add).then_inc(s_sum, 1)
                if after(g, 1):
                    v.wait_ge(s_reduced, g)
                for j in range(TILES):
                    last = v.tensor_tensor(prod[:, :, j, :].rearrange("p b (h d) -> p b h d", h=HEADS0),
                                           mix[:, slot, j, :].rearrange("p (h q b o) -> p q b h o", q=AGGS, b=BASES, o=1)[:, 1].to_broadcast([P, BASES, HEADS0, D0]),
                                           p_bases[:, j, :].rearrange("p (b o d) -> p b o d", b=BASES, o=1).to_broadcast([P, BASES, HEADS0, D0]),
                                           ALU.mult)
                last.then_inc(s_prod, 1)

            def finish(g, slot, turn):
                small.start(g)
                v.wait_ge(s_sum, g + 1)
                small(v.reciprocal(mixsum[:, :], mixsum[:, :]))
                v.tensor_tensor(selfs[:, :].rearrange("p (j h) -> p j h", j=TILES), mixsum[:, :].rearrange("p (j h) -> p j h", j=TILES),
                                keep["selfw"][:, :, bass.ds(g, 1)].to_broadcast([P, TILES, HEADS0]), ALU.mult)
                small(v.tensor_tensor(lone[:, :], lone[:, :], mixsum[:, :], ALU.mult))
                v.tensor_tensor(lone[:, :].rearrange("p (j h) -> p j h", j=TILES), lone[:, :].rearrange("p (j h) -> p j h", j=TILES),
                                keep["lonew"][:, :, bass.ds(g, 1)].to_broadcast([P, TILES, HEADS0]), ALU.mult)
                v.wait_ge(s_reduced, g + 1)
                v.tensor_tensor(part[:, :, :].rearrange("p j (h d) -> p (j h) d", h=HEADS0),
                                p_out[:, :, :].rearrange("p j (h d) -> p (j h) d", h=HEADS0), spread(selfs[:, :], D0), ALU.mult).then_inc(s_part, 1)
                v.wait_ge(s_part, 2 * g + 1)
                v.tensor_tensor(part[:, :, :].rearrange("p j (h d) -> p (j h) d", h=HEADS0),
                                part[:, :, :].rearrange("p j (h d) -> p (j h) d", h=HEADS0), spread(lone[:, :], D0), ALU.add).then_inc(s_part, 1)
                v.wait_ge(s_part, 2 * g + 2)
                v.wait_ge(s_residual, g + 1)
                if after(g, 2):
                    v.wait_ge(s_store[slot], 16 * turn)
                v.tensor_tensor(x1[:, slot, :, :], part[:, :, :], residual[:, slot, :, :], ALU.add).then_inc(s_x1, 1)

            skewed(v, GN, (row_moments, 0), (products, 1), (normalise, 0), (finish, 1), (soften, 0))

        @block.tensor
        def _(pe):
            ident = keep["ident"]
            pe.wait_ge(s_ready, 1)

            def turns(g, slot, turn):
                pe.wait_ge(s_norm, g + 1)
                if after(g, 1):
                    pe.wait_ge(s_hT, g)
                for k in range(TILES):
                    last = pe.transpose(p_turn[:, k * P:(k + 1) * P], normed[:, slot, k, :], ident[:, :])
                last.then_inc(s_turn, 1)

            def project(g, slot, turn):
                if after(g, 1):
                    pe.wait_ge(s_sub, g)
                    pe.wait_ge(s_prod, g)
                pe.wait_ge(s_hT, g + 1)
                pe.matmul(fold(p_mix[:, :, :]), ones[:, :], fold(b_mix[:, :, :]), start=True, stop=False)
                for j in range(TILES):
                    pe.matmul(p_mix[:, j, :], hT[:, slot, j * P:(j + 1) * P], w_mix[:, :], start=False, stop=(j == TILES - 1))
                    last = pe.matmul(p_bases[:, j, :], hT[:, slot, j * P:(j + 1) * P], w_bases[:, :], start=True, stop=True)
                last.then_inc(s_mix, 1)

            def reduce(g, slot, turn):
                pe.wait_ge(s_prod, g + 1)
                if after(g, 1):
                    pe.wait_ge(s_part, 2 * g - 1)
                for b in range(BASES):
                    last = pe.matmul(fold(p_out[:, :, :]), ident[:, :], fold(prod[:, b, :, :]), start=(b == 0), stop=(b == BASES - 1))
                last.then_inc(s_reduced, 1)

            skewed(pe, GN, (reduce, 1), (turns, 0), (project, 0))


def edges1(nc, shape, keep, dram, edge_attr, ln_g, ln_b, wts, biases, We):
    N, E, GE, GN = shape
    K = 2 * TILES
    names = ("k", "v", "q")
    with ExitStack() as ctx:
        m = Scope(nc, ctx, "e1")
        raw = m.sb("raw", [C, 3, C])
        weight = m.sb("weight", [C, 3, C])
        bias_raw = m.sb("bias_raw", [C, 3])
        bias = m.sb("bias", [C, 3])
        norm = m.sb("norm", [C, 2])
        w_edge = m.sb("w_edge", [TILES * EDGE_C, TILES, C])
        heads = m.sb("heads", [C, C])
        gidx = m.sb("gidx", [P, 2, K], I32)
        sidx = m.sb("sidx", [P, 2, TILES], I32)
        rows = m.sb("rows", [P, 2, K, C])
        attr = m.sb("attr", [P, 2, TILES, EDGE_C])
        same = m.sb("same", [P, 2, GROUP])
        barrier = m.sb("barrier", [P, 2, GROUP])
        stats = m.sb("stats", [P, K, 6])
        tmp = m.sb("tmp", [P, 4, K])
        mean = m.sb("mean", [P, 2, K])
        var = m.sb("var", [P, 2, K])
        root = m.sb("root", [P, 2, K])
        rstd = m.sb("rstd", [P, K])
        mean2 = m.sb("mean2", [P, K])
        var2 = m.sb("var2", [P, 2, K])
        square = m.sb("square", [P, K])
        root2 = m.sb("root2", [P, 2, K])
        factor = m.sb("factor", [P, K])
        rectified = m.sb("rectified", [P, K, C])
        normed = m.sb("normed", [P, 2, K, C])
        xT = m.sb("xT", [P, 2, 2, GROUP])
        attrT = m.sb("attrT", [TILES * EDGE_C, 2, P])
        qT = m.sb("qT", [P, 2, GROUP])
        vT = m.sb("vT", [P, 2, GROUP])
        qk = m.sb("qk", [P, 2, GROUP])
        top = m.sb("top", [P, 2, 1 + GROUP])
        fade = m.sb("fade", [P, GROUP])
        fade2 = m.sb("fade2", [P, 2, GROUP])
        prob = m.sb("prob", [P, 2, GROUP])
        pv = m.sb("pv", [P, GROUP])
        denom = m.sb("denom", [P, 2, GROUP])
        numer = m.sb("numer", [P, 2, GROUP])
        inverse = m.sb("inverse", [P, TILES * HEADS1])
        outrow = m.sb("outrow", [P, 2, TILES, C])
        p_turn = m.ps("turn", [P, 2, GROUP])
        p_k, p_v, p_q = (m.ps(n, [P, GROUP]) for n in names)
        p_score = m.ps("score", [P, GROUP])
        p_numer = m.ps("numer", [P, TILES, C])
        p_denom = m.ps("denom", [P, TILES, C])
        s_weights, s_ready, s_zero = m.sem("weights"), m.sem("ready"), m.sem("zero")
        s_bias, s_const = m.sem("bias"), m.sem("const")
        s_gidx, s_sidx, s_issue = m.sem("gidx"), m.sem("sidx"), m.sem("issue")
        s_rows = [m.sem(f"rows{i}") for i in range(2)]
        s_attr = [m.sem(f"attr{i}") for i in range(2)]
        s_same = [m.sem(f"same{i}") for i in range(2)]
        s_scatter = [m.sem(f"scatter{i}") for i in range(2)]
        s_moment, s_var, s_root, s_rstd = (m.sem(n) for n in ("moment", "var", "root", "rstd"))
        s_moment2, s_var2, s_root2, s_norm = (m.sem(n) for n in ("moment2", "var2", "root2", "norm"))
        s_turn, s_attrT, s_xT, s_k, s_qv, s_vq, s_qk, s_score = (m.sem(n) for n in ("turn", "attrT", "xT", "k", "qv", "vq", "qk", "score"))
        s_attrp, s_barrier, s_top, s_fade, s_prob, s_faded = (m.sem(n) for n in ("attrp", "barrier", "top", "fade", "prob", "faded"))
        s_pv, s_scan, s_back, s_inv, s_out = (m.sem(n) for n in ("pv", "scan", "back", "inv", "out"))
        s_den, s_tail = m.sem("den"), m.sem("tail")
        full = E // GROUP
        n_load = 3 + 3 + 2 + TILES
        tail_dmas = sum(1 for j in range(TILES) if E - full * GROUP - j * P > 0)
        s_go = m.sem("go")
        block = m.block()

        @block.sync
        def _(sp):
            for i, n in enumerate(names):
                sp.dma_start(raw[:, i, :], wts[n]).then_inc(s_weights, 16)
                sp.dma_start(bias_raw[:, i:i + 1], biases[n].rearrange("(p o) -> p o", o=1)).then_inc(s_weights, 16)
            sp.dma_start(norm[:, 0:1], ln_g.rearrange("(p o) -> p o", o=1)).then_inc(s_weights, 16)
            sp.dma_start(norm[:, 1:2], ln_b.rearrange("(p o) -> p o", o=1)).then_inc(s_weights, 16)
            sp.wait_ge(s_zero, 1)
            for j in range(TILES):
                sp.dma_start(w_edge[j * EDGE_C:(j + 1) * EDGE_C, j, :], We).then_inc(s_weights, 16)

            def load(g, slot, turn):
                if after(g, 2):
                    sp.wait_ge(s_attrp, g - 1)
                    sp.sem_inc(s_go, 1)
                if not isinstance(g, int) or g < full:
                    sp.dma_start(attr[:, slot, :, :], edge_attr[bass.ds(g * GROUP, GROUP), :].rearrange("(j p) c -> p j c", p=P)).then_inc(s_attr[slot], 16)
                else:
                    for j in range(TILES):
                        n = min(P, max(0, E - g * GROUP - j * P))
                        if n:
                            sp.dma_start(attr[0:n, slot, j, :], edge_attr[g * GROUP + j * P:g * GROUP + j * P + n, :]).then_inc(s_tail, 16)
                if after(g, 2):
                    sp.wait_ge(s_scan, g - 1)
                    sp.wait_ge(s_barrier, g - 1)
                    sp.sem_inc(s_go, 1)
                sp.dma_start(same[:, slot, :], dram["same"][bass.ds(g, 1), :].to_broadcast([P, GROUP])).then_inc(s_same[slot], 16)

            skewed(sp, GE, (load, 0), peel=2)

        @block.gpsimd
        def _(pool):
            def gather(g, slot, turn):
                if after(g, 2):
                    pool.wait_ge(s_moment2, 5 * (g - 1))
                    pool.sem_inc(s_issue, 1)
                pool.tensor_copy(gidx[:, slot, :].rearrange("p (k o) -> p k o", o=1), index_of(keep, GE, (0, 2), g)).then_inc(s_gidx, 1)
                pool.wait_ge(s_gidx, g + 1)
                pool.sem_inc(s_issue, 1)
                for k in range(K):
                    pool.indirect_dma_start(rows[:, slot, k, :], None, dram["x1"], bass.IndirectOffsetOnAxis(ap=gidx[:, slot, k:k + 1], axis=0)).then_inc(s_rows[slot], 16)

            def scatter(g, slot, turn):
                if after(g, 2):
                    pool.wait_ge(s_scatter[slot], 64 * turn)
                    pool.sem_inc(s_issue, 1)
                pool.tensor_copy(sidx[:, slot, :].rearrange("p (k o) -> p k o", o=1), index_of(keep, GE, (2, 3), g)).then_inc(s_sidx, 1)
                pool.wait_ge(s_sidx, g + 1)
                pool.wait_ge(s_out, g + 1)
                pool.sem_inc(s_issue, 1)
                for k in range(TILES):
                    pool.indirect_dma_start(dram["attended"], bass.IndirectOffsetOnAxis(ap=sidx[:, slot, k:k + 1], axis=0), outrow[:, slot, k, :], None,
                                            bounds_check=N - 1, oob_is_err=False).then_inc(s_scatter[slot], 16)

            skewed(pool, GE, (gather, 0), (scatter, 2))
            for i in range(2):
                pool.wait_ge(s_scatter[i], 64 * (GE // 2))

        @block.scalar
        def _(act):
            def roots(g, slot, turn):
                act.wait_ge(s_var, g + 1)
                act.activation(root[:, slot, :], var[:, slot, :], ACT.Sqrt, bias=keep["eps"][:, :]).then_inc(s_root, 1)

            def roots2(g, slot, turn):
                act.wait_ge(s_var2, g + 1)
                act.activation(root2[:, slot, :], var2[:, slot, :], ACT.Sqrt, bias=keep["eps"][:, :]).then_inc(s_root2, 1)
                act.wait_ge(s_same[slot], 16 * (turn + 1))
                if after(g, 2):
                    act.wait_ge(s_fade, 2 * (g - 1))
                act.activation(barrier[:, slot, :], same[:, slot, :], ACT.Copy, scale=HUGE, bias=-HUGE).then_inc(s_barrier, 1)

            def columns(g, slot, turn):
                if after(g, 2):
                    act.wait_ge(s_qv, g - 1)
                act.wait_ge(s_attrp, g + 1)
                act.activation(attrT[:, slot, :], p_score[0:TILES * EDGE_C, 0:P], ACT.Copy).then_inc(s_attrT, 1)
                act.wait_ge(s_turn, g + 1)
                act.activation(xT[:, slot, :, :], p_turn[:, :, :], ACT.Copy).then_inc(s_xT, 1)

            def query_value(g, slot, turn):
                if after(g, 2):
                    act.wait_ge(s_qk, g - 1)
                    act.wait_ge(s_pv, g - 1)
                act.wait_ge(s_qv, g + 1)
                act.activation(qT[:, slot, :], p_q[:, :], ACT.Identity, bias=bias[:, 2:3])
                act.activation(vT[:, slot, :], p_v[:, :], ACT.Identity, bias=bias[:, 1:2]).then_inc(s_vq, 1)

            def exponents(g, slot, turn):
                act.wait_ge(s_fade, 2 * g + 2)
                act.activation(prob[:, slot, :], prob[:, slot, :], ACT.Exp).then_inc(s_prob, 1)
                act.activation(fade2[:, slot, :], fade2[:, slot, :], ACT.Exp).then_inc(s_faded, 1)

            act.wait_ge(s_bias, 1)
            skewed(act, GE, (roots, 0), (exponents, 1), (roots2, 0), (columns, 0), (query_value, 0))

        @block.vector
        def _(v):
            v.memset(w_edge[:, :, :], 0.0)
            v.memset(attr[:, :, :, :], 0.0).then_inc(s_zero, 1)
            v.memset(heads[:, :], 0.0).then_inc(s_const, 1)
            v.memset(top[:, 0, 0:1], 0.0)
            v.wait_ge(s_const, 1)
            for h in range(HEADS1):
                last = v.memset(heads[h * D1:(h + 1) * D1, h * D1:(h + 1) * D1], float(D1) ** -0.5)
            last.then_inc(s_const, 1)
            v.wait_ge(s_weights, 16 * n_load)
            last = v.tensor_scalar(fold(weight[:, :, :]), fold(raw[:, :, :]), norm[:, 0:1], None, ALU.mult)
            last.then_inc(s_ready, 1)
            v.wait_ge(s_ready, 2)
            v.tensor_tensor(bias[:, :], bias_raw[:, :], p_score[:, 0:3], ALU.add).then_inc(s_bias, 1)
            moment, moment2 = Chain(v, s_moment, 3), Chain(v, s_moment2, 5)

            def row_moments(g, slot, turn):
                moment.start(g)
                v.wait_ge(s_rows[slot], 128 * (turn + 1))
                moments(v, moment, rows[:, slot], stats, tmp, mean[:, slot, :], var[:, slot, :]).then_inc(s_var, 1)

            def rectify(g, slot, turn):
                v.wait_ge(s_root, g + 1)
                v.reciprocal(rstd[:, :], root[:, slot, :]).then_inc(s_rstd, 1)
                moment2.start(g)
                for k in range(K):
                    last = v.tensor_scalar(rectified[:, k, :], rows[:, slot, k, :], mean[:, slot, k:k + 1], 0.0, ALU.subtract, ALU.max)
                moment2(last)
                moment2(moments(v, moment2, rectified, stats, tmp, mean2[:, :], square[:, :]))
                v.wait_ge(s_rstd, 3 * g + 1)
                v.tensor_tensor(square[:, :], square[:, :], rstd[:, :], ALU.mult).then_inc(s_rstd, 1)
                v.wait_ge(s_rstd, 3 * g + 2)
                v.tensor_tensor(var2[:, slot, :], square[:, :], rstd[:, :], ALU.mult).then_inc(s_var2, 1)

            def normalise(g, slot, turn):
                v.wait_ge(s_root2, g + 1)
                v.reciprocal(factor[:, :], root2[:, slot, :]).then_inc(s_rstd, 1)
                v.wait_ge(s_rstd, 3 * g + 3)
                v.tensor_tensor(factor[:, :], factor[:, :], rstd[:, :], ALU.mult).then_inc(s_inv, 1)
                if after(g, 2):
                    v.wait_ge(s_turn, g - 1)
                v.wait_ge(s_inv, g + 1)
                for k in range(K):
                    last = v.tensor_scalar(normed[:, slot, k, :], rectified[:, k, :], mean2[:, k:k + 1], factor[:, k:k + 1], ALU.subtract, ALU.mult)
                last.then_inc(s_norm, 1)

            def score(g, slot, turn):
                v.wait_ge(s_k, g + 1)
                v.wait_ge(s_vq, g + 1)
                if after(g, 2):
                    v.wait_ge(s_score, g - 1)
                v.scalar_tensor_tensor(out=qk[:, slot, :], in0=p_k[:, :], scalar=bias[:, 0:1], in1=qT[:, slot, :],
                                       op0=ALU.add, op1=ALU.mult).then_inc(s_qk, 1)

            def running_top(g, slot, turn):
                first = isinstance(g, int) and g == 0
                v.wait_ge(s_score, g + 1)
                v.wait_ge(s_barrier, g + 1)
                if not first:
                    v.tensor_copy(top[:, slot, 0:1], top[:, 1 - slot, GROUP:GROUP + 1])
                v.tensor_tensor_scan(top[:, slot, 1:GROUP + 1], barrier[:, slot, :], p_score[:, :],
                                     0.0 if first else top[:, 1 - slot, GROUP:GROUP + 1], ALU.add, ALU.max).then_inc(s_top, 1)
                v.wait_ge(s_top, g + 1)
                v.tensor_tensor(fade[:, :], top[:, slot, 0:GROUP], barrier[:, slot, :], ALU.add).then_inc(s_fade, 1)
                v.tensor_tensor(prob[:, slot, :], p_score[:, :], top[:, slot, 1:GROUP + 1], ALU.subtract)
                v.wait_ge(s_fade, 2 * g + 1)
                v.tensor_tensor(fade2[:, slot, :], fade[:, :], top[:, slot, 1:GROUP + 1], ALU.subtract).then_inc(s_fade, 1)

            def accumulate(g, slot, turn):
                def carry(tile):
                    return 0.0 if isinstance(g, int) and g == 0 else tile[:, 1 - slot, GROUP - 1:GROUP]

                v.wait_ge(s_prob, g + 1)
                v.tensor_tensor(pv[:, :], prob[:, slot, :], vT[:, slot, :], ALU.mult).then_inc(s_pv, 1)
                v.wait_ge(s_faded, g + 1)
                v.tensor_tensor_scan(denom[:, slot, :], fade2[:, slot, :], prob[:, slot, :], carry(denom), ALU.mult, ALU.add)
                v.wait_ge(s_pv, g + 1)
                v.tensor_tensor_scan(numer[:, slot, :], fade2[:, slot, :], pv[:, :], carry(numer), ALU.mult, ALU.add).then_inc(s_scan, 1)

            def finish(g, slot, turn):
                v.wait_ge(s_back, g + 1)
                v.tensor_scalar(inverse[:, :].rearrange("p (j h) -> p j h", j=TILES), p_denom[:, :, 0:C:D1], 1e-16, None, ALU.add).then_inc(s_den, 1)
                v.wait_ge(s_den, 2 * g + 1)
                v.reciprocal(inverse[:, :], inverse[:, :]).then_inc(s_den, 1)
                v.wait_ge(s_den, 2 * g + 2)
                if after(g, 2):
                    v.wait_ge(s_scatter[slot], 64 * turn)
                v.tensor_tensor(outrow[:, slot, :, :].rearrange("p j (h d) -> p (j h) d", h=HEADS1),
                                p_numer[:, :, :].rearrange("p j (h d) -> p (j h) d", h=HEADS1), spread(inverse[:, :], D1), ALU.mult).then_inc(s_out, 1)

            skewed(v, GE, (row_moments, 0), (running_top, 1), (rectify, 0), (accumulate, 1), (normalise, 0), (finish, 1), (score, 0))

        @block.tensor
        def _(pe):
            ident = keep["ident"]
            pe.wait_ge(s_weights, 16 * n_load)
            for i in range(3):
                last = pe.matmul(p_score[:, i:i + 1], raw[:, i, :], norm[:, 1:2], start=True, stop=True)
            last.then_inc(s_ready, 1)
            pe.wait_ge(s_ready, 2)
            pe.wait_ge(s_const, 2)
            pe.wait_ge(s_bias, 1)

            def scores(g, slot, turn):
                pe.wait_ge(s_qk, g + 1)
                pe.matmul(p_score[:, :], heads[:, :], qk[:, slot, :], start=True, stop=True).then_inc(s_score, 1)

            def turn_back(g, slot, turn):
                pe.wait_ge(s_scan, g + 1)
                if after(g, 1):
                    pe.wait_ge(s_out, g)
                for j in range(TILES):
                    pe.transpose(p_numer[:, j, :], numer[:, slot, j * P:(j + 1) * P], ident[:, :])
                    last = pe.transpose(p_denom[:, j, :], denom[:, slot, j * P:(j + 1) * P], ident[:, :])
                last.then_inc(s_back, 1)

            def turns(g, slot, turn):
                if after(g, 1):
                    pe.wait_ge(s_fade, 2 * g)
                if isinstance(g, int) and g == full and tail_dmas:
                    pe.wait_ge(s_tail, 16 * tail_dmas)
                elif not isinstance(g, int) or g < full:
                    pe.wait_ge(s_attr[slot], 16 * (turn + 1))
                pe.transpose(p_score[0:TILES * EDGE_C, 0:P], fold(attr[:, slot, :, :]), ident[:, :]).then_inc(s_attrp, 1)
                pe.wait_ge(s_norm, g + 1)
                if after(g, 1):
                    pe.wait_ge(s_xT, g)
                for k in range(K):
                    last = pe.transpose(p_turn[:, k // TILES, (k % TILES) * P:(k % TILES + 1) * P], normed[:, slot, k, :], ident[:, :])
                last.then_inc(s_turn, 1)

            def project(g, slot, turn):
                pe.wait_ge(s_attrT, g + 1)
                pe.wait_ge(s_xT, g + 1)
                if after(g, 1):
                    pe.wait_ge(s_qk, g)
                    pe.wait_ge(s_vq, g)
                for i, bank in enumerate((p_k, p_v)):
                    pe.matmul(bank[:, :], weight[:, i, :], xT[:, slot, 0, :], start=True, stop=False)
                    for j in range(TILES):
                        last = pe.matmul(bank[:, j * P:(j + 1) * P], w_edge[:, j, :], attrT[:, slot, :], start=False, stop=(j == TILES - 1))
                last.then_inc(s_k, 1)
                pe.matmul(p_q[:, :], weight[:, 2, :], xT[:, slot, 1, :], start=True, stop=True).then_inc(s_qv, 1)

            skewed(pe, GE, (scores, 1), (turn_back, 1), (turns, 0), (project, 0), peel=2)


def nodes1(nc, shape, keep, dram, prm, out):
    N, E, GE, GN = shape
    with ExitStack() as ctx:
        m = Scope(nc, ctx, "n1")
        skip_raw = m.sb("skip_raw", [C, C])
        w_skip = m.sb("w_skip", [C, C])
        skip_row = m.sb("skip_row", [1, C])
        b_skip = m.sb("b_skip", [1, TILES, C])
        norm = m.sb("norm", [C, 4])
        beta_rows = m.sb("beta_rows", [P, 3, C])
        beta_out = m.sb("beta_out", [P, C])
        beta_skip = m.sb("beta_skip", [P, C])
        scratch = m.sb("scratch", [P, 2, C])
        w_gate = m.sb("w_gate", [C, 1])
        b_gate = m.sb("b_gate", [P, 1])
        w1_raw = m.sb("w1_raw", [C, HID])
        w1 = m.sb("w1", [C, HID])
        b1_raw = m.sb("b1_raw", [P, HID // P])
        b1 = m.sb("b1", [P, HID // P])
        w2 = m.sb("w2", [P, HID // P, C])
        b2_row = m.sb("b2_row", [1, C])
        b2 = m.sb("b2", [1, TILES, C])
        ones = m.sb("ones", [1, P])
        rows = m.sb("rows", [P, 2, TILES, C])
        attended = m.sb("attended", [P, 2, TILES, C])
        stats = m.sb("stats", [P, TILES, 6])
        tmp = m.sb("tmp", [P, 4, TILES])
        mean, var, root = (m.sb(n, [P, 2, TILES]) for n in ("mean", "var", "root"))
        rstd = m.sb("rstd", [P, 2, TILES])
        mean2, square, factor = (m.sb(n, [P, TILES]) for n in ("mean2", "square", "factor"))
        var2, root2 = (m.sb(n, [P, 2, TILES]) for n in ("var2", "root2"))
        rectified = m.sb("rectified", [P, 2, TILES, C])
        normed = m.sb("normed", [P, 2, TILES, C])
        xT = m.sb("xT", [P, 2, GROUP])
        weighed = m.sb("weighed", [P, 2, TILES, C])
        h1 = m.sb("h1", [P, 2, TILES, C])
        logit = m.sb("logit", [P, TILES])
        gate = m.sb("gate", [P, 2, TILES])
        beta = m.sb("beta", [P, TILES])
        differ = m.sb("differ", [P, TILES, C])
        blend = m.sb("blend", [P, TILES, C])
        inner = m.sb("inner", [P, 2, TILES, C])
        residual = m.sb("residual", [P, 2, TILES, C])
        mean3, var3, root3 = (m.sb(n, [P, 2, TILES]) for n in ("mean3", "var3", "root3"))
        rstd3 = m.sb("rstd3", [P, TILES])
        normed3 = m.sb("normed3", [P, 2, TILES, C])
        x3T = m.sb("x3T", [P, 2, GROUP])
        hidden = m.sb("hidden", [P, HID // P, GROUP])
        result = m.sb("result", [P, 2, TILES, C])
        p_turn = m.ps("turn", [P, GROUP])
        p_skip = m.ps("skip", [P, TILES, C])
        p_gate = m.ps("gate", [P, GROUP])
        p_turn3 = m.ps("turn3", [P, GROUP])
        p_hid = [m.ps(f"hid{i}", [P, GROUP]) for i in range(2)]
        p_y = [m.ps(f"y{i}", [P, TILES, C]) for i in range(2)]
        s_weights, s_consts, s_prep, s_ready = m.sem("weights"), m.sem("consts"), m.sem("prep"), m.sem("ready")
        s_rows = [m.sem(f"rows{i}") for i in range(2)]
        s_att = [m.sem(f"att{i}") for i in range(2)]
        s_store = [m.sem(f"store{i}") for i in range(2)]
        s_moment, s_var, s_root, s_rstd = (m.sem(n) for n in ("moment", "var", "root", "rstd"))
        s_moment2, s_var2, s_root2, s_norm = (m.sem(n) for n in ("moment2", "var2", "root2", "norm"))
        s_turn, s_xT, s_skip, s_weighed, s_h1 = (m.sem(n) for n in ("turn", "xT", "skip", "weighed", "h1"))
        s_logit, s_gate, s_beta, s_blend, s_inner, s_inner1 = (m.sem(n) for n in ("logit", "gate", "beta", "blend", "inner", "inner1"))
        s_residual, s_moment3, s_var3, s_root3, s_norm3 = (m.sem(n) for n in ("residual", "moment3", "var3", "root3", "norm3"))
        s_turn3, s_x3T, s_up, s_hidden, s_down, s_result = (m.sem(n) for n in ("turn3", "x3T", "up", "hidden", "down", "result"))
        s_factor, s_rstd3, s_chain = m.sem("factor"), m.sem("rstd3"), m.sem("chain")
        CH = HID // P
        s_go = m.sem("go")
        block = m.block()

        @block.sync
        def _(sp):
            def column(vec):
                return vec.rearrange("(p o) -> p o", o=1)

            def row(vec):
                return vec.rearrange("(o n) -> o n", o=1)

            for tile, source in (
                (skip_raw[:, :], prm["Wskip"]), (w1_raw[:, :], prm["W1"]),
                (w2[:, :, :], prm["W2"].rearrange("(k p) c -> p k c", p=P)),
                (norm[:, 0:1], column(prm["ln1_g"])), (norm[:, 1:2], column(prm["ln1_b"])),
                (norm[:, 2:3], column(prm["ln2_g"])), (norm[:, 3:4], column(prm["ln2_b"])),
                (skip_row[:, :], row(prm["bskip"])), (b2_row[:, :], row(prm["b2"])),
            ):
                sp.dma_start(tile, source).then_inc(s_weights, 16)
            for k in range(CH):
                sp.dma_start(b1_raw[:, k:k + 1], column(prm["b1"][k * P:(k + 1) * P])).then_inc(s_weights, 16)
            for k in range(3):
                sp.dma_start(beta_rows[:, k, :], row_of(prm["Wbeta"][k * C:(k + 1) * C, :].rearrange("n o -> (n o)"))).then_inc(s_weights, 16)

            def load(g, slot, turn):
                if after(g, 2):
                    sp.wait_ge(s_moment2, 5 * (g - 1))
                    sp.sem_inc(s_go, 1)
                    sp.wait_ge(s_residual, g - 1)
                    sp.sem_inc(s_go, 1)
                sp.dma_start(rows[:, slot, :, :], node_rows(dram["x1"], GN * GROUP, g)[0]).then_inc(s_rows[slot], 16)
                if after(g, 2):
                    sp.wait_ge(s_blend, 2 * (g - 1))
                    sp.wait_ge(s_weighed, g - 1)
                    sp.sem_inc(s_go, 1)
                sp.dma_start(attended[:, slot, :, :], node_rows(dram["attended"], GN * GROUP, g)[0]).then_inc(s_att[slot], 16)

            def store(g, slot, turn):
                sp.wait_ge(s_result, g + 1)
                sp.sem_inc(s_go, 1)
                target, n = node_rows(out, N, g)
                sp.dma_start(target, result[0:n, slot, :, :]).then_inc(s_store[slot], 16)

            skewed(sp, GN, (load, 0), (store, 3), peel=2)
            for i in range(2):
                sp.wait_ge(s_store[i], 16 * (GN // 2))

        @block.gpsimd
        def _(pool):
            pool.wait_ge(s_ready, 1)

            def weigh(g, slot, turn):
                pool.wait_ge(s_att[slot], 16 * (turn + 1))
                if after(g, 2):
                    pool.wait_ge(s_logit, 2 * (g - 1))
                pool.tensor_tensor(weighed[:, slot, :, :], attended[:, slot, :, :], over(beta_out[:, :], TILES), ALU.mult).then_inc(s_weighed, 1)
                pool.wait_ge(s_moment2, 5 * g + 1)
                if after(g, 2):
                    pool.wait_ge(s_inner, g - 1)
                pool.tensor_tensor(h1[:, slot, :, :], rectified[:, slot, :, :], spread(rstd[:, slot, :], C), ALU.mult).then_inc(s_h1, 1)

            def add(g, slot, turn):
                pool.wait_ge(s_inner, g + 1)
                if after(g, 2):
                    pool.wait_ge(s_result, g - 1)
                pool.tensor_tensor(residual[:, slot, :, :], rows[:, slot, :, :], inner[:, slot, :, :], ALU.add).then_inc(s_residual, 1)

            skewed(pool, GN, (weigh, 0), (add, 1))

        @block.scalar
        def _(act):
            def roots(g, slot, turn):
                act.wait_ge(s_var, g + 1)
                act.activation(root[:, slot, :], var[:, slot, :], ACT.Sqrt, bias=keep["eps"][:, :]).then_inc(s_root, 1)

            def roots2(g, slot, turn):
                act.wait_ge(s_var2, g + 1)
                act.activation(root2[:, slot, :], var2[:, slot, :], ACT.Sqrt, bias=keep["eps"][:, :]).then_inc(s_root2, 1)

            def gates(g, slot, turn):
                act.wait_ge(s_logit, 2 * g + 2)
                act.activation(gate[:, slot, :], logit[:, :], ACT.Exp, scale=-1.0).then_inc(s_gate, 1)

            def columns(g, slot, turn):
                if after(g, 2):
                    act.wait_ge(s_skip, g - 1)
                act.wait_ge(s_turn, g + 1)
                act.activation(xT[:, slot, :], p_turn[:, :], ACT.Copy).then_inc(s_xT, 1)

            def roots3(g, slot, turn):
                act.wait_ge(s_var3, g + 1)
                act.activation(root3[:, slot, :], var3[:, slot, :], ACT.Sqrt, bias=keep["eps"][:, :]).then_inc(s_root3, 1)

            def mlp(g, slot, turn):
                if after(g, 2):
                    act.wait_ge(s_up, CH * (g - 1))
                act.wait_ge(s_turn3, g + 1)
                act.activation(x3T[:, slot, :], p_turn3[:, :], ACT.Copy).then_inc(s_x3T, 1)
                for k in range(CH):
                    if after(g, 1):
                        act.wait_ge(s_down, CH * (g - 1) + k + 1)
                    act.wait_ge(s_up, CH * g + k + 1)
                    act.activation(hidden[:, k, :], p_hid[k % 2][:, :], ACT.Relu, bias=b1[:, k:k + 1]).then_inc(s_hidden, 1)

            act.wait_ge(s_ready, 1)
            skewed(act, GN, (roots, 0), (gates, 1), (roots2, 0), (roots3, 1), (columns, 0), (mlp, 1))

        @block.vector
        def _(v):
            done = [0]

            def chain(instruction):
                done[0] += 1
                instruction.then_inc(s_chain, 1)
                v.wait_ge(s_chain, done[0])

            v.memset(ones[:, :], 1.0).then_inc(s_consts, 1)
            v.wait_ge(s_weights, 16 * (9 + CH + 3))
            v.tensor_scalar(w1[:, :], w1_raw[:, :], norm[:, 2:3], None, ALU.mult)
            v.tensor_tensor(beta_out[:, :], beta_rows[:, 0, :], beta_rows[:, 2, :], ALU.add)
            v.tensor_tensor(beta_skip[:, :], beta_rows[:, 1, :], beta_rows[:, 2, :], ALU.subtract)
            chain(v.tensor_scalar(w_skip[:, :], skip_raw[:, :], norm[:, 0:1], None, ALU.mult))
            v.wait_ge(s_prep, 1)
            v.tensor_tensor(b1[:, :], b1_raw[:, :], p_gate[:, 0:CH], ALU.add)
            for j in range(TILES):
                v.tensor_copy(b2[:, j, :], b2_row[:, :])
                last = v.tensor_tensor(b_skip[:, j, :], skip_row[:, :], p_turn[0:1, 0:C], ALU.add)
            last.then_inc(s_consts, 1)
            v.tensor_tensor(scratch[:, 0, :], w_skip[:, :], beta_skip[:, :], ALU.mult)
            v.wait_ge(s_prep, 2)
            chain(v.tensor_tensor(scratch[:, 1, :], p_skip[:, 0, :], beta_skip[:, :], ALU.mult))
            v.tensor_reduce(w_gate[:, :], scratch[:, 0, :], AX_X, ALU.add)
            v.tensor_reduce(b_gate[:, :], scratch[:, 1, :], AX_X, ALU.add).then_inc(s_ready, 1)
            moment, moment2, moment3 = Chain(v, s_moment, 3), Chain(v, s_moment2, 5), Chain(v, s_moment3, 3)

            def row_moments(g, slot, turn):
                moment.start(g)
                v.wait_ge(s_rows[slot], 16 * (turn + 1))
                moments(v, moment, rows[:, slot], stats, tmp, mean[:, slot, :], var[:, slot, :]).then_inc(s_var, 1)

            def rectify(g, slot, turn):
                v.wait_ge(s_root, g + 1)
                if after(g, 2):
                    v.wait_ge(s_h1, g - 1)
                v.reciprocal(rstd[:, slot, :], root[:, slot, :]).then_inc(s_rstd, 1)
                v.wait_ge(s_rstd, 3 * g + 1)
                moment2.start(g)
                for k in range(TILES):
                    last = v.tensor_scalar(rectified[:, slot, k, :], rows[:, slot, k, :], mean[:, slot, k:k + 1], 0.0, ALU.subtract, ALU.max)
                moment2(last)
                moment2(moments(v, moment2, rectified[:, slot], stats, tmp, mean2[:, :], square[:, :]))
                v.tensor_tensor(square[:, :], square[:, :], rstd[:, slot, :], ALU.mult).then_inc(s_rstd, 1)
                v.wait_ge(s_rstd, 3 * g + 2)
                v.tensor_tensor(var2[:, slot, :], square[:, :], rstd[:, slot, :], ALU.mult).then_inc(s_var2, 1)

            def normalise(g, slot, turn):
                v.wait_ge(s_root2, g + 1)
                v.reciprocal(factor[:, :], root2[:, slot, :]).then_inc(s_rstd, 1)
                v.wait_ge(s_rstd, 3 * g + 3)
                v.tensor_tensor(factor[:, :], factor[:, :], rstd[:, slot, :], ALU.mult).then_inc(s_factor, 1)
                if after(g, 2):
                    v.wait_ge(s_turn, g - 1)
                v.wait_ge(s_factor, g + 1)
                for k in range(TILES):
                    last = v.tensor_scalar(normed[:, slot, k, :], rectified[:, slot, k, :], mean2[:, k:k + 1], factor[:, k:k + 1], ALU.subtract, ALU.mult)
                last.then_inc(s_norm, 1)

            def logits(g, slot, turn):
                v.wait_ge(s_weighed, g + 1)
                v.tensor_reduce(logit[:, :], weighed[:, slot, :, :], AX_X, ALU.add).then_inc(s_logit, 1)
                v.wait_ge(s_logit, 2 * g + 1)
                v.wait_ge(s_skip, g + 1)
                v.scalar_tensor_tensor(out=logit[:, :], in0=p_gate[:, 0:TILES], scalar=b_gate[:, 0:1], in1=logit[:, :],
                                       op0=ALU.add, op1=ALU.add).then_inc(s_logit, 1)
                v.tensor_tensor(differ[:, :, :], p_skip[:, :, :], attended[:, slot, :, :], ALU.subtract).then_inc(s_blend, 1)

            def blends(g, slot, turn):
                v.wait_ge(s_gate, g + 1)
                chain3(v.tensor_scalar(beta[:, :], gate[:, slot, :], 1.0, None, ALU.add), g, 1)
                chain3(v.reciprocal(beta[:, :], beta[:, :]), g, 2)
                v.wait_ge(s_blend, 2 * g + 1)
                for k in range(TILES):
                    last = v.scalar_tensor_tensor(out=blend[:, k, :], in0=differ[:, k, :], scalar=beta[:, k:k + 1], in1=attended[:, slot, k, :],
                                                  op0=ALU.mult, op1=ALU.add)
                last.then_inc(s_blend, 1)
                v.wait_ge(s_blend, 2 * g + 2)
                v.wait_ge(s_h1, g + 1)
                if after(g, 2):
                    v.wait_ge(s_residual, g - 1)
                v.tensor_tensor(inner[:, slot, :, :], blend[:, :, :], h1[:, slot, :, :], ALU.add).then_inc(s_inner, 1)

            def chain3(instruction, g, step):
                instruction.then_inc(s_beta, 1)
                v.wait_ge(s_beta, 2 * g + step)

            def inner_moments(g, slot, turn):
                moment3.start(g)
                v.wait_ge(s_inner, g + 1)
                moments(v, moment3, inner[:, slot], stats, tmp, mean3[:, slot, :], var3[:, slot, :]).then_inc(s_var3, 1)

            def normalise3(g, slot, turn):
                v.wait_ge(s_root3, g + 1)
                v.reciprocal(rstd3[:, :], root3[:, slot, :]).then_inc(s_rstd3, 1)
                if after(g, 2):
                    v.wait_ge(s_turn3, g - 1)
                v.wait_ge(s_rstd3, g + 1)
                for k in range(TILES):
                    last = v.tensor_scalar(normed3[:, slot, k, :], inner[:, slot, k, :], mean3[:, slot, k:k + 1], rstd3[:, k:k + 1], ALU.subtract, ALU.mult)
                last.then_inc(s_norm3, 1)

            def finish(g, slot, turn):
                v.wait_ge(s_down, CH * (g + 1))
                v.wait_ge(s_residual, g + 1)
                if after(g, 2):
                    v.wait_ge(s_store[slot], 16 * turn)
                v.tensor_tensor(result[:, slot, :, :], p_y[slot][:, :, :], residual[:, slot, :, :], ALU.add).then_inc(s_result, 1)

            skewed(v, GN, (row_moments, 0), (logits, 1), (rectify, 0), (blends, 1), (normalise, 0), (inner_moments, 1),
                   (finish, 2), (normalise3, 1))

        @block.tensor
        def _(pe):
            ident = keep["ident"]
            pe.wait_ge(s_weights, 16 * (9 + CH + 3))
            pe.matmul(p_turn[0:1, 0:C], norm[:, 1:2], skip_raw[:, :], start=True, stop=True)
            for k in range(CH):
                last = pe.matmul(p_gate[:, k:k + 1], w1_raw[:, k * P:(k + 1) * P], norm[:, 3:4], start=True, stop=True)
            last.then_inc(s_prep, 1)
            pe.wait_ge(s_consts, 2)
            pe.matmul(p_skip[:, 0, :], ones[:, :], b_skip[:, 0, :], start=True, stop=True).then_inc(s_prep, 1)
            pe.wait_ge(s_ready, 1)

            def turns(g, slot, turn):
                pe.wait_ge(s_norm, g + 1)
                if after(g, 1):
                    pe.wait_ge(s_xT, g)
                for k in range(TILES):
                    last = pe.transpose(p_turn[:, k * P:(k + 1) * P], normed[:, slot, k, :], ident[:, :])
                last.then_inc(s_turn, 1)

            def skips(g, slot, turn):
                pe.wait_ge(s_xT, g + 1)
                if after(g, 1):
                    pe.wait_ge(s_blend, 2 * g - 1)
                    pe.wait_ge(s_logit, 2 * g)
                pe.matmul(fold(p_skip[:, :, :]), ones[:, :], fold(b_skip[:, :, :]), start=True, stop=False)
                for j in range(TILES):
                    pe.matmul(p_skip[:, j, :], xT[:, slot, j * P:(j + 1) * P], w_skip[:, :], start=False, stop=(j == TILES - 1))
                    last = pe.matmul(p_gate[:, j:j + 1], xT[:, slot, j * P:(j + 1) * P], w_gate[:, :], start=True, stop=True)
                last.then_inc(s_skip, 1)

            def mlp(g, slot, turn):
                pe.wait_ge(s_norm3, g + 1)
                if after(g, 1):
                    pe.wait_ge(s_x3T, g)
                for k in range(TILES):
                    last = pe.transpose(p_turn3[:, k * P:(k + 1) * P], normed3[:, slot, k, :], ident[:, :])
                last.then_inc(s_turn3, 1)
                pe.wait_ge(s_x3T, g + 1)
                if after(g, 2):
                    pe.wait_ge(s_result, g - 1)
                y = p_y[slot]
                pe.matmul(fold(y[:, :, :]), ones[:, :], fold(b2[:, :, :]), start=True, stop=False)

                def up(k):
                    if after(g, 1) or k >= 2:
                        pe.wait_ge(s_hidden, CH * g + k - 1)
                    pe.matmul(p_hid[k % 2][:, :], w1[:, k * P:(k + 1) * P], x3T[:, slot, :], start=True, stop=True).then_inc(s_up, 1)

                def down(k):
                    pe.wait_ge(s_hidden, CH * g + k + 1)
                    for j in range(TILES):
                        last = pe.matmul(y[:, j, :], hidden[:, k, j * P:(j + 1) * P], w2[:, k, :], start=False, stop=(k == CH - 1 and j == TILES - 1))
                    last.then_inc(s_down, 1)

                up(0)
                up(1)
                down(0)
                up(2)
                down(1)
                up(3)
                down(2)
                down(3)

            skewed(pe, GN, (turns, 0), (skips, 0), (mlp, 1))


def build(nc, a, out):
    N, E = a["x"].shape[0], a["src"].shape[0]
    GE, GN = -(-E // GROUP), -(-N // GROUP)
    assert N % TILES == 0 and GE % 2 == 0 and GN % 2 == 0 and GE <= P and GN <= 2 * P
    shape = (N, E, GE, GN)
    dram = {name: nc.dram_tensor(name, dims, F32).ap() for name, dims in (
        ("mixed", (GN * GROUP, C)), ("attended", (GN * GROUP, C)), ("x1", (GN * GROUP, C)),
        ("same", (GE, GROUP)), ("factor", (GE, 2, GROUP)), ("dinv", (GN * GROUP, 1)))}
    with ExitStack() as ctx:
        def sb(name, dims, dt=F32):
            return ctx.enter_context(nc.sbuf_tensor(name, dims, dt))

        keep = dict(ident=sb("ident", [P, P]), eps=sb("eps", [P, 1]), one=sb("one", [P, 1]),
                    index=sb("index", [P, 3, TILES * GE], I32),
                    selfw=sb("selfw", [P, TILES, GN]), lonew=sb("lonew", [P, TILES, GN]))
        prepare(nc, shape, keep, dram, a["src"], a["dst"])
        edges0(nc, shape, keep, dram, a["x"], a["L0_gnn_bases_W"], a["L0_gnn_comb_W"], a["L0_gnn_comb_b"])
        nodes0(nc, shape, keep, dram, a["x"], a["L0_gnn_bases_W"], a["L0_gnn_comb_W"], a["L0_gnn_comb_b"], a["L0_gnn_bias"])
        prm = {n[len("L1_gnn_"):]: v for n, v in a.items() if n.startswith("L1_gnn_")}
        edges1(nc, shape, keep, dram, a["edge_attr_4"], prm["ln1_g"], prm["ln1_b"],
               {"k": prm["Wk"], "v": prm["Wv"], "q": prm["Wq"]}, {"k": prm["bk"], "v": prm["bv"], "q": prm["bq"]}, prm["We"])
        nodes1(nc, shape, keep, dram, prm, out)


def kernel(**inputs):
    import numpy as np
    import concourse.bacc as bacc
    from concourse.bass_utils import run_bass_kernel_spmd

    nc = bacc.Bacc("TRN2", target_bir_lowering=False, num_devices=1)
    arrays, views = {}, {}
    for name, value in inputs.items():
        array = np.ascontiguousarray(value)
        arrays[f"in_{name}"] = array
        views[name] = nc.dram_tensor(f"in_{name}", array.shape, mybir.dt.from_np(array.dtype), kind="ExternalInput").ap()
    out = nc.dram_tensor("out_x", tuple(inputs["x"].shape), F32, kind="ExternalOutput").ap()
    build(nc, views, out)
    result = run_bass_kernel_spmd(nc, [arrays], core_ids=[0])
    return result.results[0]["out_x"]
```

```python
from contextlib import ExitStack

import concourse.bass as bass
from concourse import mybir

ALU = mybir.AluOpType
ACT = mybir.ActivationFunctionType
F32 = mybir.dt.float32
F16 = mybir.dt.float16
BF16 = mybir.dt.bfloat16
I32 = mybir.dt.int32
AX_X = mybir.AxisListType.X

P = 128
TILES = 4
GROUP = P * TILES
C = 128
EPS = 1e-5
NOWHERE = 1 << 20
HUGE = 3.0e38
INV_E = 0.36787944117144233

HEADS0, BASES, AGGS = 8, 4, 4
D0 = C // HEADS0
BD = BASES * D0
MIX = BASES * AGGS
AGG_ORDER = (1, 0, 3, 2)
HEADS1 = 4
D1 = C // HEADS1
EDGE_C = 4
HID = 4 * C


def after(g, n):
    return not isinstance(g, int) or g >= n


def skewed(eng, count, *stages, peel=0, width=2):
    deepest = max(lag for _, lag in stages)
    head = width * -(-(deepest + width) // width)
    steps = max(0, (count - peel - head) // width)

    def peeled(begin, end):
        for t in range(begin, end):
            for stage, lag in stages:
                if 0 <= t - lag < count:
                    stage(t - lag, (t - lag) % width, (t - lag) // width)

    peeled(0, head)
    if steps:
        with eng.Fori(0, steps) as k:
            for u in range(width):
                for stage, lag in stages:
                    slot = (u - lag) % width
                    turn = k + (head + u - lag - slot) // width
                    stage(turn * width + slot, slot, turn)
    peeled(head + width * steps, count + deepest)


def row_of(vec):
    return vec.rearrange("(o n) -> o n", o=1).to_broadcast([P, vec.shape[0]])


def fold(ap):
    return ap.rearrange("p a b -> p (a b)")


def spread(ap, n):
    return ap.rearrange("p (a o) -> p a o", o=1).to_broadcast([ap.shape[0], ap.shape[1], n])


def over(ap, n):
    return ap.rearrange("p (o a) -> p o a", o=1).to_broadcast([ap.shape[0], n, ap.shape[1]])


class Scope:

    def __init__(self, nc, ctx, tag):
        self.nc, self.ctx, self.tag = nc, ctx, tag
        self.sems = []

    def sb(self, name, shape, dt=F32):
        return self.ctx.enter_context(self.nc.sbuf_tensor(f"{self.tag}_{name}", list(shape), dt))

    def ps(self, name, shape, dt=F32):
        return self.ctx.enter_context(self.nc.psum_tensor(f"{self.tag}_ps_{name}", list(shape), dt))

    def sem(self, name):
        self.sems.append(self.ctx.enter_context(self.nc.semaphore(f"{self.tag}_{name}")))
        return self.sems[-1]

    def clear(self):
        for sem in self.sems:
            self.nc.sync.sem_clear(sem)

    def block(self):
        self.ctx.callback(self.clear)
        return self.ctx.enter_context(self.nc.Block())


def prepare(nc, shape, keep, dram, src, dst):
    N, E, GE, GN = shape
    HB = GN // 2
    with ExitStack() as ctx:
        m = Scope(nc, ctx, "pre")
        dst_i = m.sb("dst_i", [GE, GROUP], I32)
        src_i = m.sb("src_i", [GE, GROUP], I32)
        part_i = m.sb("part_i", [GE, 2, GROUP], I32)
        edge_i = m.sb("edge_i", [GE, 2], I32)
        edge_f = m.sb("edge_f", [GE, 2])
        dst_f = m.sb("dst_f", [GE, GROUP])
        same = m.sb("same", [GE, GROUP])
        same_next = m.sb("same_next", [GE, 1])
        cols = m.sb("cols", [GE, 5, GROUP])
        place_i = m.sb("place_i", [GE, GROUP], I32)
        place = m.sb("place", [GE, GROUP])
        begin = m.sb("begin", [GE, GROUP])
        zero_row = m.sb("zero_row", [GE, GROUP])
        begin_row = m.sb("begin_row", [1, GE + 1])
        factor = m.sb("factor", [GE, 2, GROUP])
        parts = m.sb("parts", [P, 2, TILES * GE])
        zeros = m.sb("zeros", [P, 3584])
        count_i = m.sb("count_i", [P, GROUP], I32)
        ramp = m.sb("ramp", [P, GROUP], F16)
        hot = m.sb("hot", [P, 2, TILES, GROUP + GN], BF16)
        counts = m.sb("counts", [HB, 2, GROUP])
        degree = m.sb("degree", [HB, 2, GROUP])
        dinv = m.sb("dinv", [HB, 2, GROUP])
        turned = [m.ps(f"turned{i}", [P, TILES * GE]) for i in range(5)]
        hist = [m.ps(f"hist{i}", [HB, GROUP]) for i in range(2)]
        s_blank, s_load, s_zero, s_fill = m.sem("blank"), m.sem("load"), m.sem("zero"), m.sem("fill")
        s_id, s_iota, s_ramp, s_chain = m.sem("id"), m.sem("iota"), m.sem("ramp"), m.sem("chain")
        s_last, s_carry, s_runs, s_runroot = m.sem("last"), m.sem("carry"), m.sem("runs"), m.sem("runroot")
        s_same, s_cols, s_turned, s_parts = m.sem("same"), m.sem("cols"), m.sem("turned"), m.sem("parts")
        s_hot, s_hist, s_counts, s_root = m.sem("hot"), m.sem("hist"), m.sem("counts"), m.sem("root")
        s_dinv, s_store, s_node, s_taken = m.sem("dinv"), m.sem("store"), m.sem("node"), m.sem("taken")
        full = (GE - 1) * GROUP
        table = GN * GROUP * C // P
        fills = []
        at = 0
        while at < table:
            fills.append((at, min(3584, table - at)))
            at += 3584
        block = m.block()

        @block.sync
        def _(sp):
            sp.wait_ge(s_blank, 3)
            sp.dma_start(dst_i[0:GE - 1, :], dst[0:full].rearrange("(g c) -> g c", c=GROUP)).then_inc(s_load, 16)
            sp.dma_start(dst_i[GE - 1:GE, 0:E - full], dst[full:E].rearrange("(o c) -> o c", o=1)).then_inc(s_load, 16)
            sp.dma_start(src_i[0:GE - 1, :], src[0:full].rearrange("(g c) -> g c", c=GROUP)).then_inc(s_load, 16)
            sp.dma_start(src_i[GE - 1:GE, 0:E - full], src[full:E].rearrange("(o c) -> o c", o=1)).then_inc(s_load, 16)
            sp.dma_start(edge_i[1:GE, 0:1], dst[0:full].rearrange("(g c) -> g c", c=GROUP)[:, GROUP - 1:GROUP], allow_slow_non_contiguous=True).then_inc(s_load, 16)
            sp.dma_start(edge_i[0:GE - 2, 1:2], dst[GROUP:full].rearrange("(g c) -> g c", c=GROUP)[:, 0:1], allow_slow_non_contiguous=True).then_inc(s_load, 16)
            sp.dma_start(edge_i[GE - 2:GE - 1, 1:2], dst[full:full + 1].rearrange("(o c) -> o c", o=1)).then_inc(s_load, 16)
            sp.wait_ge(s_zero, 1)
            for name in ("mixed", "attended"):
                rows = dram[name].rearrange("(p r) c -> p (r c)", p=P)
                for a, n in fills:
                    sp.dma_start(rows[:, a:a + n], zeros[:, 0:n]).then_inc(s_fill, 16)
            sp.wait_ge(s_same, 1)
            sp.dma_start(dram["same"], same[:, :]).then_inc(s_store, 16)
            sp.wait_ge(s_runs, 3)
            sp.dma_start(dram["factor"].rearrange("g k c -> g (k c)"), factor[:, :, :].rearrange("g k c -> g (k c)")).then_inc(s_store, 16)
            sp.wait_ge(s_dinv, 1)
            sp.dma_start(dram["dinv"].rearrange("(b g c) o -> g b (c o)", b=2, c=GROUP), dinv[:, :, :]).then_inc(s_store, 16)
            sp.wait_ge(s_store, 48)
            sp.wait_ge(s_fill, 16 * 2 * len(fills))

        @block.gpsimd
        def _(pool):
            pool.iota(count_i[:, :], pattern=[[1, GROUP]], base=0, channel_multiplier=0).then_inc(s_iota, 1)
            pool.iota(place_i[:, :], pattern=[[1, GROUP]], base=0, channel_multiplier=GROUP).then_inc(s_iota, 1)
            pool.memset(keep["ident"][:, :], 0.0).then_inc(s_id, 1)
            pool.wait_ge(s_id, 1)
            pool.affine_select(out=keep["ident"][:, :], in_=keep["ident"][:, :], compare_op=ALU.not_equal, fill=1.0,
                               base=0, pattern=[[-1, P]], channel_multiplier=1).then_inc(s_id, 1)

        @block.scalar
        def _(act):
            act.wait_ge(s_runs, 1)
            act.activation(factor[:, 1, :], factor[:, 0, :], ACT.Sqrt, bias=keep["one"][0:GE, :]).then_inc(s_runroot, 1)
            act.wait_ge(s_counts, 2)
            act.activation(dinv[:, :, :], degree[:, :, :], ACT.Sqrt).then_inc(s_root, 1)

        @block.vector
        def _(v):
            done = [0]

            def chain(instruction):
                done[0] += 1
                instruction.then_inc(s_chain, 1)
                v.wait_ge(s_chain, done[0])

            v.memset(dst_i[:, :], NOWHERE).then_inc(s_blank, 1)
            v.memset(src_i[:, :], 0).then_inc(s_blank, 1)
            v.memset(edge_i[:, 0:1], -1)
            v.memset(edge_i[:, 1:2], NOWHERE).then_inc(s_blank, 1)
            v.memset(zeros[:, :], 0.0).then_inc(s_zero, 1)
            v.memset(keep["eps"][:, :], EPS)
            v.memset(keep["one"][:, :], 1.0)
            v.memset(zero_row[:, :], 0.0)
            v.wait_ge(s_iota, 2)
            v.tensor_copy(ramp[:, :], count_i[:, :]).then_inc(s_ramp, 1)
            v.wait_ge(s_load, 16 * 7)
            v.tensor_copy(edge_f[:, :], edge_i[:, :])
            v.tensor_copy(cols[:, 0, :], src_i[:, :])
            v.tensor_scalar(part_i[:, 0, :], dst_i[:, :], 9, None, ALU.logical_shift_right)
            v.tensor_scalar(part_i[:, 1, :], dst_i[:, :], GROUP - 1, None, ALU.bitwise_and)
            chain(v.tensor_copy(dst_f[:, :], dst_i[:, :]))
            v.tensor_copy(cols[:, 3:5, :], part_i[:, :, :])
            v.tensor_scalar(cols[:, 1, :], dst_f[:, :], float(N - 1), None, ALU.min)
            v.tensor_tensor(same[:, 1:GROUP], dst_f[:, 1:GROUP], dst_f[:, 0:GROUP - 1], ALU.is_equal)
            v.tensor_tensor(same[:, 0:1], dst_f[:, 0:1], edge_f[:, 0:1], ALU.is_equal).then_inc(s_same, 1)
            chain(v.tensor_tensor(same_next[:, :], dst_f[:, GROUP - 1:GROUP], edge_f[:, 1:2], ALU.is_equal))
            v.scalar_tensor_tensor(out=cols[:, 2, 0:GROUP - 1], in0=same[:, 1:GROUP], scalar=float(NOWHERE),
                                   in1=dst_f[:, 0:GROUP - 1], op0=ALU.mult, op1=ALU.max)
            v.scalar_tensor_tensor(out=cols[:, 2, GROUP - 1:GROUP], in0=same_next[:, :], scalar=float(NOWHERE),
                                   in1=dst_f[:, GROUP - 1:GROUP], op0=ALU.mult, op1=ALU.max).then_inc(s_cols, 1)
            chain(v.tensor_scalar(begin[:, :], same[:, :], -1.0, 1.0, ALU.mult, ALU.add))
            chain(v.tensor_copy(place[:, :], place_i[:, :]))
            chain(v.tensor_tensor(begin[:, :], begin[:, :], place[:, :], ALU.mult))
            v.tensor_tensor_scan(begin[:, :], zero_row[:, :], begin[:, :], 0.0, ALU.add, ALU.max).then_inc(s_last, 1)
            v.wait_ge(s_carry, 1)
            v.memset(begin_row[:, 0:1], 0.0)
            v.tensor_tensor_scan(begin_row[:, 1:GE + 1], zero_row[0:1, 0:GE], turned[0][0:1, 0:GE], 0.0, ALU.add, ALU.max).then_inc(s_last, 1)
            v.wait_ge(s_carry, 2)
            chain(v.tensor_scalar(begin[:, :], begin[:, :], turned[1][0:GE, 0:1], None, ALU.max))
            chain(v.tensor_tensor(factor[:, 0, :], place[:, :], begin[:, :], ALU.subtract))
            v.tensor_scalar(factor[:, 0, :], factor[:, 0, :], 1.0, None, ALU.add).then_inc(s_runs, 1)
            v.wait_ge(s_runroot, 1)
            v.reciprocal(factor[:, :, :], factor[:, :, :]).then_inc(s_runs, 2)
            for i in range(3):
                v.wait_ge(s_turned, i + 1)
                v.tensor_copy(keep["index"][:, i, :], turned[i][:, :])
            for i in range(2):
                v.wait_ge(s_turned, i + 4)
                last = v.tensor_copy(parts[:, i, :], turned[3 + i][:, :])
            last.then_inc(s_parts, 1)
            v.wait_ge(s_parts, 1)
            v.wait_ge(s_ramp, 1)

            def one_hot(g, slot, turn):
                if after(g, 2):
                    v.wait_ge(s_hist, g - 1)
                for j in range(TILES):
                    v.tensor_scalar(hot[:, slot, j, 0:GROUP], ramp[:, :], parts[:, 1, bass.ds(g + j * GE, 1)], None, ALU.is_equal)
                    last = v.tensor_scalar(hot[:, slot, j, GROUP:GROUP + GN], ramp[:, 0:GN],
                                           parts[:, 0, bass.ds(g + j * GE, 1)], None, ALU.is_equal)
                last.then_inc(s_hot, 1)

            skewed(v, GE, (one_hot, 0))
            v.wait_ge(s_hist, GE)
            for b in range(2):
                v.tensor_copy(counts[:, b, :], hist[b][:, :])
                last = v.tensor_scalar(degree[:, b, :], hist[b][:, :], 1.0, None, ALU.add)
            last.then_inc(s_counts, 2)
            v.wait_ge(s_root, 1)
            v.reciprocal(dinv[:, :, :], dinv[:, :, :]).then_inc(s_dinv, 1)
            for j in range(TILES):
                v.wait_ge(s_node, j + 1)
                taken = turned[j][:, 0:GN]
                chain(v.tensor_scalar(keep["selfw"][:, j, :], taken, 1.0, None, ALU.add))
                v.reciprocal(keep["selfw"][:, j, :], keep["selfw"][:, j, :])
                v.tensor_scalar(keep["lonew"][:, j, :], taken, 0.0, float(EPS) ** 0.5, ALU.is_equal, ALU.mult).then_inc(s_taken, 1)

        @block.tensor
        def _(pe):
            ident = keep["ident"]
            pe.wait_ge(s_id, 2)
            pe.wait_ge(s_last, 1)
            pe.transpose(turned[0][0:1, 0:GE], begin[:, GROUP - 1:GROUP], ident[0:GE, 0:GE]).then_inc(s_carry, 1)
            pe.wait_ge(s_last, 2)
            pe.transpose(turned[1][0:GE, 0:1], begin_row[:, 0:GE], ident[0:1, 0:1]).then_inc(s_carry, 1)
            pe.wait_ge(s_runs, 1)
            pe.wait_ge(s_cols, 1)
            for i in range(5):
                for j in range(TILES):
                    last = pe.transpose(turned[i][:, j * GE:(j + 1) * GE], cols[:, i, j * P:(j + 1) * P], ident[0:GE, 0:GE])
                last.then_inc(s_turned, 1)

            def histogram(g, slot, turn):
                pe.wait_ge(s_hot, g + 1)
                for j in range(TILES):
                    first = isinstance(g, int) and g == 0 and j == 0
                    final = isinstance(g, int) and g == GE - 1 and j == TILES - 1
                    for b in range(2):
                        last = pe.matmul(hist[b][:, :], hot[:, slot, j, GROUP + b * HB:GROUP + (b + 1) * HB],
                                         hot[:, slot, j, 0:GROUP], start=first, stop=final)
                last.then_inc(s_hist, 1)

            skewed(pe, GE, (histogram, 1))
            pe.wait_ge(s_counts, 2)
            pe.wait_ge(s_parts, 1)
            for j in range(TILES):
                for b in range(2):
                    last = pe.transpose(turned[j][:, b * HB:(b + 1) * HB], counts[:, b, j:GROUP:TILES], ident[0:HB, 0:HB])
                last.then_inc(s_node, 1)


class Chain:

    def __init__(self, eng, sem, steps):
        self.eng, self.sem, self.steps = eng, sem, steps

    def start(self, g):
        self.at = g * self.steps

    def __call__(self, instruction):
        instruction.then_inc(self.sem, 1)
        self.at = self.at + 1
        self.eng.wait_ge(self.sem, self.at)


def moments(v, chain, rows, stats, tmp, mean, var, less=False):
    for k in range(rows.shape[1]):
        last = v.bn_stats(stats[:, k, :], rows[:, k, :])
    chain(last)
    v.tensor_tensor(tmp[:, 0, :], stats[:, :, 1], stats[:, :, 4], ALU.add)
    v.tensor_tensor(tmp[:, 1, :], stats[:, :, 1], stats[:, :, 4], ALU.subtract)
    chain(v.tensor_tensor(tmp[:, 2, :], stats[:, :, 2], stats[:, :, 5], ALU.add))
    v.tensor_scalar(mean, tmp[:, 0, :], -0.5 if less else 0.5, None, ALU.mult)
    chain(v.scalar_tensor_tensor(out=tmp[:, 3, :], in0=tmp[:, 1, :], scalar=0.25, in1=tmp[:, 1, :],
                                 op0=ALU.mult, op1=ALU.mult))
    return v.scalar_tensor_tensor(out=var, in0=tmp[:, 2, :], scalar=1.0 / C, in1=tmp[:, 3, :],
                                  op0=ALU.mult, op1=ALU.add)


def index_of(keep, GE, kinds, g):
    a, b = kinds
    return keep["index"][:, a:b, :].rearrange("p k (j g) -> p (k j) g", g=GE)[:, :, bass.ds(g, 1)]


def bf16_parts(chain, v, target, source, remain):
    chain(v.tensor_copy(remain, source))
    for i in range(3):
        chain(v.tensor_copy(target[i], remain))
        chain(v.tensor_tensor(remain, remain, target[i], ALU.subtract))


def edges0(nc, shape, keep, dram, x, bases_W, comb_W, comb_b):
    N, E, GE, GN = shape
    K = 2 * TILES
    with ExitStack() as ctx:
        m = Scope(nc, ctx, "e0")
        w_bases = m.sb("w_bases", [C, 2 * BD])
        w_raw = m.sb("w_raw", [C, HEADS0 * MIX])
        w_mix = m.sb("w_mix", [C, HEADS0 * MIX])
        b_raw = m.sb("b_raw", [1, HEADS0 * MIX])
        b_mix = m.sb("b_mix", [1, HEADS0 * MIX])
        b_rest = m.sb("b_rest", [1, HEADS0 * MIX])
        b_parts = m.sb("b_parts", [1, 3, TILES, HEADS0 * MIX], BF16)
        ones = m.sb("ones", [1, P], BF16)
        gidx = m.sb("gidx", [P, 2, K], I32)
        sidx = m.sb("sidx", [P, 2, TILES], I32)
        rows = m.sb("rows", [P, 2, K, C])
        scale = m.sb("scale", [P, 2, TILES])
        same = m.sb("same", [P, 2, GROUP])
        barrier = m.sb("barrier", [P, 2, GROUP])
        stats = m.sb("stats", [P, K, 6])
        tmp = m.sb("tmp", [P, 4, K])
        lessmean, var, root, rstd, shift = (m.sb(n, [P, 2, K]) for n in ("lessmean", "var", "root", "rstd", "shift"))
        normed = m.sb("normed", [P, 2, K, C])
        hT = m.sb("hT", [P, 2, 2, GROUP])
        wide = m.sb("wide", [P, 2, TILES, P])
        twin = m.sb("twin", [P, 2, GROUP])
        square = m.sb("square", [BD, 2, GROUP])
        value = m.sb("value", [P, GROUP])
        factor = m.sb("factor", [P, 2, GROUP])
        total = m.sb("total", [P, 2, GROUP])
        total_sq = m.sb("total_sq", [BD, 2, GROUP])
        aggs = m.sb("aggs", [P, 2, 2, GROUP])
        msq = m.sb("msq", [BD, 2, GROUP])
        mean_sq = m.sb("mean_sq", [BD, GROUP])
        top = m.sb("top", [P, TILES * HEADS0])
        mix = m.sb("mix", [P, 2, TILES, HEADS0 * MIX])
        mixsum = m.sb("mixsum", [P, TILES * HEADS0])
        inverse = m.sb("inverse", [P, 2, TILES * HEADS0])
        prod = m.sb("prod", [P, TILES, MIX, C])
        outrow = m.sb("outrow", [P, 2, TILES, C])
        p_turn = m.ps("turn", [P, GROUP])
        p_twin = m.ps("twin", [P, GROUP])
        p_wide = m.ps("wide", [P, GROUP])
        p_mix = m.ps("mix", [P, TILES, HEADS0 * MIX])
        p_aggs = m.ps("aggs", [P, TILES, 2 * P])
        p_out = [m.ps(f"out{i}", [P, TILES, C]) for i in range(2)]
        s_weights, s_prep, s_ready = m.sem("weights"), m.sem("prep"), m.sem("ready")
        s_gidx, s_sidx, s_issue = m.sem("gidx"), m.sem("sidx"), m.sem("issue")
        s_rows = [m.sem(f"rows{i}") for i in range(2)]
        s_dinv = [m.sem(f"dinv{i}") for i in range(2)]
        s_same = [m.sem(f"same{i}") for i in range(2)]
        s_scatter = [m.sem(f"scatter{i}") for i in range(2)]
        s_factor = [m.sem(f"factor{i}") for i in range(2)]
        s_moment, s_var, s_root, s_rstd, s_shift, s_norm = (m.sem(n) for n in ("moment", "var", "root", "rstd", "shift", "norm"))
        s_turn, s_hT, s_wide, s_bases, s_scales, s_mix = (m.sem(n) for n in ("turn", "hT", "wide", "bases", "scales", "mix"))
        s_twin, s_top, s_sub, s_exp, s_barrier = (m.sem(n) for n in ("twin", "top", "sub", "exp", "barrier"))
        s_scan, s_mean, s_meansq, s_less, s_varb, s_std = (m.sem(n) for n in ("scan", "mean", "meansq", "less", "varb", "std"))
        s_aggs, s_mixsum, s_inverse, s_prod, s_reduced = (m.sem(n) for n in ("aggs", "mixsum", "inverse", "prod", "reduced"))
        s_out = m.sem("out")
        s_go = m.sem("go")
        block = m.block()

        @block.sync
        def _(sp):
            sp.dma_start(w_bases[:, 0:BD].rearrange("c (b d) -> c b d", b=BASES), bases_W.rearrange("b c d -> c b d")).then_inc(s_weights, 16)
            sp.dma_start(w_bases[:, BD:2 * BD].rearrange("c (b d) -> c b d", b=BASES), bases_W.rearrange("b c d -> c b d")).then_inc(s_weights, 16)
            sp.dma_start(w_raw[:, :], comb_W).then_inc(s_weights, 16)
            sp.dma_start(b_raw[:, :], comb_b.rearrange("(o n) -> o n", o=1)).then_inc(s_weights, 16)

            def load(g, slot, turn):
                if after(g, 2):
                    sp.wait_ge(s_scan, 2 * (g - 1))
                    sp.sem_inc(s_go, 1)
                    sp.wait_ge(s_barrier, g - 1)
                    sp.sem_inc(s_go, 1)
                sp.dma_start(same[:, slot, :], dram["same"][bass.ds(g, 1), :].to_broadcast([P, GROUP])).then_inc(s_same[slot], 16)
                if after(g, 2):
                    sp.wait_ge(s_mean, g - 1)
                    sp.sem_inc(s_go, 1)
                for i in range(2):
                    sp.dma_start(factor[i * BD:(i + 1) * BD, slot, :],
                                 dram["factor"][bass.ds(g, 1), i, :].to_broadcast([BD, GROUP])).then_inc(s_factor[slot], 16)

            skewed(sp, GE, (load, 0))

        @block.gpsimd
        def _(pool):
            def gather(g, slot, turn):
                if after(g, 2):
                    pool.wait_ge(s_norm, g - 1)
                    pool.wait_ge(s_wide, g - 1)
                    pool.sem_inc(s_issue, 1)
                pool.tensor_copy(gidx[:, slot, :].rearrange("p (k o) -> p k o", o=1), index_of(keep, GE, (0, 2), g)).then_inc(s_gidx, 1)
                pool.wait_ge(s_gidx, g + 1)
                pool.sem_inc(s_issue, 1)
                for k in range(K):
                    pool.indirect_dma_start(rows[:, slot, k, :], None, x, bass.IndirectOffsetOnAxis(ap=gidx[:, slot, k:k + 1], axis=0)).then_inc(s_rows[slot], 16)
                for k in range(TILES):
                    pool.indirect_dma_start(scale[:, slot, k:k + 1], None, dram["dinv"],
                                            bass.IndirectOffsetOnAxis(ap=gidx[:, slot, k:k + 1], axis=0)).then_inc(s_dinv[slot], 16)

            def scatter(g, slot, turn):
                if after(g, 2):
                    pool.wait_ge(s_scatter[slot], 64 * turn)
                    pool.sem_inc(s_issue, 1)
                pool.tensor_copy(sidx[:, slot, :].rearrange("p (k o) -> p k o", o=1), index_of(keep, GE, (2, 3), g)).then_inc(s_sidx, 1)
                pool.wait_ge(s_sidx, g + 1)
                pool.wait_ge(s_out, g + 1)
                pool.sem_inc(s_issue, 1)
                for k in range(TILES):
                    pool.indirect_dma_start(dram["mixed"], bass.IndirectOffsetOnAxis(ap=sidx[:, slot, k:k + 1], axis=0), outrow[:, slot, k, :], None,
                                            bounds_check=N - 1, oob_is_err=False).then_inc(s_scatter[slot], 16)

            skewed(pool, GE, (gather, 0), (scatter, 6))
            for i in range(2):
                pool.wait_ge(s_scatter[i], 64 * (GE // 2))

        @block.scalar
        def _(act):
            def deviation(g, slot, turn):
                act.wait_ge(s_varb, g + 1)
                act.activation(aggs[0:BD, slot, 1, :], msq[:, slot, :], ACT.Sqrt).then_inc(s_std, 1)

            def columns(g, slot, turn):
                if after(g, 2):
                    act.wait_ge(s_mix, g - 1)
                for i in range(2):
                    act.wait_ge(s_turn, 2 * g + i + 1)
                    act.activation(hT[:, slot, i, :], p_turn[:, :], ACT.Relu).then_inc(s_hT, 1)

            def roots(g, slot, turn):
                act.wait_ge(s_var, g + 1)
                act.activation(root[:, slot, :], var[:, slot, :], ACT.Sqrt, bias=keep["eps"][:, :]).then_inc(s_root, 1)

            def widen(g, slot, turn):
                if after(g, 2):
                    act.wait_ge(s_scales, g - 1)
                act.wait_ge(s_dinv[slot], 64 * (turn + 1))
                act.activation(wide[:, slot, :, BD:P], scale[:, slot, :].rearrange("p (j o) -> p j o", o=1).to_broadcast([P, TILES, P - BD]),
                               ACT.Copy).then_inc(s_wide, 1)

            def twins(g, slot, turn):
                act.wait_ge(s_bases, g + 1)
                if after(g, 2):
                    act.wait_ge(s_scan, 2 * (g - 1))
                act.activation(twin[:, slot, :], p_twin[:, :], ACT.Copy)
                act.activation(square[:, slot, :], p_twin[0:BD, :], ACT.Square).then_inc(s_twin, 1)
                act.wait_ge(s_same[slot], 16 * (turn + 1))
                act.activation(barrier[BD:P, slot, :], same[BD:P, slot, :], ACT.Copy, scale=HUGE, bias=-HUGE).then_inc(s_barrier, 1)

            def mean_squares(g, slot, turn):
                act.wait_ge(s_mean, g + 1)
                if after(g, 1):
                    act.wait_ge(s_less, g)
                act.activation(mean_sq[:, :], aggs[0:BD, slot, 0, :], ACT.Square).then_inc(s_meansq, 1)

            def normalise(g, slot, turn):
                act.wait_ge(s_shift, g + 1)
                if after(g, 2):
                    act.wait_ge(s_turn, 2 * (g - 1))
                for k in range(K):
                    last = act.activation(normed[:, slot, k, :], rows[:, slot, k, :], ACT.Identity,
                                          scale=rstd[:, slot, k:k + 1], bias=shift[:, slot, k:k + 1])
                last.then_inc(s_norm, 1)

            def exponent(g, slot, turn):
                act.wait_ge(s_sub, g + 1)
                act.activation(fold(mix[:, slot, :, :]), fold(mix[:, slot, :, :]), ACT.Exp).then_inc(s_exp, 1)

            act.wait_ge(s_ready, 1)
            skewed(act, GE, (deviation, 4), (columns, 2), (roots, 1), (widen, 1), (twins, 2), (mean_squares, 3), (normalise, 1),
                   (exponent, 3))

        @block.vector
        def _(v):
            v.memset(ones[:, :], 1.0)
            v.memset(wide[:, 0, :, 0:BD], 1.0)
            v.memset(wide[:, 1, :, 0:BD], 1.0)
            v.wait_ge(s_weights, 64)
            prep = Chain(v, s_prep, 0)
            prep.start(0)
            order_mix(v, prep, w_mix, w_raw, b_mix, b_raw)
            bf16_parts(prep, v, [b_parts[:, i, 0, :] for i in range(3)], b_mix[:, :], b_rest[:, :])
            for j in range(1, TILES):
                last = v.tensor_copy(b_parts[:, :, j, :], b_parts[:, :, 0, :])
            last.then_inc(s_ready, 1)
            moment, scan = Chain(v, s_moment, 3), Chain(v, s_scan, 2)

            def row_moments(g, slot, turn):
                moment.start(g)
                v.wait_ge(s_rows[slot], 128 * (turn + 1))
                if after(g, 2):
                    v.wait_ge(s_shift, g - 1)
                moments(v, moment, rows[:, slot], stats, tmp, lessmean[:, slot, :], var[:, slot, :], less=True).then_inc(s_var, 1)

            def scales(g, slot, turn):
                v.wait_ge(s_root, g + 1)
                if after(g, 2):
                    v.wait_ge(s_norm, g - 1)
                v.reciprocal(rstd[:, slot, :], root[:, slot, :]).then_inc(s_rstd, 1)
                v.wait_ge(s_rstd, g + 1)
                v.tensor_tensor(shift[:, slot, :], lessmean[:, slot, :], rstd[:, slot, :], ALU.mult).then_inc(s_shift, 1)

            def soften(g, slot, turn):
                v.wait_ge(s_mix, g + 1)
                v.tensor_reduce(top[:, :], p_mix[:, :, :].rearrange("p j (h k) -> p (j h) k", k=MIX), AX_X, ALU.max).then_inc(s_top, 1)
                v.wait_ge(s_top, g + 1)
                if after(g, 2):
                    v.wait_ge(s_prod, 4 * (g - 1))
                v.tensor_tensor(mix[:, slot, :, :].rearrange("p j (h k) -> p (j h) k", k=MIX),
                                p_mix[:, :, :].rearrange("p j (h k) -> p (j h) k", k=MIX), spread(top[:, :], MIX), ALU.subtract).then_inc(s_sub, 1)

            def scans(g, slot, turn):
                first = isinstance(g, int) and g == 0

                def carry(tile):
                    return 0.0 if first else tile[:, GROUP - 1:GROUP]

                scan.start(g)
                v.wait_ge(s_same[slot], 16 * (turn + 1))
                v.wait_ge(s_twin, g + 1)
                v.wait_ge(s_scales, g + 1)
                scan(v.tensor_tensor(value[:, :], p_wide[:, :], twin[:, slot, :], ALU.mult))
                v.tensor_tensor_scan(total[:, slot, :], same[:, slot, :], value[:, :], carry(total[:, 1 - slot, :]), ALU.mult, ALU.add)
                v.tensor_tensor_scan(total_sq[:, slot, :], same[0:BD, slot, :], square[:, slot, :],
                                     carry(total_sq[:, 1 - slot, :]), ALU.mult, ALU.add)
                v.wait_ge(s_barrier, g + 1)
                if after(g, 2):
                    v.wait_ge(s_aggs, g - 1)
                scan(v.tensor_tensor_scan(aggs[BD:P, slot, 1, :], barrier[BD:P, slot, :], twin[BD:P, slot, :],
                                          carry(aggs[BD:P, 1 - slot, 1, :]), ALU.add, ALU.max))
                v.wait_ge(s_factor[slot], 32 * (turn + 1))
                v.tensor_tensor(msq[:, slot, :], total_sq[:, slot, :], factor[0:BD, slot, :], ALU.mult)
                v.tensor_tensor(aggs[:, slot, 0, :], total[:, slot, :], factor[:, slot, :], ALU.mult).then_inc(s_mean, 1)

            def variances(g, slot, turn):
                v.wait_ge(s_meansq, g + 1)
                v.tensor_tensor(msq[:, slot, :], msq[:, slot, :], mean_sq[:, :], ALU.subtract).then_inc(s_less, 1)
                v.wait_ge(s_less, g + 1)
                v.tensor_scalar(msq[:, slot, :], msq[:, slot, :], 0.0, EPS, ALU.max, ALU.add).then_inc(s_varb, 1)

            def products(g, slot, turn):
                v.wait_ge(s_exp, g + 1)
                v.tensor_reduce(mixsum[:, :], mix[:, slot, :, :].rearrange("p j (h k) -> p (j h) k", k=MIX), AX_X, ALU.add).then_inc(s_mixsum, 1)
                v.wait_ge(s_aggs, g + 1)
                for j in range(TILES):
                    if after(g, 1):
                        v.wait_ge(s_reduced, 4 * g - 3 + j)
                    v.tensor_tensor(prod[:, j, :, :].rearrange("p k (h d) -> p k h d", h=HEADS0),
                                    mix[:, slot, j, :].rearrange("p (h k o) -> p k h o", k=MIX, o=1).to_broadcast([P, MIX, HEADS0, D0]),
                                    p_aggs[:, j, :].rearrange("p (k o d) -> p k o d", k=MIX, o=1).to_broadcast([P, MIX, HEADS0, D0]),
                                    ALU.mult).then_inc(s_prod, 1)
                v.wait_ge(s_mixsum, g + 1)
                if after(g, 2):
                    v.wait_ge(s_out, g - 1)
                v.reciprocal(inverse[:, slot, :], mixsum[:, :]).then_inc(s_inverse, 1)

            def finish(g, slot, turn):
                v.wait_ge(s_inverse, g + 1)
                v.wait_ge(s_reduced, TILES * (g + 1))
                if after(g, 2):
                    v.wait_ge(s_scatter[slot], 64 * turn)
                v.tensor_tensor(outrow[:, slot, :, :].rearrange("p j (h d) -> p (j h) d", h=HEADS0),
                                p_out[slot][:, :, :].rearrange("p j (h d) -> p (j h) d", h=HEADS0),
                                spread(inverse[:, slot, :], D0), ALU.mult).then_inc(s_out, 1)

            skewed(v, GE, (row_moments, 1), (scans, 3), (scales, 1), (products, 4), (variances, 3), (soften, 2), (finish, 5))

        @block.tensor
        def _(pe):
            ident = keep["ident"]
            pe.wait_ge(s_ready, 1)

            def turns(g, slot, i):
                for k in range(TILES):
                    last = pe.transpose(p_turn[:, k * P:(k + 1) * P], normed[:, slot, i * TILES + k, :], ident[:, :])
                last.then_inc(s_turn, 1)

            def turn_sources(g, slot, turn):
                pe.wait_ge(s_norm, g + 1)
                if after(g, 1):
                    pe.wait_ge(s_hT, 2 * g)
                turns(g, slot, 0)

            def turn_destinations(g, slot, turn):
                pe.wait_ge(s_hT, 2 * g + 1)
                turns(g, slot, 1)

            def turn_back(g, slot, turn):
                pe.wait_ge(s_std, g + 1)
                pe.wait_ge(s_mean, g + 1)
                if after(g, 1):
                    pe.wait_ge(s_prod, 4 * g)
                for j in range(TILES):
                    for i in range(2):
                        last = pe.transpose(p_aggs[:, j, i * P:(i + 1) * P], aggs[:, slot, i, j * P:(j + 1) * P], ident[:, :])
                last.then_inc(s_aggs, 1)

            def project(g, slot, turn):
                if after(g, 1):
                    pe.wait_ge(s_twin, g)
                pe.matmul(p_twin[:, :], w_bases[:, :], hT[:, slot, 0, :], start=True, stop=True).then_inc(s_bases, 1)
                if after(g, 1):
                    pe.wait_ge(s_sub, g)
                for i in range(3):
                    pe.matmul(fold(p_mix[:, :, :]), ones[:, :], fold(b_parts[:, i, :, :]), start=(i == 0), stop=False)
                pe.wait_ge(s_hT, 2 * g + 2)
                for j in range(TILES):
                    last = pe.matmul(p_mix[:, j, :], hT[:, slot, 1, j * P:(j + 1) * P], w_mix[:, :], start=False, stop=(j == TILES - 1))
                last.then_inc(s_mix, 1)
                pe.wait_ge(s_wide, g + 1)
                if after(g, 1):
                    pe.wait_ge(s_scan, 2 * g - 1)
                for j in range(TILES):
                    last = pe.transpose(p_wide[:, j * P:(j + 1) * P], wide[:, slot, j, :], ident[:, :])
                last.then_inc(s_scales, 1)

            def reduce(g, slot, tiles):
                for j in tiles:
                    pe.wait_ge(s_prod, TILES * g + j + 1)
                    for k in range(MIX):
                        last = pe.matmul(p_out[slot][:, j, :], ident[:, :], prod[:, j, k, :], start=(k == 0), stop=(k == MIX - 1))
                    last.then_inc(s_reduced, 1)

            def reduce_first(g, slot, turn):
                if after(g, 2):
                    pe.wait_ge(s_out, g - 1)
                reduce(g, slot, (0, 1))

            def reduce_last(g, slot, turn):
                reduce(g, slot, (2, 3))

            skewed(pe, GE, (turn_sources, 2), (turn_back, 4), (turn_destinations, 2), (project, 2), (reduce_last, 5), (reduce_first, 4))


def order_mix(v, chain, w_mix, w_raw, b_mix, b_raw):
    for i, a in enumerate(AGG_ORDER):
        for target, source in ((w_mix, w_raw), (b_mix, b_raw)):
            last = v.tensor_copy(target[:, :].rearrange("c (h q b) -> c h q b", h=HEADS0, q=AGGS)[:, :, i, :],
                                 source[:, :].rearrange("c (h b q) -> c h b q", h=HEADS0, q=AGGS)[:, :, :, a])
    chain(last)


def node_rows(table, N, g):
    if not isinstance(g, int):
        return table[bass.ds(g * GROUP, GROUP), :].rearrange("(p j) c -> p j c", j=TILES), P
    n = min(GROUP, N - g * GROUP) // TILES
    return table[g * GROUP:g * GROUP + n * TILES, :].rearrange("(p j) c -> p j c", j=TILES), n


def nodes0(nc, shape, keep, dram, x, bases_W, comb_W, comb_b, bias):
    N, E, GE, GN = shape
    JH = TILES * HEADS0
    with ExitStack() as ctx:
        m = Scope(nc, ctx, "n0")
        w_bases = m.sb("w_bases", [C, BD])
        w_raw = m.sb("w_raw", [C, HEADS0 * MIX])
        w_mix = m.sb("w_mix", [C, HEADS0 * MIX])
        b_raw = m.sb("b_raw", [1, HEADS0 * MIX])
        b_mix = m.sb("b_mix", [1, HEADS0 * MIX])
        b_rest = m.sb("b_rest", [1, HEADS0 * MIX])
        b_parts = m.sb("b_parts", [1, 3, TILES, HEADS0 * MIX], BF16)
        b_out = m.sb("b_out", [P, C])
        ones = m.sb("ones", [1, P], BF16)
        half = m.sb("half", [P, TILES])
        rows = m.sb("rows", [P, 4, TILES, C])
        mixed = m.sb("mixed", [P, 4, TILES, C])
        stats = m.sb("stats", [P, TILES, 6])
        tmp = m.sb("tmp", [P, 4, TILES])
        lessmean, var, spreads = (m.sb(n, [P, 2, TILES]) for n in ("lessmean", "var", "spreads"))
        scale, shift = (m.sb(n, [P, 2, TILES]) for n in ("scale", "shift"))
        normed = m.sb("normed", [P, 2, TILES, C])
        hT = m.sb("hT", [P, 2, GROUP])
        bases = m.sb("bases", [P, 4, TILES, BD])
        top = m.sb("top", [P, JH])
        mix = m.sb("mix", [P, 2, TILES, HEADS0 * MIX])
        mixsum = m.sb("mixsum", [P, JH])
        inverse = m.sb("inverse", [P, JH])
        lone = m.sb("lone", [P, 3, JH])
        selfs = m.sb("selfs", [P, 2, JH])
        lones = m.sb("lones", [P, 2, JH])
        prod = m.sb("prod", [P, 2, BASES, TILES, C])
        residual = m.sb("residual", [P, 2, TILES, C])
        part = m.sb("part", [P, TILES, C])
        x1 = m.sb("x1", [P, 2, TILES, C])
        p_turn = m.ps("turn", [P, GROUP])
        p_mix = [m.ps(f"mix{i}", [P, TILES, HEADS0 * MIX]) for i in range(2)]
        p_bases = m.ps("bases", [P, TILES, BD])
        p_out = [m.ps(f"out{i}", [P, TILES, C]) for i in range(2)]
        s_weights, s_ready, s_consts, s_prep = m.sem("weights"), m.sem("ready"), m.sem("consts"), m.sem("prep")
        s_rows = [m.sem(f"rows{i}") for i in range(4)]
        s_mixed = [m.sem(f"mixed{i}") for i in range(4)]
        s_store = [m.sem(f"store{i}") for i in range(2)]
        s_moment, s_var, s_scale, s_shift, s_norm = (m.sem(n) for n in ("moment", "var", "scale", "shift", "norm"))
        s_turn, s_hT, s_mix, s_bases, s_top, s_sub, s_exp = (m.sem(n) for n in ("turn", "hT", "mix", "bases", "top", "sub", "exp"))
        s_small, s_selfs, s_prod, s_prod_last, s_reduced = (m.sem(n) for n in ("small", "selfs", "prod", "prod_last", "reduced"))
        s_part, s_x1, s_added, s_residual = (m.sem(n) for n in ("part", "x1", "added", "residual"))
        s_go = m.sem("go")
        block = m.block()

        def products_of(eng, j, slot, two):
            return eng.tensor_tensor(prod[:, two, :, j, :].rearrange("p b (h d) -> p b h d", h=HEADS0),
                                     mix[:, two, j, :].rearrange("p (h q b o) -> p q b h o", q=AGGS, b=BASES, o=1)[:, 1].to_broadcast([P, BASES, HEADS0, D0]),
                                     bases[:, slot, j, :].rearrange("p (b o d) -> p b o d", b=BASES, o=1).to_broadcast([P, BASES, HEADS0, D0]),
                                     ALU.mult)

        @block.sync
        def _(sp):
            sp.dma_start(w_bases[:, :].rearrange("c (b d) -> c b d", b=BASES), bases_W.rearrange("b c d -> c b d")).then_inc(s_weights, 16)
            sp.dma_start(w_raw[:, :], comb_W).then_inc(s_weights, 16)
            sp.dma_start(b_raw[:, :], comb_b.rearrange("(o n) -> o n", o=1)).then_inc(s_weights, 16)
            sp.dma_start(b_out[:, :], row_of(bias)).then_inc(s_weights, 16)

            def load(g, slot, turn):
                if after(g, 4):
                    sp.wait_ge(s_norm, g - 3)
                    sp.sem_inc(s_go, 1)
                    sp.wait_ge(s_added, 3 * (g - 3))
                    sp.sem_inc(s_go, 1)
                source, n = node_rows(x, N, g)
                sp.dma_start(rows[0:n, slot, :, :], source).then_inc(s_rows[slot], 16)
                source, n = node_rows(dram["mixed"], GN * GROUP, g)
                sp.dma_start(mixed[:, slot, :, :], source).then_inc(s_mixed[slot], 16)

            def store(g, slot, turn):
                sp.wait_ge(s_x1, g + 1)
                sp.sem_inc(s_go, 1)
                sp.dma_start(node_rows(dram["x1"], GN * GROUP, g)[0], x1[:, slot % 2, :, :]).then_inc(s_store[slot % 2], 16)

            skewed(sp, GN, (load, 0), (store, 5), peel=2, width=4)
            for i in range(2):
                sp.wait_ge(s_store[i], 16 * (GN // 2))

        @block.gpsimd
        def _(pool):
            pool.memset(half[:, :], -0.5).then_inc(s_consts, 1)
            pool.wait_ge(s_consts, 1)
            pool.wait_ge(s_weights, 64)

            def scales(g, slot, turn):
                slot %= 2
                pool.wait_ge(s_var, g + 1)
                if after(g, 2):
                    pool.wait_ge(s_norm, g - 1)
                pool.tensor_tensor(scale[:, slot, :], spreads[:, slot, :], half[:, :], ALU.pow).then_inc(s_scale, 1)
                pool.wait_ge(s_scale, g + 1)
                pool.tensor_tensor(shift[:, slot, :], lessmean[:, slot, :], scale[:, slot, :], ALU.mult).then_inc(s_shift, 1)

            def last_products(g, slot, turn):
                pool.wait_ge(s_exp, g + 1)
                pool.wait_ge(s_bases, g + 1)
                if after(g, 2):
                    pool.wait_ge(s_reduced, g - 1)
                products_of(pool, TILES - 1, slot, slot % 2).then_inc(s_prod_last, 1)

            def add(g, slot, turn):
                two = slot % 2
                if after(g, 2):
                    pool.wait_ge(s_x1, g - 1)
                pool.wait_ge(s_mixed[slot], 16 * (turn + 1))
                pool.wait_ge(s_rows[slot], 16 * (turn + 1))
                pool.tensor_tensor(residual[:, two, :, :], rows[:, slot, :, :], mixed[:, slot, :, :], ALU.add).then_inc(s_added, 1)
                pool.wait_ge(s_added, 3 * g + 1)
                pool.tensor_tensor(residual[:, two, :, :], residual[:, two, :, :], over(b_out[:, :], TILES), ALU.add).then_inc(s_added, 1)
                pool.wait_ge(s_added, 3 * g + 2)
                pool.wait_ge(s_selfs, g + 1)
                pool.tensor_tensor(residual[:, two, :, :].rearrange("p j (h d) -> p (j h) d", h=HEADS0),
                                   residual[:, two, :, :].rearrange("p j (h d) -> p (j h) d", h=HEADS0), spread(lones[:, two, :], D0), ALU.add).then_inc(s_added, 1)

            skewed(pool, GN, (last_products, 2), (scales, 0), (add, 2), width=4)

        @block.scalar
        def _(act):
            def normalise(g, slot, turn):
                two = slot % 2
                act.wait_ge(s_shift, g + 1)
                if after(g, 2):
                    act.wait_ge(s_turn, g - 1)
                for k in range(TILES):
                    last = act.activation(normed[:, two, k, :], rows[:, slot, k, :], ACT.Identity,
                                          scale=scale[:, two, k:k + 1], bias=shift[:, two, k:k + 1])
                last.then_inc(s_norm, 1)

            def exponent(g, slot, turn):
                act.wait_ge(s_sub, g + 1)
                act.activation(fold(mix[:, slot % 2, :, :]), fold(mix[:, slot % 2, :, :]), ACT.Exp).then_inc(s_exp, 1)

            def columns(g, slot, turn):
                if after(g, 2):
                    act.wait_ge(s_mix, g - 1)
                act.wait_ge(s_turn, g + 1)
                act.activation(hT[:, slot % 2, :], p_turn[:, :], ACT.Relu).then_inc(s_hT, 1)

            def copy_bases(g, slot, turn):
                act.wait_ge(s_mix, g + 1)
                if after(g, 4):
                    act.wait_ge(s_prod, g - 3)
                    act.wait_ge(s_prod_last, g - 3)
                act.activation(bases[:, slot, :, :], p_bases[:, :, :], ACT.Copy).then_inc(s_bases, 1)

            skewed(act, GN, (normalise, 0), (exponent, 1), (columns, 0), (copy_bases, 0), width=4)

        @block.vector
        def _(v):
            v.memset(ones[:, :], 1.0)
            v.wait_ge(s_weights, 64)
            prep = Chain(v, s_prep, 0)
            prep.start(0)
            order_mix(v, prep, w_mix, w_raw, b_mix, b_raw)
            bf16_parts(prep, v, [b_parts[:, i, 0, :] for i in range(3)], b_mix[:, :], b_rest[:, :])
            for j in range(1, TILES):
                last = v.tensor_copy(b_parts[:, :, j, :], b_parts[:, :, 0, :])
            last.then_inc(s_ready, 1)
            moment, small = Chain(v, s_moment, 4), Chain(v, s_small, 3)

            def row_moments(g, slot, turn):
                two = slot % 2
                moment.start(g)
                v.wait_ge(s_rows[slot], 16 * (turn + 1))
                if after(g, 2):
                    v.wait_ge(s_shift, g - 1)
                moment(moments(v, moment, rows[:, slot], stats, tmp, lessmean[:, two, :], var[:, two, :], less=True))
                v.tensor_scalar(spreads[:, two, :], var[:, two, :], EPS, None, ALU.add).then_inc(s_var, 1)

            def soften(g, slot, turn):
                two = slot % 2
                v.wait_ge(s_mix, g + 1)
                v.tensor_reduce(top[:, :], p_mix[two][:, :, :].rearrange("p j (h k) -> p (j h) k", k=MIX), AX_X, ALU.max).then_inc(s_top, 1)
                v.wait_ge(s_top, g + 1)
                v.tensor_tensor(mix[:, two, :, :].rearrange("p j (h k) -> p (j h) k", k=MIX),
                                p_mix[two][:, :, :].rearrange("p j (h k) -> p (j h) k", k=MIX), spread(top[:, :], MIX), ALU.subtract).then_inc(s_sub, 1)

            def products(g, slot, turn):
                two = slot % 2
                small.start(g)
                v.wait_ge(s_exp, g + 1)
                v.wait_ge(s_bases, g + 1)
                if after(g, 2):
                    v.wait_ge(s_reduced, g - 1)
                    v.wait_ge(s_added, 3 * (g - 1))
                    v.wait_ge(s_part, g - 1)
                v.tensor_reduce(mixsum[:, :], mix[:, two, :, :].rearrange("p j (h k) -> p (j h) k", k=MIX), AX_X, ALU.add)
                last = v.tensor_reduce(lone[:, 0, :], mix[:, two, :, :].rearrange("p j (h q b) -> p (j h) q b", q=AGGS, b=BASES)[:, :, 2, :],
                                       AX_X, ALU.add)
                last.then_inc(s_small, 1)
                products_of(v, 0, slot, two)
                v.wait_ge(s_small, 3 * g + 1)
                v.reciprocal(inverse[:, :], mixsum[:, :])
                v.tensor_tensor(lone[:, 1, :].rearrange("p (j h) -> p j h", j=TILES), lone[:, 0, :].rearrange("p (j h) -> p j h", j=TILES),
                                keep["lonew"][:, :, bass.ds(g, 1)].to_broadcast([P, TILES, HEADS0]), ALU.mult).then_inc(s_small, 1)
                products_of(v, 1, slot, two)
                v.wait_ge(s_small, 3 * g + 2)
                v.tensor_tensor(selfs[:, two, :].rearrange("p (j h) -> p j h", j=TILES), inverse[:, :].rearrange("p (j h) -> p j h", j=TILES),
                                keep["selfw"][:, :, bass.ds(g, 1)].to_broadcast([P, TILES, HEADS0]), ALU.mult).then_inc(s_small, 1)
                v.tensor_tensor(lones[:, two, :], lone[:, 1, :], inverse[:, :], ALU.mult).then_inc(s_selfs, 1)
                products_of(v, 2, slot, two).then_inc(s_prod, 1)

            def finish(g, slot, turn):
                slot %= 2
                v.wait_ge(s_reduced, g + 1)
                v.wait_ge(s_small, 3 * g + 3)
                if after(g, 1):
                    v.wait_ge(s_x1, g)
                v.tensor_tensor(part[:, :, :].rearrange("p j (h d) -> p (j h) d", h=HEADS0),
                                p_out[slot][:, :, :].rearrange("p j (h d) -> p (j h) d", h=HEADS0), spread(selfs[:, slot, :], D0), ALU.mult).then_inc(s_part, 1)
                v.wait_ge(s_part, g + 1)
                v.wait_ge(s_added, 3 * (g + 1))
                if after(g, 2):
                    v.wait_ge(s_store[slot], 8 * (g - slot))
                v.tensor_tensor(x1[:, slot, :, :], part[:, :, :], residual[:, slot, :, :], ALU.add).then_inc(s_x1, 1)

            skewed(v, GN, (row_moments, 0), (soften, 1), (products, 2), (finish, 3), width=4)

        @block.tensor
        def _(pe):
            ident = keep["ident"]
            pe.wait_ge(s_ready, 1)

            def turns(g, slot, turn):
                pe.wait_ge(s_norm, g + 1)
                if after(g, 1):
                    pe.wait_ge(s_hT, g)
                for k in range(TILES):
                    last = pe.transpose(p_turn[:, k * P:(k + 1) * P], normed[:, slot % 2, k, :], ident[:, :])
                last.then_inc(s_turn, 1)

            def project(g, slot, turn):
                two = slot % 2
                if after(g, 2):
                    pe.wait_ge(s_sub, g - 1)
                for i in range(3):
                    pe.matmul(fold(p_mix[two][:, :, :]), ones[:, :], fold(b_parts[:, i, :, :]), start=(i == 0), stop=False)
                if after(g, 1):
                    pe.wait_ge(s_bases, g)
                pe.wait_ge(s_hT, g + 1)
                for j in range(TILES):
                    pe.matmul(p_mix[two][:, j, :], hT[:, two, j * P:(j + 1) * P], w_mix[:, :], start=False, stop=(j == TILES - 1))
                    last = pe.matmul(p_bases[:, j, :], hT[:, two, j * P:(j + 1) * P], w_bases[:, :], start=True, stop=True)
                last.then_inc(s_mix, 1)

            def reduce(g, slot, turn):
                two = slot % 2
                pe.wait_ge(s_prod, g + 1)
                pe.wait_ge(s_prod_last, g + 1)
                if after(g, 2):
                    pe.wait_ge(s_part, g - 1)
                for b in range(BASES):
                    last = pe.matmul(fold(p_out[two][:, :, :]), ident[:, :], fold(prod[:, two, b, :, :]), start=(b == 0), stop=(b == BASES - 1))
                last.then_inc(s_reduced, 1)

            skewed(pe, GN, (reduce, 3), (turns, 0), (project, 0), width=4)


def edges1(nc, shape, keep, dram, edge_attr, ln_g, ln_b, wts, biases, We):
    N, E, GE, GN = shape
    K = 2 * TILES
    names = ("k", "v", "q")
    with ExitStack() as ctx:
        m = Scope(nc, ctx, "e1")
        raw = m.sb("raw", [C, 3, C])
        weight = m.sb("weight", [C, 3, C])
        bias_raw = m.sb("bias_raw", [C, 3])
        bias = m.sb("bias", [C, 3])
        norm = m.sb("norm", [C, 2])
        w_edge = m.sb("w_edge", [TILES * EDGE_C, TILES, C])
        heads = m.sb("heads", [C, C])
        gidx = m.sb("gidx", [P, 2, K], I32)
        sidx = m.sb("sidx", [P, 2, TILES], I32)
        rows = m.sb("rows", [P, 2, K, C])
        attr = m.sb("attr", [P, 2, TILES, EDGE_C])
        same = m.sb("same", [P, 2, GROUP])
        barrier = m.sb("barrier", [P, 2, GROUP])
        stats = m.sb("stats", [P, K, 6])
        tmp = m.sb("tmp", [P, 4, K])
        mean = m.sb("mean", [P, K])
        var = m.sb("var", [P, K])
        floor = m.sb("floor", [P, K])
        stats2 = m.sb("stats2", [P, K, 6])
        tmp2 = m.sb("tmp2", [P, 4, K])
        var2 = m.sb("var2", [P, K])
        half = m.sb("half", [P, K])
        lessmean2, spreads, factor, shift = (m.sb(n, [P, 2, K]) for n in ("lessmean2", "spreads", "factor", "shift"))
        rectified = m.sb("rectified", [P, 2, K, C])
        normed = m.sb("normed", [P, 2, K, C])
        xT = m.sb("xT", [P, 2, 2, GROUP])
        attrT = m.sb("attrT", [TILES * EDGE_C, 2, P])
        qT = m.sb("qT", [P, 2, GROUP])
        vT = m.sb("vT", [P, 4, GROUP])
        qk = m.sb("qk", [P, 2, GROUP])
        top = m.sb("top", [P, 2, 1 + GROUP])
        fade = m.sb("fade", [P, GROUP])
        fade2 = m.sb("fade2", [P, 2, GROUP])
        prob = m.sb("prob", [P, 2, GROUP])
        pv = m.sb("pv", [P, GROUP])
        denom = m.sb("denom", [P, 2, GROUP])
        numer = m.sb("numer", [P, 2, GROUP])
        inverse = m.sb("inverse", [P, TILES * HEADS1])
        outrow = m.sb("outrow", [P, 2, TILES, C])
        p_turn = m.ps("turn", [P, 2, GROUP])
        p_k, p_v, p_q = (m.ps(n, [P, GROUP]) for n in names)
        p_score = m.ps("score", [P, GROUP])
        p_numer = m.ps("numer", [P, TILES, C])
        p_denom = m.ps("denom", [P, TILES, C])
        s_weights, s_ready, s_zero = m.sem("weights"), m.sem("ready"), m.sem("zero")
        s_bias, s_const = m.sem("bias"), m.sem("const")
        s_gidx, s_sidx, s_issue = m.sem("gidx"), m.sem("sidx"), m.sem("issue")
        s_rows = [m.sem(f"rows{i}") for i in range(2)]
        s_attr = [m.sem(f"attr{i}") for i in range(2)]
        s_same = [m.sem(f"same{i}") for i in range(2)]
        s_scatter = [m.sem(f"scatter{i}") for i in range(2)]
        s_moment, s_var, s_factor, s_shift, s_norm = (m.sem(n) for n in ("moment", "var", "factor", "shift", "norm"))
        s_turn, s_attrT, s_xT, s_k, s_qv, s_vq, s_qk, s_score = (m.sem(n) for n in ("turn", "attrT", "xT", "k", "qv", "vq", "qk", "score"))
        s_attrp, s_barrier, s_top, s_fade, s_prob, s_faded = (m.sem(n) for n in ("attrp", "barrier", "top", "fade", "prob", "faded"))
        s_pv, s_scan, s_back, s_inv, s_out = (m.sem(n) for n in ("pv", "scan", "back", "inv", "out"))
        s_den, s_tail, s_half = m.sem("den"), m.sem("tail"), m.sem("half")
        full = E // GROUP
        n_load = 3 + 3 + 2 + TILES
        tail_dmas = sum(1 for j in range(TILES) if E - full * GROUP - j * P > 0)
        s_go = m.sem("go")
        block = m.block()

        @block.sync
        def _(sp):
            for i, n in enumerate(names):
                sp.dma_start(raw[:, i, :], wts[n]).then_inc(s_weights, 16)
                sp.dma_start(bias_raw[:, i:i + 1], biases[n].rearrange("(p o) -> p o", o=1)).then_inc(s_weights, 16)
            sp.dma_start(norm[:, 0:1], ln_g.rearrange("(p o) -> p o", o=1)).then_inc(s_weights, 16)
            sp.dma_start(norm[:, 1:2], ln_b.rearrange("(p o) -> p o", o=1)).then_inc(s_weights, 16)
            sp.wait_ge(s_zero, 1)
            for j in range(TILES):
                sp.dma_start(w_edge[j * EDGE_C:(j + 1) * EDGE_C, j, :], We).then_inc(s_weights, 16)

            def load(g, slot, turn):
                if after(g, 2):
                    sp.wait_ge(s_attrp, g - 1)
                    sp.sem_inc(s_go, 1)
                if not isinstance(g, int) or g < full:
                    sp.dma_start(attr[:, slot, :, :], edge_attr[bass.ds(g * GROUP, GROUP), :].rearrange("(j p) c -> p j c", p=P)).then_inc(s_attr[slot], 16)
                else:
                    for j in range(TILES):
                        n = min(P, max(0, E - g * GROUP - j * P))
                        if n:
                            sp.dma_start(attr[0:n, slot, j, :], edge_attr[g * GROUP + j * P:g * GROUP + j * P + n, :]).then_inc(s_tail, 16)
                if after(g, 2):
                    sp.wait_ge(s_barrier, g - 1)
                    sp.sem_inc(s_go, 1)
                sp.dma_start(same[:, slot, :], dram["same"][bass.ds(g, 1), :].to_broadcast([P, GROUP])).then_inc(s_same[slot], 16)

            skewed(sp, GE, (load, 0), peel=2)

        @block.gpsimd
        def _(pool):
            pool.memset(half[:, :], -0.5).then_inc(s_half, 1)
            pool.wait_ge(s_half, 1)

            def gather(g, slot, turn):
                slot %= 2
                if after(g, 2):
                    pool.wait_ge(s_var, g - 1)
                    pool.sem_inc(s_issue, 1)
                pool.tensor_copy(gidx[:, slot, :].rearrange("p (k o) -> p k o", o=1), index_of(keep, GE, (0, 2), g)).then_inc(s_gidx, 1)
                pool.wait_ge(s_gidx, g + 1)
                pool.sem_inc(s_issue, 1)
                for k in range(K):
                    pool.indirect_dma_start(rows[:, slot, k, :], None, dram["x1"], bass.IndirectOffsetOnAxis(ap=gidx[:, slot, k:k + 1], axis=0)).then_inc(s_rows[slot], 16)

            def scales(g, slot, turn):
                slot %= 2
                pool.wait_ge(s_var, g + 1)
                if after(g, 2):
                    pool.wait_ge(s_norm, g - 1)
                pool.tensor_tensor(factor[:, slot, :], spreads[:, slot, :], half[:, :], ALU.pow).then_inc(s_factor, 1)
                pool.wait_ge(s_factor, g + 1)
                pool.tensor_tensor(shift[:, slot, :], lessmean2[:, slot, :], factor[:, slot, :], ALU.mult).then_inc(s_shift, 1)

            def scatter(g, slot, turn):
                turn, slot = turn * 2 + slot // 2, slot % 2
                if after(g, 2):
                    pool.wait_ge(s_scatter[slot], 64 * turn)
                    pool.sem_inc(s_issue, 1)
                pool.tensor_copy(sidx[:, slot, :].rearrange("p (k o) -> p k o", o=1), index_of(keep, GE, (2, 3), g)).then_inc(s_sidx, 1)
                pool.wait_ge(s_sidx, g + 1)
                pool.wait_ge(s_out, g + 1)
                pool.sem_inc(s_issue, 1)
                for k in range(TILES):
                    pool.indirect_dma_start(dram["attended"], bass.IndirectOffsetOnAxis(ap=sidx[:, slot, k:k + 1], axis=0), outrow[:, slot, k, :], None,
                                            bounds_check=N - 1, oob_is_err=False).then_inc(s_scatter[slot], 16)

            skewed(pool, GE, (gather, 0), (scales, 1), (scatter, 5), width=4)
            for i in range(2):
                pool.wait_ge(s_scatter[i], 64 * (GE // 2))

        @block.scalar
        def _(act):
            def normalise(g, slot, turn):
                slot %= 2
                act.wait_ge(s_shift, g + 1)
                if after(g, 2):
                    act.wait_ge(s_turn, g - 1)
                for k in range(K):
                    last = act.activation(normed[:, slot, k, :], rectified[:, slot, k, :], ACT.Identity,
                                          scale=factor[:, slot, k:k + 1], bias=shift[:, slot, k:k + 1])
                last.then_inc(s_norm, 1)

            def barriers(g, slot, turn):
                turn, slot = turn * 2 + slot // 2, slot % 2
                act.wait_ge(s_same[slot], 16 * (turn + 1))
                if after(g, 2):
                    act.wait_ge(s_fade, 2 * (g - 1))
                act.activation(barrier[:, slot, :], same[:, slot, :], ACT.Copy, scale=HUGE, bias=-HUGE).then_inc(s_barrier, 1)

            def columns(g, slot, turn):
                slot %= 2
                if after(g, 2):
                    act.wait_ge(s_qv, g - 1)
                act.wait_ge(s_attrp, g + 1)
                act.activation(attrT[:, slot, :], p_k[0:TILES * EDGE_C, 0:P], ACT.Copy).then_inc(s_attrT, 1)
                act.wait_ge(s_turn, g + 1)
                act.activation(xT[:, slot, :, :], p_turn[:, :, :], ACT.Copy).then_inc(s_xT, 1)

            def query_value(g, slot, turn):
                if after(g, 2):
                    act.wait_ge(s_qk, g - 1)
                if after(g, 4):
                    act.wait_ge(s_pv, g - 3)
                act.wait_ge(s_qv, g + 1)
                act.activation(qT[:, slot % 2, :], p_q[:, :], ACT.Identity, bias=bias[:, 2:3])
                act.activation(vT[:, slot, :], p_v[:, :], ACT.Identity, bias=bias[:, 1:2]).then_inc(s_vq, 1)

            def exponents(g, slot, turn):
                slot %= 2
                act.wait_ge(s_fade, 2 * g + 2)
                act.activation(prob[:, slot, :], prob[:, slot, :], ACT.Exp).then_inc(s_prob, 1)
                act.activation(fade2[:, slot, :], fade2[:, slot, :], ACT.Exp).then_inc(s_faded, 1)

            act.wait_ge(s_bias, 1)
            skewed(act, GE, (columns, 2), (barriers, 2), (exponents, 3), (query_value, 2), (normalise, 1), width=4)

        @block.vector
        def _(v):
            v.memset(w_edge[:, :, :], 0.0)
            v.memset(attr[:, :, :, :], 0.0).then_inc(s_zero, 1)
            v.memset(heads[:, :], 0.0).then_inc(s_const, 1)
            v.memset(top[:, 0, 0:1], 0.0)
            v.wait_ge(s_const, 1)
            for h in range(HEADS1):
                last = v.memset(heads[h * D1:(h + 1) * D1, h * D1:(h + 1) * D1], float(D1) ** -0.5)
            last.then_inc(s_const, 1)
            v.wait_ge(s_weights, 16 * n_load)
            last = v.tensor_scalar(fold(weight[:, :, :]), fold(raw[:, :, :]), norm[:, 0:1], None, ALU.mult)
            last.then_inc(s_ready, 1)
            v.wait_ge(s_ready, 2)
            v.tensor_tensor(bias[:, :], bias_raw[:, :], p_score[:, 0:3], ALU.add).then_inc(s_bias, 1)
            moment = Chain(v, s_moment, 8)

            def first_norms(g, slot, turn):
                turn, slot = turn * 2 + slot // 2, slot % 2
                moment.start(g)
                v.wait_ge(s_rows[slot], 128 * (turn + 1))
                if after(g, 2):
                    v.wait_ge(s_norm, g - 1)
                moments(v, moment, rows[:, slot], stats, tmp, mean[:, :], var[:, :])
                for k in range(K):
                    last = v.tensor_scalar(rectified[:, slot, k, :], rows[:, slot, k, :], mean[:, k:k + 1], 0.0, ALU.subtract, ALU.max)
                moment(last)
                v.tensor_scalar(floor[:, :], var[:, :], EPS, EPS, ALU.add, ALU.mult)
                moment(moments(v, moment, rectified[:, slot], stats2, tmp2, lessmean2[:, slot, :], var2[:, :], less=True))
                v.tensor_tensor(spreads[:, slot, :], floor[:, :], var2[:, :], ALU.add).then_inc(s_var, 1)

            def score(g, slot, turn):
                slot %= 2
                v.wait_ge(s_k, g + 1)
                v.wait_ge(s_vq, g + 1)
                if after(g, 2):
                    v.wait_ge(s_score, g - 1)
                v.scalar_tensor_tensor(out=qk[:, slot, :], in0=p_k[:, :], scalar=bias[:, 0:1], in1=qT[:, slot, :],
                                       op0=ALU.add, op1=ALU.mult).then_inc(s_qk, 1)

            def running_top(g, slot, turn):
                slot %= 2
                first = isinstance(g, int) and g == 0
                v.wait_ge(s_score, g + 1)
                v.wait_ge(s_barrier, g + 1)
                if not first:
                    v.tensor_copy(top[:, slot, 0:1], top[:, 1 - slot, GROUP:GROUP + 1])
                v.tensor_tensor_scan(top[:, slot, 1:GROUP + 1], barrier[:, slot, :], p_score[:, :],
                                     0.0 if first else top[:, 1 - slot, GROUP:GROUP + 1], ALU.add, ALU.max).then_inc(s_top, 1)
                v.wait_ge(s_top, g + 1)
                v.tensor_tensor(fade[:, :], top[:, slot, 0:GROUP], barrier[:, slot, :], ALU.add).then_inc(s_fade, 1)
                v.tensor_tensor(prob[:, slot, :], p_score[:, :], top[:, slot, 1:GROUP + 1], ALU.subtract)
                v.wait_ge(s_fade, 2 * g + 1)
                v.tensor_tensor(fade2[:, slot, :], fade[:, :], top[:, slot, 1:GROUP + 1], ALU.subtract).then_inc(s_fade, 1)

            def accumulate(g, slot, turn):
                four, slot = slot, slot % 2

                def carry(tile):
                    return 0.0 if isinstance(g, int) and g == 0 else tile[:, 1 - slot, GROUP - 1:GROUP]

                v.wait_ge(s_prob, g + 1)
                v.tensor_tensor(pv[:, :], prob[:, slot, :], vT[:, four, :], ALU.mult).then_inc(s_pv, 1)
                v.wait_ge(s_faded, g + 1)
                v.tensor_tensor_scan(denom[:, slot, :], fade2[:, slot, :], prob[:, slot, :], carry(denom), ALU.mult, ALU.add)
                v.wait_ge(s_pv, g + 1)
                v.tensor_tensor_scan(numer[:, slot, :], fade2[:, slot, :], pv[:, :], carry(numer), ALU.mult, ALU.add).then_inc(s_scan, 1)

            def finish(g, slot, turn):
                turn, slot = turn * 2 + slot // 2, slot % 2
                v.wait_ge(s_back, g + 1)
                v.tensor_scalar(inverse[:, :].rearrange("p (j h) -> p j h", j=TILES), p_denom[:, :, 0:C:D1], 1e-16, None, ALU.add).then_inc(s_den, 1)
                v.wait_ge(s_den, 2 * g + 1)
                v.reciprocal(inverse[:, :], inverse[:, :]).then_inc(s_den, 1)
                v.wait_ge(s_den, 2 * g + 2)
                if after(g, 2):
                    v.wait_ge(s_scatter[slot], 64 * turn)
                v.tensor_tensor(outrow[:, slot, :, :].rearrange("p j (h d) -> p (j h) d", h=HEADS1),
                                p_numer[:, :, :].rearrange("p j (h d) -> p (j h) d", h=HEADS1), spread(inverse[:, :], D1), ALU.mult).then_inc(s_out, 1)

            skewed(v, GE, (first_norms, 1), (running_top, 3), (accumulate, 4), (finish, 5), (score, 2), width=4)

        @block.tensor
        def _(pe):
            ident = keep["ident"]
            pe.wait_ge(s_weights, 16 * n_load)
            for i in range(3):
                last = pe.matmul(p_score[:, i:i + 1], raw[:, i, :], norm[:, 1:2], start=True, stop=True)
            last.then_inc(s_ready, 1)
            pe.wait_ge(s_ready, 2)
            pe.wait_ge(s_const, 2)
            pe.wait_ge(s_bias, 1)

            def scores(g, slot, turn):
                slot %= 2
                pe.wait_ge(s_qk, g + 1)
                if after(g, 1):
                    pe.wait_ge(s_fade, 2 * g)
                pe.matmul(p_score[:, :], heads[:, :], qk[:, slot, :], start=True, stop=True).then_inc(s_score, 1)

            def turn_back(g, slot, turn):
                slot %= 2
                pe.wait_ge(s_scan, g + 1)
                if after(g, 1):
                    pe.wait_ge(s_out, g)
                for j in range(TILES):
                    pe.transpose(p_numer[:, j, :], numer[:, slot, j * P:(j + 1) * P], ident[:, :])
                    last = pe.transpose(p_denom[:, j, :], denom[:, slot, j * P:(j + 1) * P], ident[:, :])
                last.then_inc(s_back, 1)

            def turns(g, slot, turn):
                turn, slot = turn * 2 + slot // 2, slot % 2
                if after(g, 1):
                    pe.wait_ge(s_qk, g)
                if isinstance(g, int) and g == full and tail_dmas:
                    pe.wait_ge(s_tail, 16 * tail_dmas)
                elif not isinstance(g, int) or g < full:
                    pe.wait_ge(s_attr[slot], 16 * (turn + 1))
                pe.transpose(p_k[0:TILES * EDGE_C, 0:P], fold(attr[:, slot, :, :]), ident[:, :]).then_inc(s_attrp, 1)
                pe.wait_ge(s_norm, g + 1)
                if after(g, 1):
                    pe.wait_ge(s_xT, g)
                for k in range(K):
                    last = pe.transpose(p_turn[:, k // TILES, (k % TILES) * P:(k % TILES + 1) * P], normed[:, slot, k, :], ident[:, :])
                last.then_inc(s_turn, 1)

            def project(g, slot, turn):
                slot %= 2
                pe.wait_ge(s_attrT, g + 1)
                pe.wait_ge(s_xT, g + 1)
                if after(g, 1):
                    pe.wait_ge(s_qk, g)
                    pe.wait_ge(s_vq, g)
                for i, bank in enumerate((p_k, p_v)):
                    pe.matmul(bank[:, :], weight[:, i, :], xT[:, slot, 0, :], start=True, stop=False)
                    for j in range(TILES):
                        last = pe.matmul(bank[:, j * P:(j + 1) * P], w_edge[:, j, :], attrT[:, slot, :], start=False, stop=(j == TILES - 1))
                last.then_inc(s_k, 1)
                pe.matmul(p_q[:, :], weight[:, 2, :], xT[:, slot, 1, :], start=True, stop=True).then_inc(s_qv, 1)

            skewed(pe, GE, (scores, 3), (turn_back, 5), (turns, 2), (project, 2), peel=2, width=4)


def nodes1(nc, shape, keep, dram, prm, out):
    N, E, GE, GN = shape
    CH = HID // P
    with ExitStack() as ctx:
        m = Scope(nc, ctx, "n1")
        skip_raw = m.sb("skip_raw", [C, C])
        w_skip = m.sb("w_skip", [C, C + 1])
        skip_row = m.sb("skip_row", [1, C])
        b_skip = m.sb("b_skip", [1, C + 1])
        norm = m.sb("norm", [C, 4])
        beta_rows = m.sb("beta_rows", [P, 3, C])
        beta_out = m.sb("beta_out", [P, C])
        beta_skip = m.sb("beta_skip", [P, C])
        scratch = m.sb("scratch", [P, 2, C])
        w1_raw = m.sb("w1_raw", [C, HID])
        w1 = m.sb("w1", [C, HID])
        b1_raw = m.sb("b1_raw", [P, CH])
        b1 = m.sb("b1", [P, CH])
        w2 = m.sb("w2", [P, CH, C])
        b2_row = m.sb("b2_row", [1, C])
        rest = m.sb("rest", [1, 2, C + 1])
        skip_parts = m.sb("skip_parts", [1, 3, 2, C + 1], BF16)
        b2_parts = m.sb("b2_parts", [1, 3, TILES, C], BF16)
        ones = m.sb("ones", [1, P])
        ones_bf = m.sb("ones_bf", [1, P], BF16)
        half = m.sb("half", [P, 2 * TILES])
        base = m.sb("base", [P, TILES])
        rows = m.sb("rows", [P, 4, TILES, C])
        attended = m.sb("attended", [P, 4, TILES, C])
        stats = [m.sb(f"stats{i}", [P, TILES, 6]) for i in range(3)]
        tmp = [m.sb(f"tmp{i}", [P, 4, TILES]) for i in range(3)]
        mean, var, var2 = (m.sb(n, [P, 2, TILES]) for n in ("mean", "var", "var2"))
        lessmean2, lessmean3, var3 = (m.sb(n, [P, 2, TILES]) for n in ("lessmean2", "lessmean3", "var3"))
        spreads = m.sb("spreads", [P, 2, 2 * TILES])
        scales = m.sb("scales", [P, 2, 2 * TILES])
        shift2, shift3, scale3 = (m.sb(n, [P, 2, TILES]) for n in ("shift2", "shift3", "scale3"))
        rectified = m.sb("rectified", [P, 2, TILES, C])
        normed = m.sb("normed", [P, 2, TILES, C])
        xT = m.sb("xT", [P, 2, GROUP])
        weighed = m.sb("weighed", [P, 2, TILES, C])
        h1 = m.sb("h1", [P, 2, TILES, C])
        logit = m.sb("logit", [P, 2, TILES])
        gate = m.sb("gate", [P, 2, TILES])
        beta = m.sb("beta", [P, TILES])
        differ = m.sb("differ", [P, TILES, C])
        blend = m.sb("blend", [P, TILES, C])
        inner = m.sb("inner", [P, 2, TILES, C])
        residual = m.sb("residual", [P, 2, TILES, C])
        normed3 = m.sb("normed3", [P, 2, TILES, C])
        x3T = m.sb("x3T", [P, 2, GROUP])
        hidden = m.sb("hidden", [P, CH, GROUP])
        result = m.sb("result", [P, 2, TILES, C])
        p_turn = m.ps("turn", [P, GROUP])
        p_skip = m.ps("skip", [P, 2, GROUP])
        p_turn3 = m.ps("turn3", [P, GROUP])
        p_hid = [m.ps(f"hid{i}", [P, GROUP]) for i in range(2)]
        p_y = [m.ps(f"y{i}", [P, TILES, C]) for i in range(2)]
        s_weights, s_consts, s_prep, s_ready = m.sem("weights"), m.sem("consts"), m.sem("prep"), m.sem("ready")
        s_rows = [m.sem(f"rows{i}") for i in range(4)]
        s_att = [m.sem(f"att{i}") for i in range(4)]
        s_store = [m.sem(f"store{i}") for i in range(2)]
        s_moment, s_moment3, s_var, s_scales, s_shift2, s_norm = (m.sem(n) for n in ("moment", "moment3", "var", "scales", "shift2", "norm"))
        s_turn, s_xT, s_skip, s_weighed, s_h1 = (m.sem(n) for n in ("turn", "xT", "skip", "weighed", "h1"))
        s_logit, s_gate, s_beta, s_blend, s_inner = (m.sem(n) for n in ("logit", "gate", "beta", "blend", "inner"))
        s_residual, s_var3, s_scale3, s_shift3, s_norm3 = (m.sem(n) for n in ("residual", "var3", "scale3", "shift3", "norm3"))
        s_turn3, s_x3T, s_up, s_hidden, s_down, s_result = (m.sem(n) for n in ("turn3", "x3T", "up", "hidden", "down", "result"))
        s_chain = m.sem("chain")
        s_go = m.sem("go")
        block = m.block()

        def skip_tiles(part):
            return p_skip[:, :, 0:2 * (C + 1)].rearrange("p b (k c) -> p b k c", k=2)[:, :, :, part]

        def by_bank(tiles):
            return tiles.rearrange("p (b k) c -> p b k c", b=2)

        @block.sync
        def _(sp):
            def column(vec):
                return vec.rearrange("(p o) -> p o", o=1)

            def row(vec):
                return vec.rearrange("(o n) -> o n", o=1)

            for tile, source in (
                (skip_raw[:, :], prm["Wskip"]), (w1_raw[:, :], prm["W1"]),
                (w2[:, :, :], prm["W2"].rearrange("(k p) c -> p k c", p=P)),
                (norm[:, 0:1], column(prm["ln1_g"])), (norm[:, 1:2], column(prm["ln1_b"])),
                (norm[:, 2:3], column(prm["ln2_g"])), (norm[:, 3:4], column(prm["ln2_b"])),
                (skip_row[:, :], row(prm["bskip"])), (b2_row[:, :], row(prm["b2"])),
            ):
                sp.dma_start(tile, source).then_inc(s_weights, 16)
            for k in range(CH):
                sp.dma_start(b1_raw[:, k:k + 1], column(prm["b1"][k * P:(k + 1) * P])).then_inc(s_weights, 16)
            for k in range(3):
                sp.dma_start(beta_rows[:, k, :], row_of(prm["Wbeta"][k * C:(k + 1) * C, :].rearrange("n o -> (n o)"))).then_inc(s_weights, 16)

            def load(g, slot, turn):
                if after(g, 4):
                    sp.wait_ge(s_residual, g - 3)
                    sp.sem_inc(s_go, 1)
                sp.dma_start(rows[:, slot, :, :], node_rows(dram["x1"], GN * GROUP, g)[0]).then_inc(s_rows[slot], 16)
                if after(g, 4):
                    sp.wait_ge(s_blend, 2 * (g - 3))
                    sp.sem_inc(s_go, 1)
                    sp.wait_ge(s_weighed, g - 3)
                    sp.sem_inc(s_go, 1)
                sp.dma_start(attended[:, slot, :, :], node_rows(dram["attended"], GN * GROUP, g)[0]).then_inc(s_att[slot], 16)

            def store(g, slot, turn):
                sp.wait_ge(s_result, g + 1)
                sp.sem_inc(s_go, 1)
                target, n = node_rows(out, N, g)
                sp.dma_start(target, result[0:n, slot % 2, :, :]).then_inc(s_store[slot % 2], 16)

            skewed(sp, GN, (load, 0), (store, 5), peel=2, width=4)
            for i in range(2):
                sp.wait_ge(s_store[i], 16 * (GN // 2))

        @block.gpsimd
        def _(pool):
            pool.memset(half[:, :], -0.5)
            pool.memset(base[:, :], INV_E).then_inc(s_consts, 1)
            pool.wait_ge(s_consts, 2)
            pool.wait_ge(s_ready, 1)

            def scale(g, slot, turn):
                slot %= 2
                pool.wait_ge(s_var, g + 1)
                if after(g, 2):
                    pool.wait_ge(s_norm, g - 1)
                pool.tensor_tensor(scales[:, slot, :], spreads[:, slot, :], half[:, :], ALU.pow).then_inc(s_scales, 1)
                pool.wait_ge(s_scales, g + 1)
                pool.tensor_tensor(shift2[:, slot, :], lessmean2[:, slot, :], scales[:, slot, TILES:2 * TILES], ALU.mult).then_inc(s_shift2, 1)

            def gates(g, slot, turn):
                slot %= 2
                pool.wait_ge(s_logit, 2 * g + 2)
                pool.tensor_tensor(gate[:, slot, :], base[:, :], logit[:, slot, :], ALU.pow).then_inc(s_gate, 1)

            def weigh(g, slot, turn):
                pool.wait_ge(s_att[slot], 16 * (turn + 1))
                if after(g, 2):
                    pool.wait_ge(s_logit, 2 * (g - 1))
                pool.tensor_tensor(weighed[:, slot % 2, :, :], attended[:, slot, :, :], over(beta_out[:, :], TILES), ALU.mult).then_inc(s_weighed, 1)

            def first_norm(g, slot, turn):
                slot %= 2
                if after(g, 2):
                    pool.wait_ge(s_inner, g - 1)
                pool.tensor_tensor(h1[:, slot, :, :], rectified[:, slot, :, :], spread(scales[:, slot, 0:TILES], C), ALU.mult).then_inc(s_h1, 1)

            def scale_inner(g, slot, turn):
                slot %= 2
                pool.wait_ge(s_var3, g + 1)
                if after(g, 2):
                    pool.wait_ge(s_norm3, g - 1)
                pool.tensor_tensor(scale3[:, slot, :], var3[:, slot, :], half[:, 0:TILES], ALU.pow).then_inc(s_scale3, 1)
                pool.wait_ge(s_scale3, g + 1)
                pool.tensor_tensor(shift3[:, slot, :], lessmean3[:, slot, :], scale3[:, slot, :], ALU.mult).then_inc(s_shift3, 1)

            def add(g, slot, turn):
                pool.wait_ge(s_inner, g + 1)
                if after(g, 2):
                    pool.wait_ge(s_result, g - 1)
                pool.tensor_tensor(residual[:, slot % 2, :, :], rows[:, slot, :, :], inner[:, slot % 2, :, :], ALU.add).then_inc(s_residual, 1)

            skewed(pool, GN, (scale, 0), (gates, 1), (first_norm, 0), (weigh, 0), (scale_inner, 1), (add, 1), width=4)

        @block.scalar
        def _(act):
            def normalise3(g, slot, turn):
                slot %= 2
                act.wait_ge(s_shift3, g + 1)
                if after(g, 2):
                    act.wait_ge(s_turn3, g - 1)
                for k in range(TILES):
                    last = act.activation(normed3[:, slot, k, :], inner[:, slot, k, :], ACT.Identity,
                                          scale=scale3[:, slot, k:k + 1], bias=shift3[:, slot, k:k + 1])
                last.then_inc(s_norm3, 1)

            def columns3(g, slot, turn):
                if after(g, 2):
                    act.wait_ge(s_up, CH * (g - 1))
                act.wait_ge(s_turn3, g + 1)
                act.activation(x3T[:, slot % 2, :], p_turn3[:, :], ACT.Copy).then_inc(s_x3T, 1)

            def relu(g, k):
                if after(g, 1):
                    act.wait_ge(s_down, CH * (g - 1) + k + 1)
                act.wait_ge(s_up, CH * g + k + 1)
                act.activation(hidden[:, k, :], p_hid[k % 2][:, :], ACT.Relu, bias=b1[:, k:k + 1]).then_inc(s_hidden, 1)

            def relus_first(g, slot, turn):
                relu(g, 0)
                relu(g, 1)

            def normalise(g, slot, turn):
                slot %= 2
                act.wait_ge(s_shift2, g + 1)
                if after(g, 2):
                    act.wait_ge(s_turn, g - 1)
                for k in range(TILES):
                    last = act.activation(normed[:, slot, k, :], rectified[:, slot, k, :], ACT.Identity,
                                          scale=scales[:, slot, TILES + k:TILES + k + 1], bias=shift2[:, slot, k:k + 1])
                last.then_inc(s_norm, 1)

            def relu_third(g, slot, turn):
                relu(g, 2)

            def columns(g, slot, turn):
                if after(g, 2):
                    act.wait_ge(s_skip, g - 1)
                act.wait_ge(s_turn, g + 1)
                act.activation(xT[:, slot % 2, :], p_turn[:, :], ACT.Copy).then_inc(s_xT, 1)

            def relu_last(g, slot, turn):
                relu(g, 3)

            act.wait_ge(s_ready, 1)
            skewed(act, GN, (normalise3, 2), (columns3, 2), (relus_first, 2), (normalise, 0), (relu_third, 2), (columns, 0),
                   (relu_last, 2), width=4)

        @block.vector
        def _(v):
            done = [0]

            def chain(instruction):
                done[0] += 1
                instruction.then_inc(s_chain, 1)
                v.wait_ge(s_chain, done[0])

            v.memset(ones[:, :], 1.0)
            v.memset(ones_bf[:, :], 1.0).then_inc(s_consts, 1)
            v.wait_ge(s_weights, 16 * (9 + CH + 3))
            v.tensor_scalar(w1[:, :], w1_raw[:, :], norm[:, 2:3], None, ALU.mult)
            v.tensor_tensor(beta_out[:, :], beta_rows[:, 0, :], beta_rows[:, 2, :], ALU.add)
            v.tensor_tensor(beta_skip[:, :], beta_rows[:, 1, :], beta_rows[:, 2, :], ALU.subtract)
            chain(v.tensor_scalar(w_skip[:, 0:C], skip_raw[:, :], norm[:, 0:1], None, ALU.mult))
            v.wait_ge(s_prep, 1)
            v.tensor_tensor(b1[:, :], b1_raw[:, :], p_hid[0][:, 0:CH], ALU.add)
            chain(v.tensor_tensor(b_skip[:, 0:C], skip_row[:, :], p_turn[0:1, 0:C], ALU.add))
            v.tensor_tensor(scratch[:, 0, :], w_skip[:, 0:C], beta_skip[:, :], ALU.mult)
            chain(v.tensor_tensor(scratch[0:1, 1, :], b_skip[:, 0:C], beta_skip[0:1, :], ALU.mult))
            v.tensor_reduce(w_skip[:, C:C + 1], scratch[:, 0, :], AX_X, ALU.add)
            chain(v.tensor_reduce(b_skip[:, C:C + 1], scratch[0:1, 1, :], AX_X, ALU.add))
            bf16_parts(chain, v, [skip_parts[:, i, 0, :] for i in range(3)], b_skip[:, :], rest[:, 0, :])
            bf16_parts(chain, v, [b2_parts[:, i, 0, :] for i in range(3)], b2_row[:, :], rest[:, 1, 0:C])
            for i in range(3):
                v.tensor_copy(skip_parts[:, i, 1, :], skip_parts[:, i, 0, :])
                for j in range(1, TILES):
                    last = v.tensor_copy(b2_parts[:, i, j, :], b2_parts[:, i, 0, :])
            last.then_inc(s_ready, 1)
            moment, moment3 = Chain(v, s_moment, 8), Chain(v, s_moment3, 4)

            def first_norms(g, slot, turn):
                moment.start(g)
                v.wait_ge(s_rows[slot], 16 * (turn + 1))
                two = slot % 2
                if after(g, 2):
                    v.wait_ge(s_norm, g - 1)
                    v.wait_ge(s_h1, g - 1)
                moments(v, moment, rows[:, slot], stats[0], tmp[0], mean[:, two, :], var[:, two, :])
                for k in range(TILES):
                    last = v.tensor_scalar(rectified[:, two, k, :], rows[:, slot, k, :], mean[:, two, k:k + 1], 0.0, ALU.subtract, ALU.max)
                moment(last)
                v.tensor_scalar(spreads[:, two, 0:TILES], var[:, two, :], EPS, None, ALU.add)
                moment(moments(v, moment, rectified[:, two], stats[1], tmp[1], lessmean2[:, two, :], var2[:, two, :], less=True))
                v.scalar_tensor_tensor(out=spreads[:, two, TILES:2 * TILES], in0=spreads[:, two, 0:TILES], scalar=EPS, in1=var2[:, two, :],
                                       op0=ALU.mult, op1=ALU.add).then_inc(s_var, 1)

            def logits(g, slot, turn):
                two = slot % 2
                v.wait_ge(s_weighed, g + 1)
                v.tensor_reduce(logit[:, two, :], weighed[:, two, :, :], AX_X, ALU.add).then_inc(s_logit, 1)
                v.wait_ge(s_logit, 2 * g + 1)
                v.wait_ge(s_skip, g + 1)
                v.tensor_tensor(logit[:, two, :].rearrange("p (b k) -> p b k", b=2), skip_tiles(C),
                                logit[:, two, :].rearrange("p (b k) -> p b k", b=2), ALU.add).then_inc(s_logit, 1)
                v.tensor_tensor(by_bank(differ[:, :, :]), skip_tiles(slice(0, C)), by_bank(attended[:, slot, :, :]), ALU.subtract).then_inc(s_blend, 1)

            def finish(g, slot, turn):
                slot %= 2
                v.wait_ge(s_down, CH * (g + 1))
                v.wait_ge(s_residual, g + 1)
                if after(g, 2):
                    v.wait_ge(s_store[slot], 8 * (g - slot))
                v.tensor_tensor(result[:, slot, :, :], p_y[slot][:, :, :], residual[:, slot, :, :], ALU.add).then_inc(s_result, 1)

            def blends(g, slot, turn):
                two = slot % 2
                v.wait_ge(s_gate, g + 1)
                v.tensor_scalar(beta[:, :], gate[:, two, :], 1.0, None, ALU.add).then_inc(s_beta, 1)
                v.wait_ge(s_beta, 2 * g + 1)
                v.reciprocal(beta[:, :], beta[:, :]).then_inc(s_beta, 1)
                v.wait_ge(s_beta, 2 * g + 2)
                v.wait_ge(s_blend, 2 * g + 1)
                for k in range(TILES):
                    last = v.scalar_tensor_tensor(out=blend[:, k, :], in0=differ[:, k, :], scalar=beta[:, k:k + 1], in1=attended[:, slot, k, :],
                                                  op0=ALU.mult, op1=ALU.add)
                last.then_inc(s_blend, 1)
                v.wait_ge(s_blend, 2 * g + 2)
                v.wait_ge(s_h1, g + 1)
                if after(g, 2):
                    v.wait_ge(s_residual, g - 1)
                    v.wait_ge(s_norm3, g - 1)
                v.tensor_tensor(inner[:, two, :, :], blend[:, :, :], h1[:, two, :, :], ALU.add).then_inc(s_inner, 1)
                moment3.start(g)
                v.wait_ge(s_inner, g + 1)
                moment3(moments(v, moment3, inner[:, two], stats[2], tmp[2], lessmean3[:, two, :], var3[:, two, :], less=True))
                v.tensor_scalar(var3[:, two, :], var3[:, two, :], EPS, None, ALU.add).then_inc(s_var3, 1)

            skewed(v, GN, (first_norms, 0), (logits, 1), (finish, 3), (blends, 1), width=4)

        @block.tensor
        def _(pe):
            ident = keep["ident"]
            pe.wait_ge(s_weights, 16 * (9 + CH + 3))
            pe.matmul(p_turn[0:1, 0:C], norm[:, 1:2], skip_raw[:, :], start=True, stop=True)
            for k in range(CH):
                last = pe.matmul(p_hid[0][:, k:k + 1], w1_raw[:, k * P:(k + 1) * P], norm[:, 3:4], start=True, stop=True)
            last.then_inc(s_prep, 1)
            pe.wait_ge(s_consts, 2)
            pe.wait_ge(s_ready, 1)

            def turns3(g, slot, turn):
                pe.wait_ge(s_norm3, g + 1)
                if after(g, 1):
                    pe.wait_ge(s_x3T, g)
                for k in range(TILES):
                    last = pe.transpose(p_turn3[:, k * P:(k + 1) * P], normed3[:, slot % 2, k, :], ident[:, :])
                last.then_inc(s_turn3, 1)

            def up(g, slot, k):
                if after(g, 1) or k >= 2:
                    pe.wait_ge(s_hidden, CH * g + k - 1)
                pe.matmul(p_hid[k % 2][:, :], w1[:, k * P:(k + 1) * P], x3T[:, slot % 2, :], start=True, stop=True).then_inc(s_up, 1)

            def down(g, slot, k):
                pe.wait_ge(s_hidden, CH * g + k + 1)
                for j in range(TILES):
                    last = pe.matmul(p_y[slot % 2][:, j, :], hidden[:, k, j * P:(j + 1) * P], w2[:, k, :], start=False, stop=(k == CH - 1 and j == TILES - 1))
                last.then_inc(s_down, 1)

            def mlp_first(g, slot, turn):
                if after(g, 2):
                    pe.wait_ge(s_result, g - 1)
                for i in range(3):
                    pe.matmul(fold(p_y[slot % 2][:, :, :]), ones_bf[:, :], fold(b2_parts[:, i, :, :]), start=(i == 0), stop=False)
                pe.wait_ge(s_x3T, g + 1)
                up(g, slot, 0)
                up(g, slot, 1)
                down(g, slot, 0)
                up(g, slot, 2)
                down(g, slot, 1)

            def turns(g, slot, turn):
                pe.wait_ge(s_norm, g + 1)
                if after(g, 1):
                    pe.wait_ge(s_xT, g)
                for k in range(TILES):
                    last = pe.transpose(p_turn[:, k * P:(k + 1) * P], normed[:, slot % 2, k, :], ident[:, :])
                last.then_inc(s_turn, 1)

            def mlp_last(g, slot, turn):
                up(g, slot, 3)
                down(g, slot, 2)
                down(g, slot, 3)

            def skips(g, slot, turn):
                if after(g, 1):
                    pe.wait_ge(s_blend, 2 * g - 1)
                    pe.wait_ge(s_logit, 2 * g)
                for b in range(2):
                    for i in range(3):
                        pe.matmul(p_skip[:, b, 0:2 * (C + 1)], ones_bf[:, :], fold(skip_parts[:, i, :, :]), start=(i == 0), stop=False)
                pe.wait_ge(s_xT, g + 1)
                for j in range(TILES):
                    last = pe.matmul(p_skip[:, j // 2, (j % 2) * (C + 1):(j % 2 + 1) * (C + 1)], xT[:, slot % 2, j * P:(j + 1) * P], w_skip[:, :],
                                     start=False, stop=(j % 2 == 1))
                last.then_inc(s_skip, 1)

            skewed(pe, GN, (turns3, 2), (mlp_first, 2), (turns, 0), (mlp_last, 2), (skips, 0), width=4)


def build(nc, a, out):
    N, E = a["x"].shape[0], a["src"].shape[0]
    GE, GN = -(-E // GROUP), -(-N // GROUP)
    assert N % TILES == 0 and GE % 2 == 0 and GN % 2 == 0 and GE <= P and GN <= 2 * P
    shape = (N, E, GE, GN)
    dram = {name: nc.dram_tensor(name, dims, F32).ap() for name, dims in (
        ("mixed", (GN * GROUP, C)), ("attended", (GN * GROUP, C)), ("x1", (GN * GROUP, C)),
        ("same", (GE, GROUP)), ("factor", (GE, 2, GROUP)), ("dinv", (GN * GROUP, 1)))}
    with ExitStack() as ctx:
        def sb(name, dims, dt=F32):
            return ctx.enter_context(nc.sbuf_tensor(name, dims, dt))

        keep = dict(ident=sb("ident", [P, P]), eps=sb("eps", [P, 1]), one=sb("one", [P, 1]),
                    index=sb("index", [P, 3, TILES * GE], I32),
                    selfw=sb("selfw", [P, TILES, GN]), lonew=sb("lonew", [P, TILES, GN]))
        prepare(nc, shape, keep, dram, a["src"], a["dst"])
        edges0(nc, shape, keep, dram, a["x"], a["L0_gnn_bases_W"], a["L0_gnn_comb_W"], a["L0_gnn_comb_b"])
        nodes0(nc, shape, keep, dram, a["x"], a["L0_gnn_bases_W"], a["L0_gnn_comb_W"], a["L0_gnn_comb_b"], a["L0_gnn_bias"])
        prm = {n[len("L1_gnn_"):]: v for n, v in a.items() if n.startswith("L1_gnn_")}
        edges1(nc, shape, keep, dram, a["edge_attr_4"], prm["ln1_g"], prm["ln1_b"],
               {"k": prm["Wk"], "v": prm["Wv"], "q": prm["Wq"]}, {"k": prm["bk"], "v": prm["bv"], "q": prm["bq"]}, prm["We"])
        nodes1(nc, shape, keep, dram, prm, out)


def kernel(**inputs):
    import numpy as np
    import concourse.bacc as bacc
    from concourse.bass_utils import run_bass_kernel_spmd

    nc = bacc.Bacc("TRN2", target_bir_lowering=False, num_devices=1)
    arrays, views = {}, {}
    for name, value in inputs.items():
        array = np.ascontiguousarray(value)
        arrays[f"in_{name}"] = array
        views[name] = nc.dram_tensor(f"in_{name}", array.shape, mybir.dt.from_np(array.dtype), kind="ExternalInput").ap()
    out = nc.dram_tensor("out_x", tuple(inputs["x"].shape), F32, kind="ExternalOutput").ap()
    build(nc, views, out)
    result = run_bass_kernel_spmd(nc, [arrays], core_ids=[0])
    return result.results[0]["out_x"]
```

```python
from contextlib import ExitStack

import concourse.bass as bass
from concourse import mybir

ALU = mybir.AluOpType
ACT = mybir.ActivationFunctionType
F32 = mybir.dt.float32
F16 = mybir.dt.float16
BF16 = mybir.dt.bfloat16
I32 = mybir.dt.int32
AX_X = mybir.AxisListType.X

P = 128
TILES = 4
GROUP = P * TILES
C = 128
EPS = 1e-5
NOWHERE = 1 << 20
HUGE = 3.0e38
INV_E = 0.36787944117144233

HEADS0, BASES, AGGS = 8, 4, 4
D0 = C // HEADS0
BD = BASES * D0
MIX = BASES * AGGS
AGG_ORDER = (1, 0, 3, 2)
HEADS1 = 4
D1 = C // HEADS1
EDGE_C = 4
HID = 4 * C


def after(g, n):
    return not isinstance(g, int) or g >= n


def skewed(eng, count, *stages, peel=0, width=2):
    deepest = max(lag for _, lag in stages)
    head = width * -(-(deepest + width) // width)
    steps = max(0, (count - peel - head) // width)

    def peeled(begin, end):
        for t in range(begin, end):
            for stage, lag in stages:
                if 0 <= t - lag < count:
                    stage(t - lag, (t - lag) % width, (t - lag) // width)

    peeled(0, head)
    if steps:
        with eng.Fori(0, steps) as k:
            for u in range(width):
                for stage, lag in stages:
                    slot = (u - lag) % width
                    turn = k + (head + u - lag - slot) // width
                    stage(turn * width + slot, slot, turn)
    peeled(head + width * steps, count + deepest)


def row_of(vec):
    return vec.rearrange("(o n) -> o n", o=1).to_broadcast([P, vec.shape[0]])


def fold(ap):
    return ap.rearrange("p a b -> p (a b)")


def spread(ap, n):
    return ap.rearrange("p (a o) -> p a o", o=1).to_broadcast([ap.shape[0], ap.shape[1], n])


def over(ap, n):
    return ap.rearrange("p (o a) -> p o a", o=1).to_broadcast([ap.shape[0], n, ap.shape[1]])


class Scope:

    def __init__(self, nc, ctx, tag):
        self.nc, self.ctx, self.tag = nc, ctx, tag
        self.sems = []

    def sb(self, name, shape, dt=F32):
        return self.ctx.enter_context(self.nc.sbuf_tensor(f"{self.tag}_{name}", list(shape), dt))

    def ps(self, name, shape, dt=F32):
        return self.ctx.enter_context(self.nc.psum_tensor(f"{self.tag}_ps_{name}", list(shape), dt))

    def sem(self, name):
        self.sems.append(self.ctx.enter_context(self.nc.semaphore(f"{self.tag}_{name}")))
        return self.sems[-1]

    def clear(self):
        for sem in self.sems:
            self.nc.sync.sem_clear(sem)

    def block(self):
        self.ctx.callback(self.clear)
        return self.ctx.enter_context(self.nc.Block())


def prepare(nc, shape, keep, dram, src, dst):
    N, E, GE, GN = shape
    HB = GN // 2
    with ExitStack() as ctx:
        m = Scope(nc, ctx, "pre")
        dst_i = m.sb("dst_i", [GE, GROUP], I32)
        src_i = m.sb("src_i", [GE, GROUP], I32)
        part_i = m.sb("part_i", [GE, 2, GROUP], I32)
        edge_i = m.sb("edge_i", [GE, 2], I32)
        edge_f = m.sb("edge_f", [GE, 2])
        dst_f = m.sb("dst_f", [GE, GROUP])
        same = m.sb("same", [GE, GROUP])
        same_next = m.sb("same_next", [GE, 1])
        cols = m.sb("cols", [GE, 5, GROUP])
        place_i = m.sb("place_i", [GE, GROUP], I32)
        place = m.sb("place", [GE, GROUP])
        begin = m.sb("begin", [GE, GROUP])
        zero_row = m.sb("zero_row", [GE, GROUP])
        begin_row = m.sb("begin_row", [1, GE + 1])
        factor = m.sb("factor", [GE, 2, GROUP])
        parts = m.sb("parts", [P, 2, TILES * GE])
        zeros = m.sb("zeros", [P, 3584])
        count_i = m.sb("count_i", [P, GROUP], I32)
        ramp = m.sb("ramp", [P, GROUP], F16)
        hot = m.sb("hot", [P, 2, TILES, GROUP + GN], BF16)
        counts = m.sb("counts", [HB, 2, GROUP])
        degree = m.sb("degree", [HB, 2, GROUP])
        dinv = m.sb("dinv", [HB, 2, GROUP])
        turned = [m.ps(f"turned{i}", [P, TILES * GE]) for i in range(5)]
        hist = [m.ps(f"hist{i}", [HB, GROUP]) for i in range(2)]
        s_blank, s_load, s_zero, s_fill = m.sem("blank"), m.sem("load"), m.sem("zero"), m.sem("fill")
        s_id, s_iota, s_ramp, s_chain = m.sem("id"), m.sem("iota"), m.sem("ramp"), m.sem("chain")
        s_last, s_carry, s_runs, s_runroot = m.sem("last"), m.sem("carry"), m.sem("runs"), m.sem("runroot")
        s_same, s_cols, s_turned, s_parts = m.sem("same"), m.sem("cols"), m.sem("turned"), m.sem("parts")
        s_hot, s_hist, s_counts, s_root = m.sem("hot"), m.sem("hist"), m.sem("counts"), m.sem("root")
        s_dinv, s_store, s_node, s_taken = m.sem("dinv"), m.sem("store"), m.sem("node"), m.sem("taken")
        full = (GE - 1) * GROUP
        table = GN * GROUP * C // P
        fills = []
        at = 0
        while at < table:
            fills.append((at, min(3584, table - at)))
            at += 3584
        block = m.block()

        @block.sync
        def _(sp):
            sp.wait_ge(s_blank, 3)
            sp.dma_start(dst_i[0:GE - 1, :], dst[0:full].rearrange("(g c) -> g c", c=GROUP)).then_inc(s_load, 16)
            sp.dma_start(dst_i[GE - 1:GE, 0:E - full], dst[full:E].rearrange("(o c) -> o c", o=1)).then_inc(s_load, 16)
            sp.dma_start(src_i[0:GE - 1, :], src[0:full].rearrange("(g c) -> g c", c=GROUP)).then_inc(s_load, 16)
            sp.dma_start(src_i[GE - 1:GE, 0:E - full], src[full:E].rearrange("(o c) -> o c", o=1)).then_inc(s_load, 16)
            sp.dma_start(edge_i[1:GE, 0:1], dst[0:full].rearrange("(g c) -> g c", c=GROUP)[:, GROUP - 1:GROUP], allow_slow_non_contiguous=True).then_inc(s_load, 16)
            sp.dma_start(edge_i[0:GE - 2, 1:2], dst[GROUP:full].rearrange("(g c) -> g c", c=GROUP)[:, 0:1], allow_slow_non_contiguous=True).then_inc(s_load, 16)
            sp.dma_start(edge_i[GE - 2:GE - 1, 1:2], dst[full:full + 1].rearrange("(o c) -> o c", o=1)).then_inc(s_load, 16)
            sp.wait_ge(s_zero, 1)
            for name in ("mixed", "attended"):
                rows = dram[name].rearrange("(p r) c -> p (r c)", p=P)
                for a, n in fills:
                    sp.dma_start(rows[:, a:a + n], zeros[:, 0:n]).then_inc(s_fill, 16)
            sp.wait_ge(s_same, 1)
            sp.dma_start(dram["same"], same[:, :]).then_inc(s_store, 16)
            sp.wait_ge(s_runs, 3)
            sp.dma_start(dram["factor"].rearrange("g k c -> g (k c)"), factor[:, :, :].rearrange("g k c -> g (k c)")).then_inc(s_store, 16)
            sp.wait_ge(s_dinv, 1)
            sp.dma_start(dram["dinv"].rearrange("(b g c) o -> g b (c o)", b=2, c=GROUP), dinv[:, :, :]).then_inc(s_store, 16)
            sp.wait_ge(s_store, 48)
            sp.wait_ge(s_fill, 16 * 2 * len(fills))

        @block.gpsimd
        def _(pool):
            pool.iota(count_i[:, :], pattern=[[1, GROUP]], base=0, channel_multiplier=0).then_inc(s_iota, 1)
            pool.iota(place_i[:, :], pattern=[[1, GROUP]], base=0, channel_multiplier=GROUP).then_inc(s_iota, 1)
            pool.memset(keep["ident"][:, :], 0.0).then_inc(s_id, 1)
            pool.wait_ge(s_id, 1)
            pool.affine_select(out=keep["ident"][:, :], in_=keep["ident"][:, :], compare_op=ALU.not_equal, fill=1.0,
                               base=0, pattern=[[-1, P]], channel_multiplier=1).then_inc(s_id, 1)

        @block.scalar
        def _(act):
            act.wait_ge(s_runs, 1)
            act.activation(factor[:, 1, :], factor[:, 0, :], ACT.Sqrt, bias=keep["one"][0:GE, :]).then_inc(s_runroot, 1)
            act.wait_ge(s_counts, 2)
            act.activation(dinv[:, :, :], degree[:, :, :], ACT.Sqrt).then_inc(s_root, 1)

        @block.vector
        def _(v):
            done = [0]

            def chain(instruction):
                done[0] += 1
                instruction.then_inc(s_chain, 1)
                v.wait_ge(s_chain, done[0])

            v.memset(dst_i[:, :], NOWHERE).then_inc(s_blank, 1)
            v.memset(src_i[:, :], 0).then_inc(s_blank, 1)
            v.memset(edge_i[:, 0:1], -1)
            v.memset(edge_i[:, 1:2], NOWHERE).then_inc(s_blank, 1)
            v.memset(zeros[:, :], 0.0).then_inc(s_zero, 1)
            v.memset(keep["eps"][:, :], EPS)
            v.memset(keep["one"][:, :], 1.0)
            v.memset(zero_row[:, :], 0.0)
            v.wait_ge(s_iota, 2)
            v.tensor_copy(ramp[:, :], count_i[:, :]).then_inc(s_ramp, 1)
            v.wait_ge(s_load, 16 * 7)
            v.tensor_copy(edge_f[:, :], edge_i[:, :])
            v.tensor_copy(cols[:, 0, :], src_i[:, :])
            v.tensor_scalar(part_i[:, 0, :], dst_i[:, :], 9, None, ALU.logical_shift_right)
            v.tensor_scalar(part_i[:, 1, :], dst_i[:, :], GROUP - 1, None, ALU.bitwise_and)
            chain(v.tensor_copy(dst_f[:, :], dst_i[:, :]))
            v.tensor_copy(cols[:, 3:5, :], part_i[:, :, :])
            v.tensor_scalar(cols[:, 1, :], dst_f[:, :], float(N - 1), None, ALU.min)
            v.tensor_tensor(same[:, 1:GROUP], dst_f[:, 1:GROUP], dst_f[:, 0:GROUP - 1], ALU.is_equal)
            v.tensor_tensor(same[:, 0:1], dst_f[:, 0:1], edge_f[:, 0:1], ALU.is_equal).then_inc(s_same, 1)
            chain(v.tensor_tensor(same_next[:, :], dst_f[:, GROUP - 1:GROUP], edge_f[:, 1:2], ALU.is_equal))
            v.scalar_tensor_tensor(out=cols[:, 2, 0:GROUP - 1], in0=same[:, 1:GROUP], scalar=float(NOWHERE),
                                   in1=dst_f[:, 0:GROUP - 1], op0=ALU.mult, op1=ALU.max)
            v.scalar_tensor_tensor(out=cols[:, 2, GROUP - 1:GROUP], in0=same_next[:, :], scalar=float(NOWHERE),
                                   in1=dst_f[:, GROUP - 1:GROUP], op0=ALU.mult, op1=ALU.max).then_inc(s_cols, 1)
            chain(v.tensor_scalar(begin[:, :], same[:, :], -1.0, 1.0, ALU.mult, ALU.add))
            chain(v.tensor_copy(place[:, :], place_i[:, :]))
            chain(v.tensor_tensor(begin[:, :], begin[:, :], place[:, :], ALU.mult))
            v.tensor_tensor_scan(begin[:, :], zero_row[:, :], begin[:, :], 0.0, ALU.add, ALU.max).then_inc(s_last, 1)
            v.wait_ge(s_carry, 1)
            v.memset(begin_row[:, 0:1], 0.0)
            v.tensor_tensor_scan(begin_row[:, 1:GE + 1], zero_row[0:1, 0:GE], turned[0][0:1, 0:GE], 0.0, ALU.add, ALU.max).then_inc(s_last, 1)
            v.wait_ge(s_carry, 2)
            chain(v.tensor_scalar(begin[:, :], begin[:, :], turned[1][0:GE, 0:1], None, ALU.max))
            chain(v.tensor_tensor(factor[:, 0, :], place[:, :], begin[:, :], ALU.subtract))
            v.tensor_scalar(factor[:, 0, :], factor[:, 0, :], 1.0, None, ALU.add).then_inc(s_runs, 1)
            v.wait_ge(s_runroot, 1)
            v.reciprocal(factor[:, :, :], factor[:, :, :]).then_inc(s_runs, 2)
            for i in range(3):
                v.wait_ge(s_turned, i + 1)
                v.tensor_copy(keep["index"][:, i, :], turned[i][:, :])
            for i in range(2):
                v.wait_ge(s_turned, i + 4)
                last = v.tensor_copy(parts[:, i, :], turned[3 + i][:, :])
            last.then_inc(s_parts, 1)
            v.wait_ge(s_parts, 1)
            v.wait_ge(s_ramp, 1)

            def one_hot(g, slot, turn):
                if after(g, 2):
                    v.wait_ge(s_hist, g - 1)
                for j in range(TILES):
                    v.tensor_scalar(hot[:, slot, j, 0:GROUP], ramp[:, :], parts[:, 1, bass.ds(g + j * GE, 1)], None, ALU.is_equal)
                    last = v.tensor_scalar(hot[:, slot, j, GROUP:GROUP + GN], ramp[:, 0:GN],
                                           parts[:, 0, bass.ds(g + j * GE, 1)], None, ALU.is_equal)
                last.then_inc(s_hot, 1)

            skewed(v, GE, (one_hot, 0))
            v.wait_ge(s_hist, GE)
            for b in range(2):
                v.tensor_copy(counts[:, b, :], hist[b][:, :])
                last = v.tensor_scalar(degree[:, b, :], hist[b][:, :], 1.0, None, ALU.add)
            last.then_inc(s_counts, 2)
            v.wait_ge(s_root, 1)
            v.reciprocal(dinv[:, :, :], dinv[:, :, :]).then_inc(s_dinv, 1)
            for j in range(TILES):
                v.wait_ge(s_node, j + 1)
                taken = turned[j][:, 0:GN]
                chain(v.tensor_scalar(keep["selfw"][:, j, :], taken, 1.0, None, ALU.add))
                v.reciprocal(keep["selfw"][:, j, :], keep["selfw"][:, j, :])
                v.tensor_scalar(keep["lonew"][:, j, :], taken, 0.0, float(EPS) ** 0.5, ALU.is_equal, ALU.mult).then_inc(s_taken, 1)

        @block.tensor
        def _(pe):
            ident = keep["ident"]
            pe.wait_ge(s_id, 2)
            pe.wait_ge(s_last, 1)
            pe.transpose(turned[0][0:1, 0:GE], begin[:, GROUP - 1:GROUP], ident[0:GE, 0:GE]).then_inc(s_carry, 1)
            pe.wait_ge(s_last, 2)
            pe.transpose(turned[1][0:GE, 0:1], begin_row[:, 0:GE], ident[0:1, 0:1]).then_inc(s_carry, 1)
            pe.wait_ge(s_runs, 1)
            pe.wait_ge(s_cols, 1)
            for i in range(5):
                for j in range(TILES):
                    last = pe.transpose(turned[i][:, j * GE:(j + 1) * GE], cols[:, i, j * P:(j + 1) * P], ident[0:GE, 0:GE])
                last.then_inc(s_turned, 1)

            def histogram(g, slot, turn):
                pe.wait_ge(s_hot, g + 1)
                for j in range(TILES):
                    first = isinstance(g, int) and g == 0 and j == 0
                    final = isinstance(g, int) and g == GE - 1 and j == TILES - 1
                    for b in range(2):
                        last = pe.matmul(hist[b][:, :], hot[:, slot, j, GROUP + b * HB:GROUP + (b + 1) * HB],
                                         hot[:, slot, j, 0:GROUP], start=first, stop=final)
                last.then_inc(s_hist, 1)

            skewed(pe, GE, (histogram, 1))
            pe.wait_ge(s_counts, 2)
            pe.wait_ge(s_parts, 1)
            for j in range(TILES):
                for b in range(2):
                    last = pe.transpose(turned[j][:, b * HB:(b + 1) * HB], counts[:, b, j:GROUP:TILES], ident[0:HB, 0:HB])
                last.then_inc(s_node, 1)


class Chain:

    def __init__(self, eng, sem, steps):
        self.eng, self.sem, self.steps = eng, sem, steps

    def start(self, g):
        self.at = g * self.steps

    def __call__(self, instruction):
        instruction.then_inc(self.sem, 1)
        self.at = self.at + 1
        self.eng.wait_ge(self.sem, self.at)


class Moments:

    def __init__(self, v, sem, steps, first):
        self.v, self.sem, self.steps, self.first = v, sem, steps, first

    def stats(self, g, rows, stats):
        for k in range(rows.shape[1]):
            last = self.v.bn_stats(stats[:, k, :], rows[:, k, :])
        last.then_inc(self.sem, 1)

    def sums(self, g, stats, tmp):
        self.v.wait_ge(self.sem, g * self.steps + self.first + 1)
        self.v.tensor_tensor(tmp[:, 0, :], stats[:, :, 1], stats[:, :, 4], ALU.add)
        self.v.tensor_tensor(tmp[:, 1, :], stats[:, :, 1], stats[:, :, 4], ALU.subtract)
        self.v.tensor_tensor(tmp[:, 2, :], stats[:, :, 2], stats[:, :, 5], ALU.add).then_inc(self.sem, 1)

    def mean(self, g, tmp, mean, half):
        self.v.wait_ge(self.sem, g * self.steps + self.first + 2)
        self.v.tensor_scalar(mean, tmp[:, 0, :], half, None, ALU.mult)
        self.v.scalar_tensor_tensor(out=tmp[:, 3, :], in0=tmp[:, 1, :], scalar=0.25, in1=tmp[:, 1, :],
                                    op0=ALU.mult, op1=ALU.mult).then_inc(self.sem, 1)

    def variance(self, tmp, var):
        return self.v.scalar_tensor_tensor(out=var, in0=tmp[:, 2, :], scalar=1.0 / C, in1=tmp[:, 3, :],
                                           op0=ALU.mult, op1=ALU.add)


def moments(v, chain, rows, stats, tmp, mean, var, less=False):
    for k in range(rows.shape[1]):
        last = v.bn_stats(stats[:, k, :], rows[:, k, :])
    chain(last)
    v.tensor_tensor(tmp[:, 0, :], stats[:, :, 1], stats[:, :, 4], ALU.add)
    v.tensor_tensor(tmp[:, 1, :], stats[:, :, 1], stats[:, :, 4], ALU.subtract)
    chain(v.tensor_tensor(tmp[:, 2, :], stats[:, :, 2], stats[:, :, 5], ALU.add))
    v.tensor_scalar(mean, tmp[:, 0, :], -0.5 if less else 0.5, None, ALU.mult)
    chain(v.scalar_tensor_tensor(out=tmp[:, 3, :], in0=tmp[:, 1, :], scalar=0.25, in1=tmp[:, 1, :],
                                 op0=ALU.mult, op1=ALU.mult))
    return v.scalar_tensor_tensor(out=var, in0=tmp[:, 2, :], scalar=1.0 / C, in1=tmp[:, 3, :],
                                  op0=ALU.mult, op1=ALU.add)


def index_of(keep, GE, kinds, g):
    a, b = kinds
    return keep["index"][:, a:b, :].rearrange("p k (j g) -> p (k j) g", g=GE)[:, :, bass.ds(g, 1)]


def bf16_parts(chain, v, target, source, remain):
    chain(v.tensor_copy(remain, source))
    for i in range(3):
        chain(v.tensor_copy(target[i], remain))
        chain(v.tensor_tensor(remain, remain, target[i], ALU.subtract))


def edges0(nc, shape, keep, dram, x, bases_W, comb_W, comb_b):
    N, E, GE, GN = shape
    K = 2 * TILES
    with ExitStack() as ctx:
        m = Scope(nc, ctx, "e0")
        w_bases = m.sb("w_bases", [C, 2 * BD])
        w_raw = m.sb("w_raw", [C, HEADS0 * MIX])
        w_mix = m.sb("w_mix", [C, HEADS0 * MIX])
        b_raw = m.sb("b_raw", [1, HEADS0 * MIX])
        b_mix = m.sb("b_mix", [1, HEADS0 * MIX])
        b_rest = m.sb("b_rest", [1, HEADS0 * MIX])
        b_parts = m.sb("b_parts", [1, 3, TILES, HEADS0 * MIX], BF16)
        b_three = m.sb("b_three", [3, TILES * HEADS0 * MIX], BF16)
        ones = m.sb("ones", [3, P], BF16)
        gidx = m.sb("gidx", [P, 2, K], I32)
        sidx = m.sb("sidx", [P, 2, TILES], I32)
        rows = m.sb("rows", [P, 2, K, C])
        scale = m.sb("scale", [P, 2, TILES])
        same = m.sb("same", [P, 2, GROUP])
        barrier = m.sb("barrier", [P, 2, GROUP])
        stats = m.sb("stats", [P, K, 6])
        tmp = m.sb("tmp", [P, 4, K])
        lessmean, var, root, rstd, shift = (m.sb(n, [P, 2, K]) for n in ("lessmean", "var", "root", "rstd", "shift"))
        normed = m.sb("normed", [P, 2, K, C])
        hT = m.sb("hT", [P, 2, 2, GROUP])
        wide = m.sb("wide", [P, 2, TILES, P])
        twin = m.sb("twin", [P, 2, GROUP])
        square = m.sb("square", [BD, 2, GROUP])
        value = m.sb("value", [P, GROUP])
        factor = m.sb("factor", [P, 2, GROUP])
        total = m.sb("total", [P, 2, GROUP])
        total_sq = m.sb("total_sq", [BD, 2, GROUP])
        aggs = m.sb("aggs", [P, 2, 2, GROUP])
        msq = m.sb("msq", [BD, 2, GROUP])
        mean_sq = m.sb("mean_sq", [BD, GROUP])
        relu_var = m.sb("relu_var", [BD, GROUP])
        top = m.sb("top", [P, TILES * HEADS0])
        mix = m.sb("mix", [P, 2, TILES, HEADS0 * MIX])
        mixsum = m.sb("mixsum", [P, TILES * HEADS0])
        inverse = m.sb("inverse", [P, 2, TILES * HEADS0])
        prod = m.sb("prod", [P, TILES, MIX, C])
        outrow = m.sb("outrow", [P, 2, TILES, C])
        p_turn = m.ps("turn", [P, GROUP])
        p_twin = m.ps("twin", [P, GROUP])
        p_wide = m.ps("wide", [P, GROUP])
        p_mix = m.ps("mix", [P, TILES, HEADS0 * MIX])
        p_aggs = m.ps("aggs", [P, TILES, 2 * P])
        p_out = [m.ps(f"out{i}", [P, TILES, C]) for i in range(2)]
        s_weights, s_prep, s_ready, s_three = m.sem("weights"), m.sem("prep"), m.sem("ready"), m.sem("three")
        s_gidx, s_sidx, s_issue = m.sem("gidx"), m.sem("sidx"), m.sem("issue")
        s_rows = [m.sem(f"rows{i}") for i in range(2)]
        s_dinv = [m.sem(f"dinv{i}") for i in range(2)]
        s_same = [m.sem(f"same{i}") for i in range(2)]
        s_scatter = [m.sem(f"scatter{i}") for i in range(2)]
        s_factor = [m.sem(f"factor{i}") for i in range(2)]
        s_moment, s_var, s_root, s_rstd, s_shift, s_norm = (m.sem(n) for n in ("moment", "var", "root", "rstd", "shift", "norm"))
        s_turn, s_hT, s_wide, s_bases, s_scales, s_mix = (m.sem(n) for n in ("turn", "hT", "wide", "bases", "scales", "mix"))
        s_twin, s_top, s_sub, s_exp, s_barrier = (m.sem(n) for n in ("twin", "top", "sub", "exp", "barrier"))
        s_scan, s_mean, s_meansq, s_varb, s_relu, s_std = (m.sem(n) for n in ("scan", "mean", "meansq", "varb", "relu", "std"))
        s_aggs, s_mixsum, s_inverse, s_prod, s_reduced = (m.sem(n) for n in ("aggs", "mixsum", "inverse", "prod", "reduced"))
        s_out = m.sem("out")
        s_go = m.sem("go")
        block = m.block()

        @block.sync
        def _(sp):
            sp.dma_start(w_bases[:, 0:BD].rearrange("c (b d) -> c b d", b=BASES), bases_W.rearrange("b c d -> c b d")).then_inc(s_weights, 16)
            sp.dma_start(w_bases[:, BD:2 * BD].rearrange("c (b d) -> c b d", b=BASES), bases_W.rearrange("b c d -> c b d")).then_inc(s_weights, 16)
            sp.dma_start(w_raw[:, :], comb_W).then_inc(s_weights, 16)
            sp.dma_start(b_raw[:, :], comb_b.rearrange("(o n) -> o n", o=1)).then_inc(s_weights, 16)
            sp.wait_ge(s_ready, 1)
            for i in range(3):
                sp.dma_start(b_three[i:i + 1, :], fold(b_parts[:, i, :, :])).then_inc(s_three, 16)

            def load(g, slot, turn):
                if after(g, 2):
                    sp.wait_ge(s_scan, 2 * (g - 1))
                    sp.sem_inc(s_go, 1)
                    sp.wait_ge(s_barrier, g - 1)
                    sp.sem_inc(s_go, 1)
                sp.dma_start(same[:, slot, :], dram["same"][bass.ds(g, 1), :].to_broadcast([P, GROUP])).then_inc(s_same[slot], 16)
                if after(g, 2):
                    sp.wait_ge(s_mean, g - 1)
                    sp.sem_inc(s_go, 1)
                for i in range(2):
                    sp.dma_start(factor[i * BD:(i + 1) * BD, slot, :],
                                 dram["factor"][bass.ds(g, 1), i, :].to_broadcast([BD, GROUP])).then_inc(s_factor[slot], 16)

            skewed(sp, GE, (load, 0))

        @block.gpsimd
        def _(pool):
            def gather(g, slot, turn):
                if after(g, 2):
                    pool.wait_ge(s_norm, g - 1)
                    pool.wait_ge(s_wide, g - 1)
                    pool.sem_inc(s_issue, 1)
                pool.tensor_copy(gidx[:, slot, :].rearrange("p (k o) -> p k o", o=1), index_of(keep, GE, (0, 2), g)).then_inc(s_gidx, 1)
                pool.wait_ge(s_gidx, g + 1)
                pool.sem_inc(s_issue, 1)
                for k in range(K):
                    pool.indirect_dma_start(rows[:, slot, k, :], None, x, bass.IndirectOffsetOnAxis(ap=gidx[:, slot, k:k + 1], axis=0)).then_inc(s_rows[slot], 16)
                for k in range(TILES):
                    pool.indirect_dma_start(scale[:, slot, k:k + 1], None, dram["dinv"],
                                            bass.IndirectOffsetOnAxis(ap=gidx[:, slot, k:k + 1], axis=0)).then_inc(s_dinv[slot], 16)

            def scatter(g, slot, turn):
                if after(g, 2):
                    pool.wait_ge(s_scatter[slot], 64 * turn)
                    pool.sem_inc(s_issue, 1)
                pool.tensor_copy(sidx[:, slot, :].rearrange("p (k o) -> p k o", o=1), index_of(keep, GE, (2, 3), g)).then_inc(s_sidx, 1)
                pool.wait_ge(s_sidx, g + 1)
                pool.wait_ge(s_out, g + 1)
                pool.sem_inc(s_issue, 1)
                for k in range(TILES):
                    pool.indirect_dma_start(dram["mixed"], bass.IndirectOffsetOnAxis(ap=sidx[:, slot, k:k + 1], axis=0), outrow[:, slot, k, :], None,
                                            bounds_check=N - 1, oob_is_err=False).then_inc(s_scatter[slot], 16)

            skewed(pool, GE, (gather, 0), (scatter, 6))
            for i in range(2):
                pool.wait_ge(s_scatter[i], 64 * (GE // 2))

        @block.scalar
        def _(act):
            def deviation(g, slot, turn):
                act.wait_ge(s_varb, g + 1)
                act.activation(relu_var[:, :], msq[:, slot, :], ACT.Relu).then_inc(s_relu, 1)
                act.wait_ge(s_relu, g + 1)
                act.activation(aggs[0:BD, slot, 1, :], relu_var[:, :], ACT.Sqrt, bias=keep["eps"][0:BD, :]).then_inc(s_std, 1)

            def columns(g, slot, turn):
                if after(g, 2):
                    act.wait_ge(s_mix, g - 1)
                for i in range(2):
                    act.wait_ge(s_turn, 2 * g + i + 1)
                    act.activation(hT[:, slot, i, :], p_turn[:, :], ACT.Relu).then_inc(s_hT, 1)

            def roots(g, slot, turn):
                act.wait_ge(s_var, g + 1)
                act.activation(root[:, slot, :], var[:, slot, :], ACT.Sqrt, bias=keep["eps"][:, :]).then_inc(s_root, 1)

            def widen(g, slot, turn):
                if after(g, 2):
                    act.wait_ge(s_scales, g - 1)
                act.wait_ge(s_dinv[slot], 64 * (turn + 1))
                act.activation(wide[:, slot, :, BD:P], scale[:, slot, :].rearrange("p (j o) -> p j o", o=1).to_broadcast([P, TILES, P - BD]),
                               ACT.Copy).then_inc(s_wide, 1)

            def twins(g, slot, turn):
                act.wait_ge(s_bases, g + 1)
                if after(g, 2):
                    act.wait_ge(s_scan, 2 * (g - 1))
                act.activation(twin[:, slot, :], p_twin[:, :], ACT.Copy)
                act.activation(square[:, slot, :], p_twin[0:BD, :], ACT.Square).then_inc(s_twin, 1)
                act.wait_ge(s_same[slot], 16 * (turn + 1))
                act.activation(barrier[BD:P, slot, :], same[BD:P, slot, :], ACT.Copy, scale=HUGE, bias=-HUGE).then_inc(s_barrier, 1)

            def mean_squares(g, slot, turn):
                act.wait_ge(s_mean, g + 1)
                if after(g, 1):
                    act.wait_ge(s_varb, g)
                act.activation(mean_sq[:, :], aggs[0:BD, slot, 0, :], ACT.Square).then_inc(s_meansq, 1)

            def normalise(g, slot, turn):
                act.wait_ge(s_shift, g + 1)
                if after(g, 2):
                    act.wait_ge(s_turn, 2 * (g - 1))
                for k in range(K):
                    last = act.activation(normed[:, slot, k, :], rows[:, slot, k, :], ACT.Identity,
                                          scale=rstd[:, slot, k:k + 1], bias=shift[:, slot, k:k + 1])
                last.then_inc(s_norm, 1)

            def exponent(g, slot, turn):
                act.wait_ge(s_sub, g + 1)
                act.activation(fold(mix[:, slot, :, :]), fold(mix[:, slot, :, :]), ACT.Exp).then_inc(s_exp, 1)

            act.wait_ge(s_ready, 1)
            skewed(act, GE, (deviation, 4), (columns, 2), (roots, 1), (widen, 1), (twins, 2), (mean_squares, 3), (normalise, 1),
                   (exponent, 3))

        @block.vector
        def _(v):
            v.memset(ones[:, :], 1.0)
            v.memset(wide[:, 0, :, 0:BD], 1.0)
            v.memset(wide[:, 1, :, 0:BD], 1.0)
            v.wait_ge(s_weights, 64)
            prep = Chain(v, s_prep, 0)
            prep.start(0)
            order_mix(v, prep, w_mix, w_raw, b_mix, b_raw)
            bf16_parts(prep, v, [b_parts[:, i, 0, :] for i in range(3)], b_mix[:, :], b_rest[:, :])
            for j in range(1, TILES):
                last = v.tensor_copy(b_parts[:, :, j, :], b_parts[:, :, 0, :])
            last.then_inc(s_ready, 1)
            moment = Moments(v, s_moment, 3, 0)

            def row_stats(g, slot, turn):
                v.wait_ge(s_rows[slot], 128 * (turn + 1))
                if after(g, 1):
                    v.wait_ge(s_var, g)
                moment.stats(g, rows[:, slot], stats)

            def row_sums(g, slot, turn):
                moment.sums(g, stats, tmp)

            def row_means(g, slot, turn):
                if after(g, 2):
                    v.wait_ge(s_shift, g - 1)
                moment.mean(g, tmp, lessmean[:, slot, :], -0.5)

            def row_variances(g, slot, turn):
                v.wait_ge(s_moment, 3 * g + 3)
                moment.variance(tmp, var[:, slot, :]).then_inc(s_var, 1)

            def scales(g, slot, turn):
                v.wait_ge(s_root, g + 1)
                if after(g, 2):
                    v.wait_ge(s_norm, g - 1)
                v.reciprocal(rstd[:, slot, :], root[:, slot, :]).then_inc(s_rstd, 1)

            def shifts(g, slot, turn):
                v.wait_ge(s_rstd, g + 1)
                v.tensor_tensor(shift[:, slot, :], lessmean[:, slot, :], rstd[:, slot, :], ALU.mult).then_inc(s_shift, 1)

            def highest(g, slot, turn):
                v.wait_ge(s_mix, g + 1)
                v.tensor_reduce(top[:, :], p_mix[:, :, :].rearrange("p j (h k) -> p (j h) k", k=MIX), AX_X, ALU.max).then_inc(s_top, 1)

            def shift_down(g, slot, turn):
                v.wait_ge(s_top, g + 1)
                if after(g, 2):
                    v.wait_ge(s_prod, 4 * (g - 1))
                v.tensor_tensor(mix[:, slot, :, :].rearrange("p j (h k) -> p (j h) k", k=MIX),
                                p_mix[:, :, :].rearrange("p j (h k) -> p (j h) k", k=MIX), spread(top[:, :], MIX), ALU.subtract).then_inc(s_sub, 1)

            def values(g, slot, turn):
                v.wait_ge(s_twin, g + 1)
                v.wait_ge(s_scales, g + 1)
                if after(g, 1):
                    v.wait_ge(s_scan, 2 * g)
                v.tensor_tensor(value[:, :], p_wide[:, :], twin[:, slot, :], ALU.mult).then_inc(s_scan, 1)

            def carry(g, tile):
                return 0.0 if isinstance(g, int) and g == 0 else tile[:, GROUP - 1:GROUP]

            def totals(g, slot, turn):
                v.wait_ge(s_same[slot], 16 * (turn + 1))
                v.wait_ge(s_scan, 2 * g + 1)
                v.tensor_tensor_scan(total[:, slot, :], same[:, slot, :], value[:, :], carry(g, total[:, 1 - slot, :]), ALU.mult, ALU.add)
                v.tensor_tensor_scan(total_sq[:, slot, :], same[0:BD, slot, :], square[:, slot, :],
                                     carry(g, total_sq[:, 1 - slot, :]), ALU.mult, ALU.add)

            def tops(g, slot, turn):
                v.wait_ge(s_barrier, g + 1)
                if after(g, 2):
                    v.wait_ge(s_aggs, g - 1)
                v.tensor_tensor_scan(aggs[BD:P, slot, 1, :], barrier[BD:P, slot, :], twin[BD:P, slot, :],
                                     carry(g, aggs[BD:P, 1 - slot, 1, :]), ALU.add, ALU.max).then_inc(s_scan, 1)

            def averages(g, slot, turn):
                v.wait_ge(s_scan, 2 * g + 2)
                v.wait_ge(s_factor[slot], 32 * (turn + 1))
                if after(g, 2):
                    v.wait_ge(s_std, g - 1)
                v.tensor_tensor(msq[:, slot, :], total_sq[:, slot, :], factor[0:BD, slot, :], ALU.mult)
                v.tensor_tensor(aggs[:, slot, 0, :], total[:, slot, :], factor[:, slot, :], ALU.mult).then_inc(s_mean, 1)

            def variances(g, slot, turn):
                v.wait_ge(s_meansq, g + 1)
                v.tensor_tensor(msq[:, slot, :], msq[:, slot, :], mean_sq[:, :], ALU.subtract).then_inc(s_varb, 1)

            def weight_sums(g, slot, turn):
                v.wait_ge(s_exp, g + 1)
                if after(g, 1):
                    v.wait_ge(s_inverse, g)
                v.tensor_reduce(mixsum[:, :], mix[:, slot, :, :].rearrange("p j (h k) -> p (j h) k", k=MIX), AX_X, ALU.add).then_inc(s_mixsum, 1)

            def products(g, slot, turn):
                v.wait_ge(s_aggs, g + 1)
                for j in range(TILES):
                    if after(g, 1):
                        v.wait_ge(s_reduced, 4 * g - 3 + j)
                    v.tensor_tensor(prod[:, j, :, :].rearrange("p k (h d) -> p k h d", h=HEADS0),
                                    mix[:, slot, j, :].rearrange("p (h k o) -> p k h o", k=MIX, o=1).to_broadcast([P, MIX, HEADS0, D0]),
                                    p_aggs[:, j, :].rearrange("p (k o d) -> p k o d", k=MIX, o=1).to_broadcast([P, MIX, HEADS0, D0]),
                                    ALU.mult).then_inc(s_prod, 1)
                v.wait_ge(s_mixsum, g + 1)
                if after(g, 2):
                    v.wait_ge(s_out, g - 1)
                v.reciprocal(inverse[:, slot, :], mixsum[:, :]).then_inc(s_inverse, 1)

            def finish(g, slot, turn):
                v.wait_ge(s_inverse, g + 1)
                v.wait_ge(s_reduced, TILES * (g + 1))
                if after(g, 2):
                    v.wait_ge(s_scatter[slot], 64 * turn)
                v.tensor_tensor(outrow[:, slot, :, :].rearrange("p j (h d) -> p (j h) d", h=HEADS0),
                                p_out[slot][:, :, :].rearrange("p j (h d) -> p (j h) d", h=HEADS0),
                                spread(inverse[:, slot, :], D0), ALU.mult).then_inc(s_out, 1)

            skewed(v, GE, (row_stats, 1), (values, 3), (row_sums, 1), (totals, 3), (row_means, 1), (tops, 3), (row_variances, 1),
                   (averages, 3), (scales, 1), (weight_sums, 4), (shifts, 1), (products, 4), (variances, 3), (highest, 2), (finish, 5),
                   (shift_down, 2))

        @block.tensor
        def _(pe):
            ident = keep["ident"]
            pe.wait_ge(s_ready, 1)
            pe.wait_ge(s_three, 48)

            def turns(g, slot, i):
                for k in range(TILES):
                    last = pe.transpose(p_turn[:, k * P:(k + 1) * P], normed[:, slot, i * TILES + k, :], ident[:, :])
                last.then_inc(s_turn, 1)

            def turn_sources(g, slot, turn):
                pe.wait_ge(s_norm, g + 1)
                if after(g, 1):
                    pe.wait_ge(s_hT, 2 * g)
                turns(g, slot, 0)

            def turn_destinations(g, slot, turn):
                pe.wait_ge(s_hT, 2 * g + 1)
                turns(g, slot, 1)

            def turn_back(g, slot, turn):
                pe.wait_ge(s_std, g + 1)
                pe.wait_ge(s_mean, g + 1)
                if after(g, 1):
                    pe.wait_ge(s_prod, 4 * g)
                for j in range(TILES):
                    for i in range(2):
                        last = pe.transpose(p_aggs[:, j, i * P:(i + 1) * P], aggs[:, slot, i, j * P:(j + 1) * P], ident[:, :])
                last.then_inc(s_aggs, 1)

            def project(g, slot, turn):
                if after(g, 1):
                    pe.wait_ge(s_twin, g)
                pe.matmul(p_twin[:, :], w_bases[:, :], hT[:, slot, 0, :], start=True, stop=True).then_inc(s_bases, 1)
                if after(g, 1):
                    pe.wait_ge(s_sub, g)
                pe.matmul(fold(p_mix[:, :, :]), ones[:, :], b_three[:, :], start=True, stop=False)
                pe.wait_ge(s_hT, 2 * g + 2)
                for j in range(TILES):
                    last = pe.matmul(p_mix[:, j, :], hT[:, slot, 1, j * P:(j + 1) * P], w_mix[:, :], start=False, stop=(j == TILES - 1))
                last.then_inc(s_mix, 1)
                pe.wait_ge(s_wide, g + 1)
                if after(g, 1):
                    pe.wait_ge(s_scan, 2 * g - 1)
                for j in range(TILES):
                    last = pe.transpose(p_wide[:, j * P:(j + 1) * P], wide[:, slot, j, :], ident[:, :])
                last.then_inc(s_scales, 1)

            def reduce(g, slot, tiles):
                for j in tiles:
                    pe.wait_ge(s_prod, TILES * g + j + 1)
                    for k in range(MIX):
                        last = pe.matmul(p_out[slot][:, j, :], ident[:, :], prod[:, j, k, :], start=(k == 0), stop=(k == MIX - 1))
                    last.then_inc(s_reduced, 1)

            def reduce_first(g, slot, turn):
                if after(g, 2):
                    pe.wait_ge(s_out, g - 1)
                reduce(g, slot, (0, 1))

            def reduce_last(g, slot, turn):
                reduce(g, slot, (2, 3))

            skewed(pe, GE, (turn_sources, 2), (turn_back, 4), (turn_destinations, 2), (project, 2), (reduce_last, 5), (reduce_first, 4))


def order_mix(v, chain, w_mix, w_raw, b_mix, b_raw):
    for i, a in enumerate(AGG_ORDER):
        for target, source in ((w_mix, w_raw), (b_mix, b_raw)):
            last = v.tensor_copy(target[:, :].rearrange("c (h q b) -> c h q b", h=HEADS0, q=AGGS)[:, :, i, :],
                                 source[:, :].rearrange("c (h b q) -> c h b q", h=HEADS0, q=AGGS)[:, :, :, a])
    chain(last)


def node_rows(table, N, g):
    if not isinstance(g, int):
        return table[bass.ds(g * GROUP, GROUP), :].rearrange("(p j) c -> p j c", j=TILES), P
    n = min(GROUP, N - g * GROUP) // TILES
    return table[g * GROUP:g * GROUP + n * TILES, :].rearrange("(p j) c -> p j c", j=TILES), n


def nodes0(nc, shape, keep, dram, x, bases_W, comb_W, comb_b, bias):
    N, E, GE, GN = shape
    JH = TILES * HEADS0
    with ExitStack() as ctx:
        m = Scope(nc, ctx, "n0")
        w_bases = m.sb("w_bases", [C, BD])
        w_raw = m.sb("w_raw", [C, HEADS0 * MIX])
        w_mix = m.sb("w_mix", [C, HEADS0 * MIX])
        b_raw = m.sb("b_raw", [1, HEADS0 * MIX])
        b_mix = m.sb("b_mix", [1, HEADS0 * MIX])
        b_rest = m.sb("b_rest", [1, HEADS0 * MIX])
        b_parts = m.sb("b_parts", [1, 3, TILES, HEADS0 * MIX], BF16)
        b_three = m.sb("b_three", [3, TILES * HEADS0 * MIX], BF16)
        b_out = m.sb("b_out", [P, C])
        ones = m.sb("ones", [3, P], BF16)
        half = m.sb("half", [P, TILES])
        rows = m.sb("rows", [P, 4, TILES, C])
        mixed = m.sb("mixed", [P, 4, TILES, C])
        stats = m.sb("stats", [P, TILES, 6])
        tmp = m.sb("tmp", [P, 4, TILES])
        lessmean, var, spreads = (m.sb(n, [P, 2, TILES]) for n in ("lessmean", "var", "spreads"))
        scale, shift = (m.sb(n, [P, 2, TILES]) for n in ("scale", "shift"))
        normed = m.sb("normed", [P, 2, TILES, C])
        hT = m.sb("hT", [P, 2, GROUP])
        bases = m.sb("bases", [P, 4, TILES, BD])
        top = m.sb("top", [P, JH])
        mix = m.sb("mix", [P, 2, TILES, HEADS0 * MIX])
        mixsum = m.sb("mixsum", [P, JH])
        inverse = m.sb("inverse", [P, JH])
        lone = m.sb("lone", [P, 3, JH])
        selfs = m.sb("selfs", [P, 2, JH])
        lones = m.sb("lones", [P, 2, JH])
        prod = m.sb("prod", [P, 2, BASES, TILES, C])
        residual = m.sb("residual", [P, 4, TILES, C])
        part = m.sb("part", [P, TILES, C])
        x1 = m.sb("x1", [P, 2, TILES, C])
        p_turn = m.ps("turn", [P, GROUP])
        p_mix = [m.ps(f"mix{i}", [P, TILES, HEADS0 * MIX]) for i in range(2)]
        p_bases = m.ps("bases", [P, TILES, BD])
        p_out = [m.ps(f"out{i}", [P, TILES, C]) for i in range(2)]
        s_weights, s_ready, s_consts, s_prep = m.sem("weights"), m.sem("ready"), m.sem("consts"), m.sem("prep")
        s_three = m.sem("three")
        s_rows = [m.sem(f"rows{i}") for i in range(4)]
        s_mixed = [m.sem(f"mixed{i}") for i in range(4)]
        s_store = [m.sem(f"store{i}") for i in range(2)]
        s_moment, s_var, s_scale, s_shift, s_norm = (m.sem(n) for n in ("moment", "var", "scale", "shift", "norm"))
        s_turn, s_hT, s_mix, s_bases, s_top, s_sub, s_exp = (m.sem(n) for n in ("turn", "hT", "mix", "bases", "top", "sub", "exp"))
        s_small, s_selfs, s_prod, s_prod_last, s_reduced = (m.sem(n) for n in ("small", "selfs", "prod", "prod_last", "reduced"))
        s_part, s_x1, s_added, s_residual = (m.sem(n) for n in ("part", "x1", "added", "residual"))
        s_go = m.sem("go")
        block = m.block()

        def products_of(eng, j, slot, two):
            return eng.tensor_tensor(prod[:, two, :, j, :].rearrange("p b (h d) -> p b h d", h=HEADS0),
                                     mix[:, two, j, :].rearrange("p (h q b o) -> p q b h o", q=AGGS, b=BASES, o=1)[:, 1].to_broadcast([P, BASES, HEADS0, D0]),
                                     bases[:, slot, j, :].rearrange("p (b o d) -> p b o d", b=BASES, o=1).to_broadcast([P, BASES, HEADS0, D0]),
                                     ALU.mult)

        def by_head(tiles):
            return tiles.rearrange("p j (h k) -> p (j h) k", k=MIX)

        @block.sync
        def _(sp):
            sp.dma_start(w_bases[:, :].rearrange("c (b d) -> c b d", b=BASES), bases_W.rearrange("b c d -> c b d")).then_inc(s_weights, 16)
            sp.dma_start(w_raw[:, :], comb_W).then_inc(s_weights, 16)
            sp.dma_start(b_raw[:, :], comb_b.rearrange("(o n) -> o n", o=1)).then_inc(s_weights, 16)
            sp.dma_start(b_out[:, :], row_of(bias)).then_inc(s_weights, 16)
            sp.wait_ge(s_ready, 1)
            for i in range(3):
                sp.dma_start(b_three[i:i + 1, :], fold(b_parts[:, i, :, :])).then_inc(s_three, 16)

            def load(g, slot, turn):
                if after(g, 4):
                    sp.wait_ge(s_norm, g - 3)
                    sp.sem_inc(s_go, 1)
                    sp.wait_ge(s_added, 2 * (g - 3))
                    sp.sem_inc(s_go, 1)
                source, n = node_rows(x, N, g)
                sp.dma_start(rows[0:n, slot, :, :], source).then_inc(s_rows[slot], 16)
                source, n = node_rows(dram["mixed"], GN * GROUP, g)
                sp.dma_start(mixed[:, slot, :, :], source).then_inc(s_mixed[slot], 16)

            def store(g, slot, turn):
                sp.wait_ge(s_x1, g + 1)
                sp.sem_inc(s_go, 1)
                sp.dma_start(node_rows(dram["x1"], GN * GROUP, g)[0], x1[:, slot % 2, :, :]).then_inc(s_store[slot % 2], 16)

            skewed(sp, GN, (load, 0), (store, 7), peel=2, width=4)
            for i in range(2):
                sp.wait_ge(s_store[i], 16 * (GN // 2))

        @block.gpsimd
        def _(pool):
            pool.memset(half[:, :], -0.5).then_inc(s_consts, 1)
            pool.wait_ge(s_consts, 1)
            pool.wait_ge(s_weights, 64)

            def scales(g, slot, turn):
                slot %= 2
                pool.wait_ge(s_var, g + 1)
                if after(g, 2):
                    pool.wait_ge(s_norm, g - 1)
                pool.tensor_tensor(scale[:, slot, :], spreads[:, slot, :], half[:, :], ALU.pow).then_inc(s_scale, 1)
                pool.wait_ge(s_scale, g + 1)
                pool.tensor_tensor(shift[:, slot, :], lessmean[:, slot, :], scale[:, slot, :], ALU.mult).then_inc(s_shift, 1)

            def last_products(g, slot, turn):
                pool.wait_ge(s_exp, g + 1)
                pool.wait_ge(s_bases, g + 1)
                if after(g, 2):
                    pool.wait_ge(s_reduced, g - 1)
                products_of(pool, TILES - 2, slot, slot % 2)
                products_of(pool, TILES - 1, slot, slot % 2).then_inc(s_prod_last, 1)

            def add(g, slot, turn):
                if after(g, 4):
                    pool.wait_ge(s_x1, g - 3)
                pool.wait_ge(s_mixed[slot], 16 * (turn + 1))
                pool.wait_ge(s_rows[slot], 16 * (turn + 1))
                pool.tensor_tensor(residual[:, slot, :, :], rows[:, slot, :, :], mixed[:, slot, :, :], ALU.add).then_inc(s_added, 1)
                pool.wait_ge(s_added, 2 * g + 1)
                pool.tensor_tensor(residual[:, slot, :, :], residual[:, slot, :, :], over(b_out[:, :], TILES), ALU.add).then_inc(s_added, 1)

            def add_lone(g, slot, turn):
                pool.wait_ge(s_added, 2 * g + 2)
                pool.wait_ge(s_selfs, g + 1)
                pool.tensor_tensor(residual[:, slot, :, :].rearrange("p j (h d) -> p (j h) d", h=HEADS0),
                                   residual[:, slot, :, :].rearrange("p j (h d) -> p (j h) d", h=HEADS0), spread(lones[:, slot % 2, :], D0), ALU.add).then_inc(s_residual, 1)

            skewed(pool, GN, (scales, 0), (last_products, 3), (add, 2), (add_lone, 3), width=4)

        @block.scalar
        def _(act):
            def normalise(g, slot, turn):
                two = slot % 2
                act.wait_ge(s_shift, g + 1)
                if after(g, 2):
                    act.wait_ge(s_turn, g - 1)
                for k in range(TILES):
                    last = act.activation(normed[:, two, k, :], rows[:, slot, k, :], ACT.Identity,
                                          scale=scale[:, two, k:k + 1], bias=shift[:, two, k:k + 1])
                last.then_inc(s_norm, 1)

            def exponent(g, slot, turn):
                act.wait_ge(s_sub, g + 1)
                act.activation(fold(mix[:, slot % 2, :, :]), fold(mix[:, slot % 2, :, :]), ACT.Exp).then_inc(s_exp, 1)

            def columns(g, slot, turn):
                if after(g, 2):
                    act.wait_ge(s_mix, g - 1)
                act.wait_ge(s_turn, g + 1)
                act.activation(hT[:, slot % 2, :], p_turn[:, :], ACT.Relu).then_inc(s_hT, 1)

            def copy_bases(g, slot, turn):
                act.wait_ge(s_mix, g + 1)
                if after(g, 4):
                    act.wait_ge(s_prod, g - 3)
                    act.wait_ge(s_prod_last, g - 3)
                act.activation(bases[:, slot, :, :], p_bases[:, :, :], ACT.Copy).then_inc(s_bases, 1)

            skewed(act, GN, (exponent, 2), (normalise, 0), (columns, 0), (copy_bases, 0), width=4)

        @block.vector
        def _(v):
            v.memset(ones[:, :], 1.0)
            v.wait_ge(s_weights, 64)
            prep = Chain(v, s_prep, 0)
            prep.start(0)
            order_mix(v, prep, w_mix, w_raw, b_mix, b_raw)
            bf16_parts(prep, v, [b_parts[:, i, 0, :] for i in range(3)], b_mix[:, :], b_rest[:, :])
            for j in range(1, TILES):
                last = v.tensor_copy(b_parts[:, :, j, :], b_parts[:, :, 0, :])
            last.then_inc(s_ready, 1)
            def statistics(g, slot, turn):
                v.wait_ge(s_rows[slot], 16 * (turn + 1))
                if after(g, 1):
                    v.wait_ge(s_moment, 4 * g)
                for k in range(TILES):
                    last = v.bn_stats(stats[:, k, :], rows[:, slot, k, :])
                last.then_inc(s_moment, 1)

            def highest(g, slot, turn):
                v.wait_ge(s_mix, g + 1)
                if after(g, 1):
                    v.wait_ge(s_sub, g)
                v.tensor_reduce(top[:, :], by_head(p_mix[slot % 2][:, :, :]), AX_X, ALU.max).then_inc(s_top, 1)

            def sums(g, slot, turn):
                v.wait_ge(s_moment, 4 * g + 1)
                v.tensor_tensor(tmp[:, 0, :], stats[:, :, 1], stats[:, :, 4], ALU.add)
                v.tensor_tensor(tmp[:, 1, :], stats[:, :, 1], stats[:, :, 4], ALU.subtract)
                v.tensor_tensor(tmp[:, 2, :], stats[:, :, 2], stats[:, :, 5], ALU.add).then_inc(s_moment, 1)

            def shift_down(g, slot, turn):
                two = slot % 2
                v.wait_ge(s_top, g + 1)
                if after(g, 2):
                    v.wait_ge(s_prod, g - 1)
                    v.wait_ge(s_prod_last, g - 1)
                v.tensor_tensor(by_head(mix[:, two, :, :]), by_head(p_mix[two][:, :, :]), spread(top[:, :], MIX), ALU.subtract).then_inc(s_sub, 1)

            def means(g, slot, turn):
                v.wait_ge(s_moment, 4 * g + 2)
                if after(g, 2):
                    v.wait_ge(s_shift, g - 1)
                v.tensor_scalar(lessmean[:, slot % 2, :], tmp[:, 0, :], -0.5, None, ALU.mult)
                v.scalar_tensor_tensor(out=tmp[:, 3, :], in0=tmp[:, 1, :], scalar=0.25, in1=tmp[:, 1, :],
                                       op0=ALU.mult, op1=ALU.mult).then_inc(s_moment, 1)

            def weight_sums(g, slot, turn):
                two = slot % 2
                v.wait_ge(s_exp, g + 1)
                if after(g, 1):
                    v.wait_ge(s_selfs, g)
                v.tensor_reduce(mixsum[:, :], by_head(mix[:, two, :, :]), AX_X, ALU.add)
                v.tensor_reduce(lone[:, 0, :], mix[:, two, :, :].rearrange("p j (h q b) -> p (j h) q b", q=AGGS, b=BASES)[:, :, 2, :],
                                AX_X, ALU.add).then_inc(s_small, 1)

            def variances(g, slot, turn):
                v.wait_ge(s_moment, 4 * g + 3)
                v.scalar_tensor_tensor(out=var[:, slot % 2, :], in0=tmp[:, 2, :], scalar=1.0 / C, in1=tmp[:, 3, :],
                                       op0=ALU.mult, op1=ALU.add).then_inc(s_moment, 1)

            def products(g, slot, turn):
                two = slot % 2
                v.wait_ge(s_bases, g + 1)
                if after(g, 2):
                    v.wait_ge(s_reduced, g - 1)
                products_of(v, 0, slot, two)
                v.wait_ge(s_small, 3 * g + 1)
                v.reciprocal(inverse[:, :], mixsum[:, :])
                v.tensor_tensor(lone[:, 1, :].rearrange("p (j h) -> p j h", j=TILES), lone[:, 0, :].rearrange("p (j h) -> p j h", j=TILES),
                                keep["lonew"][:, :, bass.ds(g, 1)].to_broadcast([P, TILES, HEADS0]), ALU.mult).then_inc(s_small, 1)

            def spread_out(g, slot, turn):
                v.wait_ge(s_moment, 4 * g + 4)
                v.tensor_scalar(spreads[:, slot % 2, :], var[:, slot % 2, :], EPS, None, ALU.add).then_inc(s_var, 1)

            def more_products(g, slot, turn):
                two = slot % 2
                products_of(v, 1, slot, two).then_inc(s_prod, 1)
                if after(g, 2):
                    v.wait_ge(s_residual, g - 1)
                    v.wait_ge(s_part, g - 1)
                v.wait_ge(s_small, 3 * g + 2)
                v.tensor_tensor(selfs[:, two, :].rearrange("p (j h) -> p j h", j=TILES), inverse[:, :].rearrange("p (j h) -> p j h", j=TILES),
                                keep["selfw"][:, :, bass.ds(g, 1)].to_broadcast([P, TILES, HEADS0]), ALU.mult).then_inc(s_small, 1)
                v.tensor_tensor(lones[:, two, :], lone[:, 1, :], inverse[:, :], ALU.mult).then_inc(s_selfs, 1)

            def scale_sums(g, slot, turn):
                two = slot % 2
                v.wait_ge(s_reduced, g + 1)
                v.wait_ge(s_small, 3 * g + 3)
                if after(g, 1):
                    v.wait_ge(s_x1, g)
                v.tensor_tensor(part[:, :, :].rearrange("p j (h d) -> p (j h) d", h=HEADS0),
                                p_out[two][:, :, :].rearrange("p j (h d) -> p (j h) d", h=HEADS0), spread(selfs[:, two, :], D0), ALU.mult).then_inc(s_part, 1)

            def finish(g, slot, turn):
                two = slot % 2
                v.wait_ge(s_part, g + 1)
                v.wait_ge(s_residual, g + 1)
                if after(g, 2):
                    v.wait_ge(s_store[two], 8 * (g - two))
                v.tensor_tensor(x1[:, two, :, :], part[:, :, :], residual[:, slot, :, :], ALU.add).then_inc(s_x1, 1)

            skewed(v, GN, (statistics, 0), (highest, 2), (sums, 0), (scale_sums, 5), (means, 0), (shift_down, 2), (variances, 0), (finish, 5),
                   (spread_out, 0), (weight_sums, 3), (products, 3), (more_products, 3), width=4)

        @block.tensor
        def _(pe):
            ident = keep["ident"]
            pe.wait_ge(s_ready, 1)
            pe.wait_ge(s_three, 48)

            def turns(g, slot, turn):
                pe.wait_ge(s_norm, g + 1)
                if after(g, 1):
                    pe.wait_ge(s_hT, g)
                for k in range(TILES):
                    last = pe.transpose(p_turn[:, k * P:(k + 1) * P], normed[:, slot % 2, k, :], ident[:, :])
                last.then_inc(s_turn, 1)

            def project(g, slot, turn):
                two = slot % 2
                if after(g, 2):
                    pe.wait_ge(s_sub, g - 1)
                pe.matmul(fold(p_mix[two][:, :, :]), ones[:, :], b_three[:, :], start=True, stop=False)
                if after(g, 1):
                    pe.wait_ge(s_bases, g)
                pe.wait_ge(s_hT, g + 1)
                for j in range(TILES):
                    pe.matmul(p_mix[two][:, j, :], hT[:, two, j * P:(j + 1) * P], w_mix[:, :], start=False, stop=(j == TILES - 1))
                    last = pe.matmul(p_bases[:, j, :], hT[:, two, j * P:(j + 1) * P], w_bases[:, :], start=True, stop=True)
                last.then_inc(s_mix, 1)

            def reduce(g, slot, turn):
                two = slot % 2
                pe.wait_ge(s_prod, g + 1)
                pe.wait_ge(s_prod_last, g + 1)
                if after(g, 2):
                    pe.wait_ge(s_part, g - 1)
                for b in range(BASES):
                    last = pe.matmul(fold(p_out[two][:, :, :]), ident[:, :], fold(prod[:, two, b, :, :]), start=(b == 0), stop=(b == BASES - 1))
                last.then_inc(s_reduced, 1)

            skewed(pe, GN, (reduce, 4), (turns, 0), (project, 0), width=4)


def edges1(nc, shape, keep, dram, edge_attr, ln_g, ln_b, wts, biases, We):
    N, E, GE, GN = shape
    K = 2 * TILES
    names = ("k", "v", "q")
    with ExitStack() as ctx:
        m = Scope(nc, ctx, "e1")
        raw = m.sb("raw", [C, 3, C])
        weight = m.sb("weight", [C, 3, C])
        bias_raw = m.sb("bias_raw", [C, 3])
        bias = m.sb("bias", [C, 3])
        norm = m.sb("norm", [C, 2])
        w_edge = m.sb("w_edge", [TILES * EDGE_C, TILES, C])
        heads = m.sb("heads", [C, C])
        gidx = m.sb("gidx", [P, 2, K], I32)
        sidx = m.sb("sidx", [P, 2, TILES], I32)
        rows = m.sb("rows", [P, 2, K, C])
        attr = m.sb("attr", [P, 2, TILES, EDGE_C])
        same = m.sb("same", [P, 2, GROUP])
        barrier = m.sb("barrier", [P, 2, GROUP])
        stats = m.sb("stats", [P, K, 6])
        tmp = m.sb("tmp", [P, 4, K])
        mean = m.sb("mean", [P, K])
        var = m.sb("var", [P, K])
        floor = m.sb("floor", [P, K])
        stats2 = m.sb("stats2", [P, K, 6])
        tmp2 = m.sb("tmp2", [P, 4, K])
        var2 = m.sb("var2", [P, K])
        half = m.sb("half", [P, K])
        lessmean2, spreads, factor, shift = (m.sb(n, [P, 2, K]) for n in ("lessmean2", "spreads", "factor", "shift"))
        rectified = m.sb("rectified", [P, 2, K, C])
        normed = m.sb("normed", [P, 2, K, C])
        xT = m.sb("xT", [P, 2, 2, GROUP])
        attrT = m.sb("attrT", [TILES * EDGE_C, 2, P])
        qT = m.sb("qT", [P, 2, GROUP])
        vT = m.sb("vT", [P, 4, GROUP])
        qk = m.sb("qk", [P, 2, GROUP])
        top = m.sb("top", [P, 2, 1 + GROUP])
        fade = m.sb("fade", [P, GROUP])
        fade2 = m.sb("fade2", [P, 2, GROUP])
        prob = m.sb("prob", [P, 2, GROUP])
        pv = m.sb("pv", [P, GROUP])
        denom = m.sb("denom", [P, 2, GROUP])
        numer = m.sb("numer", [P, 2, GROUP])
        inverse = m.sb("inverse", [P, TILES * HEADS1])
        outrow = m.sb("outrow", [P, 2, TILES, C])
        p_turn = m.ps("turn", [P, 2, GROUP])
        p_k, p_v, p_q = (m.ps(n, [P, GROUP]) for n in names)
        p_score = m.ps("score", [P, GROUP])
        p_numer = m.ps("numer", [P, TILES, C])
        p_denom = m.ps("denom", [P, TILES, C])
        s_weights, s_ready, s_zero = m.sem("weights"), m.sem("ready"), m.sem("zero")
        s_bias, s_const = m.sem("bias"), m.sem("const")
        s_gidx, s_sidx, s_issue = m.sem("gidx"), m.sem("sidx"), m.sem("issue")
        s_rows = [m.sem(f"rows{i}") for i in range(2)]
        s_attr = [m.sem(f"attr{i}") for i in range(2)]
        s_same = [m.sem(f"same{i}") for i in range(2)]
        s_scatter = [m.sem(f"scatter{i}") for i in range(2)]
        s_moment, s_var, s_factor, s_shift, s_norm = (m.sem(n) for n in ("moment", "var", "factor", "shift", "norm"))
        s_turn, s_attrT, s_xT, s_k, s_qv, s_vq, s_qk, s_score = (m.sem(n) for n in ("turn", "attrT", "xT", "k", "qv", "vq", "qk", "score"))
        s_attrp, s_barrier, s_top, s_fade, s_prob, s_faded = (m.sem(n) for n in ("attrp", "barrier", "top", "fade", "prob", "faded"))
        s_pv, s_scan, s_back, s_out = (m.sem(n) for n in ("pv", "scan", "back", "out"))
        s_den, s_tail, s_half = m.sem("den"), m.sem("tail"), m.sem("half")
        full = E // GROUP
        n_load = 3 + 3 + 2 + TILES
        tail_dmas = sum(1 for j in range(TILES) if E - full * GROUP - j * P > 0)
        s_go = m.sem("go")
        block = m.block()

        @block.sync
        def _(sp):
            for i, n in enumerate(names):
                sp.dma_start(raw[:, i, :], wts[n]).then_inc(s_weights, 16)
                sp.dma_start(bias_raw[:, i:i + 1], biases[n].rearrange("(p o) -> p o", o=1)).then_inc(s_weights, 16)
            sp.dma_start(norm[:, 0:1], ln_g.rearrange("(p o) -> p o", o=1)).then_inc(s_weights, 16)
            sp.dma_start(norm[:, 1:2], ln_b.rearrange("(p o) -> p o", o=1)).then_inc(s_weights, 16)
            sp.wait_ge(s_zero, 1)
            for j in range(TILES):
                sp.dma_start(w_edge[j * EDGE_C:(j + 1) * EDGE_C, j, :], We).then_inc(s_weights, 16)

            def load(g, slot, turn):
                if after(g, 2):
                    sp.wait_ge(s_attrp, g - 1)
                    sp.sem_inc(s_go, 1)
                if not isinstance(g, int) or g < full:
                    sp.dma_start(attr[:, slot, :, :], edge_attr[bass.ds(g * GROUP, GROUP), :].rearrange("(j p) c -> p j c", p=P)).then_inc(s_attr[slot], 16)
                else:
                    for j in range(TILES):
                        n = min(P, max(0, E - g * GROUP - j * P))
                        if n:
                            sp.dma_start(attr[0:n, slot, j, :], edge_attr[g * GROUP + j * P:g * GROUP + j * P + n, :]).then_inc(s_tail, 16)
                if after(g, 2):
                    sp.wait_ge(s_barrier, g - 1)
                    sp.sem_inc(s_go, 1)
                sp.dma_start(same[:, slot, :], dram["same"][bass.ds(g, 1), :].to_broadcast([P, GROUP])).then_inc(s_same[slot], 16)

            skewed(sp, GE, (load, 0), peel=2)

        @block.gpsimd
        def _(pool):
            pool.memset(half[:, :], -0.5).then_inc(s_half, 1)
            pool.wait_ge(s_half, 1)

            def gather(g, slot, turn):
                slot %= 2
                if after(g, 2):
                    pool.wait_ge(s_var, g - 1)
                    pool.sem_inc(s_issue, 1)
                pool.tensor_copy(gidx[:, slot, :].rearrange("p (k o) -> p k o", o=1), index_of(keep, GE, (0, 2), g)).then_inc(s_gidx, 1)
                pool.wait_ge(s_gidx, g + 1)
                pool.sem_inc(s_issue, 1)
                for k in range(K):
                    pool.indirect_dma_start(rows[:, slot, k, :], None, dram["x1"], bass.IndirectOffsetOnAxis(ap=gidx[:, slot, k:k + 1], axis=0)).then_inc(s_rows[slot], 16)

            def scales(g, slot, turn):
                slot %= 2
                pool.wait_ge(s_var, g + 1)
                if after(g, 2):
                    pool.wait_ge(s_norm, g - 1)
                pool.tensor_tensor(factor[:, slot, :], spreads[:, slot, :], half[:, :], ALU.pow).then_inc(s_factor, 1)
                pool.wait_ge(s_factor, g + 1)
                pool.tensor_tensor(shift[:, slot, :], lessmean2[:, slot, :], factor[:, slot, :], ALU.mult).then_inc(s_shift, 1)

            def scatter(g, slot, turn):
                turn, slot = turn * 2 + slot // 2, slot % 2
                if after(g, 2):
                    pool.wait_ge(s_scatter[slot], 64 * turn)
                    pool.sem_inc(s_issue, 1)
                pool.tensor_copy(sidx[:, slot, :].rearrange("p (k o) -> p k o", o=1), index_of(keep, GE, (2, 3), g)).then_inc(s_sidx, 1)
                pool.wait_ge(s_sidx, g + 1)
                pool.wait_ge(s_out, g + 1)
                pool.sem_inc(s_issue, 1)
                for k in range(TILES):
                    pool.indirect_dma_start(dram["attended"], bass.IndirectOffsetOnAxis(ap=sidx[:, slot, k:k + 1], axis=0), outrow[:, slot, k, :], None,
                                            bounds_check=N - 1, oob_is_err=False).then_inc(s_scatter[slot], 16)

            skewed(pool, GE, (gather, 0), (scales, 1), (scatter, 5), width=4)
            for i in range(2):
                pool.wait_ge(s_scatter[i], 64 * (GE // 2))

        @block.scalar
        def _(act):
            def normalise(g, slot, turn):
                slot %= 2
                act.wait_ge(s_shift, g + 1)
                if after(g, 2):
                    act.wait_ge(s_turn, g - 1)
                for k in range(K):
                    last = act.activation(normed[:, slot, k, :], rectified[:, slot, k, :], ACT.Identity,
                                          scale=factor[:, slot, k:k + 1], bias=shift[:, slot, k:k + 1])
                last.then_inc(s_norm, 1)

            def barriers(g, slot, turn):
                turn, slot = turn * 2 + slot // 2, slot % 2
                act.wait_ge(s_same[slot], 16 * (turn + 1))
                if after(g, 2):
                    act.wait_ge(s_fade, 2 * (g - 1))
                act.activation(barrier[:, slot, :], same[:, slot, :], ACT.Copy, scale=HUGE, bias=-HUGE).then_inc(s_barrier, 1)

            def columns(g, slot, turn):
                slot %= 2
                if after(g, 2):
                    act.wait_ge(s_qv, g - 1)
                act.wait_ge(s_attrp, g + 1)
                act.activation(attrT[:, slot, :], p_k[0:TILES * EDGE_C, 0:P], ACT.Copy).then_inc(s_attrT, 1)
                act.wait_ge(s_turn, g + 1)
                act.activation(xT[:, slot, :, :], p_turn[:, :, :], ACT.Copy).then_inc(s_xT, 1)

            def query_value(g, slot, turn):
                if after(g, 2):
                    act.wait_ge(s_qk, g - 1)
                if after(g, 4):
                    act.wait_ge(s_pv, g - 3)
                act.wait_ge(s_qv, g + 1)
                act.activation(qT[:, slot % 2, :], p_q[:, :], ACT.Identity, bias=bias[:, 2:3])
                act.activation(vT[:, slot, :], p_v[:, :], ACT.Identity, bias=bias[:, 1:2]).then_inc(s_vq, 1)

            def exponents(g, slot, turn):
                slot %= 2
                act.wait_ge(s_fade, 2 * g + 2)
                act.activation(prob[:, slot, :], prob[:, slot, :], ACT.Exp).then_inc(s_prob, 1)
                act.activation(fade2[:, slot, :], fade2[:, slot, :], ACT.Exp).then_inc(s_faded, 1)

            act.wait_ge(s_bias, 1)
            skewed(act, GE, (columns, 2), (barriers, 2), (exponents, 3), (query_value, 2), (normalise, 1), width=4)

        @block.vector
        def _(v):
            v.memset(w_edge[:, :, :], 0.0)
            v.memset(attr[:, :, :, :], 0.0).then_inc(s_zero, 1)
            v.memset(heads[:, :], 0.0).then_inc(s_const, 1)
            v.memset(top[:, 0, 0:1], 0.0)
            v.wait_ge(s_const, 1)
            for h in range(HEADS1):
                last = v.memset(heads[h * D1:(h + 1) * D1, h * D1:(h + 1) * D1], float(D1) ** -0.5)
            last.then_inc(s_const, 1)
            v.wait_ge(s_weights, 16 * n_load)
            last = v.tensor_scalar(fold(weight[:, :, :]), fold(raw[:, :, :]), norm[:, 0:1], None, ALU.mult)
            last.then_inc(s_ready, 1)
            v.wait_ge(s_ready, 2)
            v.tensor_tensor(bias[:, :], bias_raw[:, :], p_score[:, 0:3], ALU.add).then_inc(s_bias, 1)
            moment = Chain(v, s_moment, 8)

            def first_norms(g, slot, turn):
                turn, slot = turn * 2 + slot // 2, slot % 2
                moment.start(g)
                v.wait_ge(s_rows[slot], 128 * (turn + 1))
                if after(g, 2):
                    v.wait_ge(s_norm, g - 1)
                moments(v, moment, rows[:, slot], stats, tmp, mean[:, :], var[:, :])
                for k in range(K):
                    last = v.tensor_scalar(rectified[:, slot, k, :], rows[:, slot, k, :], mean[:, k:k + 1], 0.0, ALU.subtract, ALU.max)
                moment(last)
                v.tensor_scalar(floor[:, :], var[:, :], EPS, EPS, ALU.add, ALU.mult)
                moment(moments(v, moment, rectified[:, slot], stats2, tmp2, lessmean2[:, slot, :], var2[:, :], less=True))
                v.tensor_tensor(spreads[:, slot, :], floor[:, :], var2[:, :], ALU.add).then_inc(s_var, 1)

            def score(g, slot, turn):
                slot %= 2
                v.wait_ge(s_k, g + 1)
                v.wait_ge(s_vq, g + 1)
                if after(g, 2):
                    v.wait_ge(s_score, g - 1)
                v.scalar_tensor_tensor(out=qk[:, slot, :], in0=p_k[:, :], scalar=bias[:, 0:1], in1=qT[:, slot, :],
                                       op0=ALU.add, op1=ALU.mult).then_inc(s_qk, 1)

            def running_top(g, slot, turn):
                slot %= 2
                first = isinstance(g, int) and g == 0
                v.wait_ge(s_score, g + 1)
                v.wait_ge(s_barrier, g + 1)
                if not first:
                    v.tensor_copy(top[:, slot, 0:1], top[:, 1 - slot, GROUP:GROUP + 1])
                v.tensor_tensor_scan(top[:, slot, 1:GROUP + 1], barrier[:, slot, :], p_score[:, :],
                                     0.0 if first else top[:, 1 - slot, GROUP:GROUP + 1], ALU.add, ALU.max).then_inc(s_top, 1)
                v.wait_ge(s_top, g + 1)
                v.tensor_tensor(fade[:, :], top[:, slot, 0:GROUP], barrier[:, slot, :], ALU.add).then_inc(s_fade, 1)
                v.tensor_tensor(prob[:, slot, :], p_score[:, :], top[:, slot, 1:GROUP + 1], ALU.subtract)
                v.wait_ge(s_fade, 2 * g + 1)
                v.tensor_tensor(fade2[:, slot, :], fade[:, :], top[:, slot, 1:GROUP + 1], ALU.subtract).then_inc(s_fade, 1)

            def accumulate(g, slot, turn):
                four, slot = slot, slot % 2

                def carry(tile):
                    return 0.0 if isinstance(g, int) and g == 0 else tile[:, 1 - slot, GROUP - 1:GROUP]

                v.wait_ge(s_prob, g + 1)
                v.tensor_tensor(pv[:, :], prob[:, slot, :], vT[:, four, :], ALU.mult).then_inc(s_pv, 1)
                v.wait_ge(s_faded, g + 1)
                v.tensor_tensor_scan(denom[:, slot, :], fade2[:, slot, :], prob[:, slot, :], carry(denom), ALU.mult, ALU.add)
                v.wait_ge(s_pv, g + 1)
                v.tensor_tensor_scan(numer[:, slot, :], fade2[:, slot, :], pv[:, :], carry(numer), ALU.mult, ALU.add).then_inc(s_scan, 1)

            def finish(g, slot, turn):
                turn, slot = turn * 2 + slot // 2, slot % 2
                v.wait_ge(s_back, g + 1)
                v.tensor_scalar(inverse[:, :].rearrange("p (j h) -> p j h", j=TILES), p_denom[:, :, 0:C:D1], 1e-16, None, ALU.add).then_inc(s_den, 1)
                v.wait_ge(s_den, 2 * g + 1)
                v.reciprocal(inverse[:, :], inverse[:, :]).then_inc(s_den, 1)
                v.wait_ge(s_den, 2 * g + 2)
                if after(g, 2):
                    v.wait_ge(s_scatter[slot], 64 * turn)
                v.tensor_tensor(outrow[:, slot, :, :].rearrange("p j (h d) -> p (j h) d", h=HEADS1),
                                p_numer[:, :, :].rearrange("p j (h d) -> p (j h) d", h=HEADS1), spread(inverse[:, :], D1), ALU.mult).then_inc(s_out, 1)

            skewed(v, GE, (first_norms, 1), (running_top, 3), (accumulate, 4), (finish, 5), (score, 2), width=4)

        @block.tensor
        def _(pe):
            ident = keep["ident"]
            pe.wait_ge(s_weights, 16 * n_load)
            for i in range(3):
                last = pe.matmul(p_score[:, i:i + 1], raw[:, i, :], norm[:, 1:2], start=True, stop=True)
            last.then_inc(s_ready, 1)
            pe.wait_ge(s_ready, 2)
            pe.wait_ge(s_const, 2)
            pe.wait_ge(s_bias, 1)

            def scores(g, slot, turn):
                slot %= 2
                pe.wait_ge(s_qk, g + 1)
                if after(g, 1):
                    pe.wait_ge(s_fade, 2 * g)
                pe.matmul(p_score[:, :], heads[:, :], qk[:, slot, :], start=True, stop=True).then_inc(s_score, 1)

            def turn_back(g, slot, turn):
                slot %= 2
                pe.wait_ge(s_scan, g + 1)
                if after(g, 1):
                    pe.wait_ge(s_out, g)
                for j in range(TILES):
                    pe.transpose(p_numer[:, j, :], numer[:, slot, j * P:(j + 1) * P], ident[:, :])
                    last = pe.transpose(p_denom[:, j, :], denom[:, slot, j * P:(j + 1) * P], ident[:, :])
                last.then_inc(s_back, 1)

            def turns(g, slot, turn):
                turn, slot = turn * 2 + slot // 2, slot % 2
                if after(g, 1):
                    pe.wait_ge(s_qk, g)
                if isinstance(g, int) and g == full and tail_dmas:
                    pe.wait_ge(s_tail, 16 * tail_dmas)
                elif not isinstance(g, int) or g < full:
                    pe.wait_ge(s_attr[slot], 16 * (turn + 1))
                pe.transpose(p_k[0:TILES * EDGE_C, 0:P], fold(attr[:, slot, :, :]), ident[:, :]).then_inc(s_attrp, 1)
                pe.wait_ge(s_norm, g + 1)
                if after(g, 1):
                    pe.wait_ge(s_xT, g)
                for k in range(K):
                    last = pe.transpose(p_turn[:, k // TILES, (k % TILES) * P:(k % TILES + 1) * P], normed[:, slot, k, :], ident[:, :])
                last.then_inc(s_turn, 1)

            def project(g, slot, turn):
                slot %= 2
                pe.wait_ge(s_attrT, g + 1)
                pe.wait_ge(s_xT, g + 1)
                if after(g, 1):
                    pe.wait_ge(s_qk, g)
                    pe.wait_ge(s_vq, g)
                for i, bank in enumerate((p_k, p_v)):
                    pe.matmul(bank[:, :], weight[:, i, :], xT[:, slot, 0, :], start=True, stop=False)
                    for j in range(TILES):
                        last = pe.matmul(bank[:, j * P:(j + 1) * P], w_edge[:, j, :], attrT[:, slot, :], start=False, stop=(j == TILES - 1))
                last.then_inc(s_k, 1)
                pe.matmul(p_q[:, :], weight[:, 2, :], xT[:, slot, 1, :], start=True, stop=True).then_inc(s_qv, 1)

            skewed(pe, GE, (scores, 3), (turn_back, 5), (turns, 2), (project, 2), peel=2, width=4)


def nodes1(nc, shape, keep, dram, prm, out):
    N, E, GE, GN = shape
    CH = HID // P
    with ExitStack() as ctx:
        m = Scope(nc, ctx, "n1")
        skip_raw = m.sb("skip_raw", [C, C])
        w_skip = m.sb("w_skip", [C, C + 1])
        skip_row = m.sb("skip_row", [1, C])
        b_skip = m.sb("b_skip", [1, C + 1])
        norm = m.sb("norm", [C, 4])
        beta_rows = m.sb("beta_rows", [P, 3, C])
        beta_out = m.sb("beta_out", [P, C])
        beta_skip = m.sb("beta_skip", [P, C])
        scratch = m.sb("scratch", [P, 2, C])
        w1_raw = m.sb("w1_raw", [C, HID])
        w1 = m.sb("w1", [C, HID])
        b1_raw = m.sb("b1_raw", [P, CH])
        b1 = m.sb("b1", [P, CH])
        w2 = m.sb("w2", [P, CH, C])
        b2_row = m.sb("b2_row", [1, C])
        rest = m.sb("rest", [1, 2, C + 1])
        skip_parts = m.sb("skip_parts", [1, 3, 2, C + 1], BF16)
        b2_parts = m.sb("b2_parts", [1, 3, TILES, C], BF16)
        skip_three = m.sb("skip_three", [3, 2 * (C + 1)], BF16)
        b2_three = m.sb("b2_three", [3, TILES * C], BF16)
        ones = m.sb("ones", [3, P], BF16)
        half = m.sb("half", [P, 2 * TILES])
        base = m.sb("base", [P, TILES])
        rows = m.sb("rows", [P, 4, TILES, C])
        attended = m.sb("attended", [P, 4, TILES, C])
        stats = [m.sb(f"stats{i}", [P, TILES, 6]) for i in range(3)]
        tmp = [m.sb(f"tmp{i}", [P, 4, TILES]) for i in range(3)]
        mean, var, var2 = (m.sb(n, [P, 2, TILES]) for n in ("mean", "var", "var2"))
        lessmean2, lessmean3, var3 = (m.sb(n, [P, 2, TILES]) for n in ("lessmean2", "lessmean3", "var3"))
        spreads = m.sb("spreads", [P, 2, 2 * TILES])
        scales = m.sb("scales", [P, 2, 2 * TILES])
        shift2, shift3, scale3 = (m.sb(n, [P, 2, TILES]) for n in ("shift2", "shift3", "scale3"))
        rectified = m.sb("rectified", [P, 2, TILES, C])
        normed = m.sb("normed", [P, 2, TILES, C])
        xT = m.sb("xT", [P, 2, GROUP])
        weighed = m.sb("weighed", [P, 2, TILES, C])
        h1 = m.sb("h1", [P, 2, TILES, C])
        logit = m.sb("logit", [P, 2, TILES])
        gate = m.sb("gate", [P, 2, TILES])
        beta = m.sb("beta", [P, TILES])
        differ = m.sb("differ", [P, TILES, C])
        blend = m.sb("blend", [P, TILES, C])
        inner = m.sb("inner", [P, 4, TILES, C])
        residual = m.sb("residual", [P, 4, TILES, C])
        normed3 = m.sb("normed3", [P, 2, TILES, C])
        x3T = m.sb("x3T", [P, 2, GROUP])
        hidden = m.sb("hidden", [P, CH, GROUP])
        result = m.sb("result", [P, 2, TILES, C])
        p_turn = m.ps("turn", [P, GROUP])
        p_skip = m.ps("skip", [P, 2, GROUP])
        p_turn3 = m.ps("turn3", [P, GROUP])
        p_hid = [m.ps(f"hid{i}", [P, GROUP]) for i in range(2)]
        p_y = [m.ps(f"y{i}", [P, TILES, C]) for i in range(2)]
        s_weights, s_consts, s_prep, s_ready = m.sem("weights"), m.sem("consts"), m.sem("prep"), m.sem("ready")
        s_rows = [m.sem(f"rows{i}") for i in range(4)]
        s_att = [m.sem(f"att{i}") for i in range(4)]
        s_store = [m.sem(f"store{i}") for i in range(2)]
        s_moment, s_moment3, s_var, s_scales, s_shift2, s_norm = (m.sem(n) for n in ("moment", "moment3", "var", "scales", "shift2", "norm"))
        s_turn, s_xT, s_skip, s_weighed, s_h1 = (m.sem(n) for n in ("turn", "xT", "skip", "weighed", "h1"))
        s_logit, s_gate, s_beta, s_blend, s_inner = (m.sem(n) for n in ("logit", "gate", "beta", "blend", "inner"))
        s_residual, s_var3, s_scale3, s_shift3, s_norm3 = (m.sem(n) for n in ("residual", "var3", "scale3", "shift3", "norm3"))
        s_turn3, s_x3T, s_up, s_hidden, s_down, s_result = (m.sem(n) for n in ("turn3", "x3T", "up", "hidden", "down", "result"))
        s_chain, s_three = m.sem("chain"), m.sem("three")
        s_go = m.sem("go")
        block = m.block()

        def skip_tiles(part):
            return p_skip[:, :, 0:2 * (C + 1)].rearrange("p b (k c) -> p b k c", k=2)[:, :, :, part]

        def by_bank(tiles):
            return tiles.rearrange("p (b k) c -> p b k c", b=2)

        @block.sync
        def _(sp):
            def column(vec):
                return vec.rearrange("(p o) -> p o", o=1)

            def row(vec):
                return vec.rearrange("(o n) -> o n", o=1)

            for tile, source in (
                (skip_raw[:, :], prm["Wskip"]), (w1_raw[:, :], prm["W1"]),
                (w2[:, :, :], prm["W2"].rearrange("(k p) c -> p k c", p=P)),
                (norm[:, 0:1], column(prm["ln1_g"])), (norm[:, 1:2], column(prm["ln1_b"])),
                (norm[:, 2:3], column(prm["ln2_g"])), (norm[:, 3:4], column(prm["ln2_b"])),
                (skip_row[:, :], row(prm["bskip"])), (b2_row[:, :], row(prm["b2"])),
            ):
                sp.dma_start(tile, source).then_inc(s_weights, 16)
            for k in range(CH):
                sp.dma_start(b1_raw[:, k:k + 1], column(prm["b1"][k * P:(k + 1) * P])).then_inc(s_weights, 16)
            for k in range(3):
                sp.dma_start(beta_rows[:, k, :], row_of(prm["Wbeta"][k * C:(k + 1) * C, :].rearrange("n o -> (n o)"))).then_inc(s_weights, 16)

            sp.wait_ge(s_ready, 1)
            for i in range(3):
                sp.dma_start(skip_three[i:i + 1, :], fold(skip_parts[:, i, :, :])).then_inc(s_three, 16)
                sp.dma_start(b2_three[i:i + 1, :], fold(b2_parts[:, i, :, :])).then_inc(s_three, 16)

            def load(g, slot, turn):
                if after(g, 4):
                    sp.wait_ge(s_residual, g - 3)
                    sp.sem_inc(s_go, 1)
                sp.dma_start(rows[:, slot, :, :], node_rows(dram["x1"], GN * GROUP, g)[0]).then_inc(s_rows[slot], 16)
                if after(g, 4):
                    sp.wait_ge(s_blend, 2 * (g - 3))
                    sp.sem_inc(s_go, 1)
                    sp.wait_ge(s_weighed, g - 3)
                    sp.sem_inc(s_go, 1)
                sp.dma_start(attended[:, slot, :, :], node_rows(dram["attended"], GN * GROUP, g)[0]).then_inc(s_att[slot], 16)

            def store(g, slot, turn):
                sp.wait_ge(s_result, g + 1)
                sp.sem_inc(s_go, 1)
                target, n = node_rows(out, N, g)
                sp.dma_start(target, result[0:n, slot % 2, :, :]).then_inc(s_store[slot % 2], 16)

            skewed(sp, GN, (load, 0), (store, 8), peel=2, width=4)
            for i in range(2):
                sp.wait_ge(s_store[i], 16 * (GN // 2))

        @block.gpsimd
        def _(pool):
            pool.memset(half[:, :], -0.5)
            pool.memset(base[:, :], INV_E).then_inc(s_consts, 1)
            pool.wait_ge(s_consts, 2)
            pool.wait_ge(s_ready, 1)

            def scale(g, slot, turn):
                slot %= 2
                pool.wait_ge(s_var, g + 1)
                if after(g, 2):
                    pool.wait_ge(s_norm, g - 1)
                pool.tensor_tensor(scales[:, slot, :], spreads[:, slot, :], half[:, :], ALU.pow).then_inc(s_scales, 1)
                pool.wait_ge(s_scales, g + 1)
                pool.tensor_tensor(shift2[:, slot, :], lessmean2[:, slot, :], scales[:, slot, TILES:2 * TILES], ALU.mult).then_inc(s_shift2, 1)

            def gates(g, slot, turn):
                slot %= 2
                pool.wait_ge(s_logit, 2 * g + 2)
                pool.tensor_tensor(gate[:, slot, :], base[:, :], logit[:, slot, :], ALU.pow).then_inc(s_gate, 1)

            def weigh(g, slot, turn):
                pool.wait_ge(s_att[slot], 16 * (turn + 1))
                if after(g, 2):
                    pool.wait_ge(s_logit, 2 * (g - 1))
                pool.tensor_tensor(weighed[:, slot % 2, :, :], attended[:, slot, :, :], over(beta_out[:, :], TILES), ALU.mult).then_inc(s_weighed, 1)

            def first_norm(g, slot, turn):
                slot %= 2
                if after(g, 2):
                    pool.wait_ge(s_inner, g - 1)
                pool.tensor_tensor(h1[:, slot, :, :], rectified[:, slot, :, :], spread(scales[:, slot, 0:TILES], C), ALU.mult).then_inc(s_h1, 1)

            def scale_inner(g, slot, turn):
                slot %= 2
                pool.wait_ge(s_var3, g + 1)
                if after(g, 2):
                    pool.wait_ge(s_norm3, g - 1)
                pool.tensor_tensor(scale3[:, slot, :], var3[:, slot, :], half[:, 0:TILES], ALU.pow).then_inc(s_scale3, 1)
                pool.wait_ge(s_scale3, g + 1)
                pool.tensor_tensor(shift3[:, slot, :], lessmean3[:, slot, :], scale3[:, slot, :], ALU.mult).then_inc(s_shift3, 1)

            def add(g, slot, turn):
                pool.wait_ge(s_inner, g + 1)
                if after(g, 4):
                    pool.wait_ge(s_result, g - 3)
                pool.tensor_tensor(residual[:, slot, :, :], rows[:, slot, :, :], inner[:, slot, :, :], ALU.add).then_inc(s_residual, 1)

            skewed(pool, GN, (gates, 2), (weigh, 1), (first_norm, 1), (scale, 0), (scale_inner, 3), (add, 2), width=4)

        @block.scalar
        def _(act):
            def normalise3(g, slot, turn):
                two = slot % 2
                act.wait_ge(s_shift3, g + 1)
                if after(g, 2):
                    act.wait_ge(s_turn3, g - 1)
                for k in range(TILES):
                    last = act.activation(normed3[:, two, k, :], inner[:, slot, k, :], ACT.Identity,
                                          scale=scale3[:, two, k:k + 1], bias=shift3[:, two, k:k + 1])
                last.then_inc(s_norm3, 1)

            def columns3(g, slot, turn):
                if after(g, 2):
                    act.wait_ge(s_up, CH * (g - 1))
                act.wait_ge(s_turn3, g + 1)
                act.activation(x3T[:, slot % 2, :], p_turn3[:, :], ACT.Copy).then_inc(s_x3T, 1)

            def relu(g, k):
                if after(g, 1):
                    act.wait_ge(s_down, CH * (g - 1) + k + 1)
                act.wait_ge(s_up, CH * g + k + 1)
                act.activation(hidden[:, k, :], p_hid[k % 2][:, :], ACT.Relu, bias=b1[:, k:k + 1]).then_inc(s_hidden, 1)

            def relus_first(g, slot, turn):
                relu(g, 0)
                relu(g, 1)

            def normalise(g, slot, turn):
                slot %= 2
                act.wait_ge(s_shift2, g + 1)
                if after(g, 2):
                    act.wait_ge(s_turn, g - 1)
                for k in range(TILES):
                    last = act.activation(normed[:, slot, k, :], rectified[:, slot, k, :], ACT.Identity,
                                          scale=scales[:, slot, TILES + k:TILES + k + 1], bias=shift2[:, slot, k:k + 1])
                last.then_inc(s_norm, 1)

            def columns(g, slot, turn):
                if after(g, 2):
                    act.wait_ge(s_skip, g - 1)
                act.wait_ge(s_turn, g + 1)
                act.activation(xT[:, slot % 2, :], p_turn[:, :], ACT.Copy).then_inc(s_xT, 1)

            def relu_third(g, slot, turn):
                relu(g, 2)

            def relu_last(g, slot, turn):
                relu(g, 3)

            act.wait_ge(s_ready, 1)
            skewed(act, GN, (relus_first, 5), (columns, 1), (normalise3, 4), (relu_third, 5), (columns3, 4), (relu_last, 5), (normalise, 0), width=4)

        @block.vector
        def _(v):
            done = [0]

            def chain(instruction):
                done[0] += 1
                instruction.then_inc(s_chain, 1)
                v.wait_ge(s_chain, done[0])

            v.memset(ones[:, :], 1.0).then_inc(s_consts, 1)
            v.wait_ge(s_weights, 16 * (9 + CH + 3))
            v.tensor_scalar(w1[:, :], w1_raw[:, :], norm[:, 2:3], None, ALU.mult)
            v.tensor_tensor(beta_out[:, :], beta_rows[:, 0, :], beta_rows[:, 2, :], ALU.add)
            v.tensor_tensor(beta_skip[:, :], beta_rows[:, 1, :], beta_rows[:, 2, :], ALU.subtract)
            chain(v.tensor_scalar(w_skip[:, 0:C], skip_raw[:, :], norm[:, 0:1], None, ALU.mult))
            v.wait_ge(s_prep, 1)
            v.tensor_tensor(b1[:, :], b1_raw[:, :], p_hid[0][:, 0:CH], ALU.add)
            chain(v.tensor_tensor(b_skip[:, 0:C], skip_row[:, :], p_turn[0:1, 0:C], ALU.add))
            v.tensor_tensor(scratch[:, 0, :], w_skip[:, 0:C], beta_skip[:, :], ALU.mult)
            chain(v.tensor_tensor(scratch[0:1, 1, :], b_skip[:, 0:C], beta_skip[0:1, :], ALU.mult))
            v.tensor_reduce(w_skip[:, C:C + 1], scratch[:, 0, :], AX_X, ALU.add)
            chain(v.tensor_reduce(b_skip[:, C:C + 1], scratch[0:1, 1, :], AX_X, ALU.add))
            bf16_parts(chain, v, [skip_parts[:, i, 0, :] for i in range(3)], b_skip[:, :], rest[:, 0, :])
            bf16_parts(chain, v, [b2_parts[:, i, 0, :] for i in range(3)], b2_row[:, :], rest[:, 1, 0:C])
            for i in range(3):
                v.tensor_copy(skip_parts[:, i, 1, :], skip_parts[:, i, 0, :])
                for j in range(1, TILES):
                    last = v.tensor_copy(b2_parts[:, i, j, :], b2_parts[:, i, 0, :])
            last.then_inc(s_ready, 1)
            moment, rest_of, moment3 = Moments(v, s_moment, 8, 0), Moments(v, s_moment, 8, 4), Moments(v, s_moment3, 4, 0)

            def row_stats(g, slot, turn):
                v.wait_ge(s_rows[slot], 16 * (turn + 1))
                if after(g, 1):
                    v.wait_ge(s_moment, 8 * g)
                moment.stats(g, rows[:, slot], stats[0])

            def row_sums(g, slot, turn):
                moment.sums(g, stats[0], tmp[0])

            def row_means(g, slot, turn):
                if after(g, 2):
                    v.wait_ge(s_shift2, g - 1)
                moment.mean(g, tmp[0], mean[:, slot % 2, :], 0.5)

            def rectify(g, slot, turn):
                two = slot % 2
                if after(g, 2):
                    v.wait_ge(s_norm, g - 1)
                    v.wait_ge(s_h1, g - 1)
                v.wait_ge(s_moment, 8 * g + 3)
                moment.variance(tmp[0], var[:, two, :])
                for k in range(TILES):
                    last = v.tensor_scalar(rectified[:, two, k, :], rows[:, slot, k, :], mean[:, two, k:k + 1], 0.0, ALU.subtract, ALU.max)
                last.then_inc(s_moment, 1)

            def rectified_stats(g, slot, turn):
                two = slot % 2
                v.wait_ge(s_moment, 8 * g + 4)
                v.tensor_scalar(spreads[:, two, 0:TILES], var[:, two, :], EPS, None, ALU.add)
                rest_of.stats(g, rectified[:, two], stats[1])

            def rectified_sums(g, slot, turn):
                rest_of.sums(g, stats[1], tmp[1])

            def rectified_means(g, slot, turn):
                rest_of.mean(g, tmp[1], lessmean2[:, slot % 2, :], -0.5)

            def rectified_variances(g, slot, turn):
                v.wait_ge(s_moment, 8 * g + 7)
                rest_of.variance(tmp[1], var2[:, slot % 2, :]).then_inc(s_moment, 1)

            def both_spreads(g, slot, turn):
                two = slot % 2
                v.wait_ge(s_moment, 8 * g + 8)
                v.scalar_tensor_tensor(out=spreads[:, two, TILES:2 * TILES], in0=spreads[:, two, 0:TILES], scalar=EPS, in1=var2[:, two, :],
                                       op0=ALU.mult, op1=ALU.add).then_inc(s_var, 1)

            def own_logits(g, slot, turn):
                two = slot % 2
                v.wait_ge(s_weighed, g + 1)
                v.tensor_reduce(logit[:, two, :], weighed[:, two, :, :], AX_X, ALU.add).then_inc(s_logit, 1)

            def logits(g, slot, turn):
                two = slot % 2
                v.wait_ge(s_logit, 2 * g + 1)
                v.wait_ge(s_skip, g + 1)
                v.tensor_tensor(logit[:, two, :].rearrange("p (b k) -> p b k", b=2), skip_tiles(C),
                                logit[:, two, :].rearrange("p (b k) -> p b k", b=2), ALU.add).then_inc(s_logit, 1)
                v.tensor_tensor(by_bank(differ[:, :, :]), skip_tiles(slice(0, C)), by_bank(attended[:, slot, :, :]), ALU.subtract).then_inc(s_blend, 1)

            def finish(g, slot, turn):
                two = slot % 2
                v.wait_ge(s_down, CH * (g + 1))
                v.wait_ge(s_residual, g + 1)
                if after(g, 2):
                    v.wait_ge(s_store[two], 8 * (g - two))
                v.tensor_tensor(result[:, two, :, :], p_y[two][:, :, :], residual[:, slot, :, :], ALU.add).then_inc(s_result, 1)

            def betas(g, slot, turn):
                v.wait_ge(s_gate, g + 1)
                v.tensor_scalar(beta[:, :], gate[:, slot % 2, :], 1.0, None, ALU.add).then_inc(s_beta, 1)

            def inverted(g, slot, turn):
                v.wait_ge(s_beta, 2 * g + 1)
                v.reciprocal(beta[:, :], beta[:, :]).then_inc(s_beta, 1)

            def blends(g, slot, turn):
                v.wait_ge(s_beta, 2 * g + 2)
                v.wait_ge(s_blend, 2 * g + 1)
                for k in range(TILES):
                    last = v.scalar_tensor_tensor(out=blend[:, k, :], in0=differ[:, k, :], scalar=beta[:, k:k + 1], in1=attended[:, slot, k, :],
                                                  op0=ALU.mult, op1=ALU.add)
                last.then_inc(s_blend, 1)

            def inners(g, slot, turn):
                v.wait_ge(s_blend, 2 * g + 2)
                v.wait_ge(s_h1, g + 1)
                if after(g, 4):
                    v.wait_ge(s_residual, g - 3)
                    v.wait_ge(s_norm3, g - 3)
                v.tensor_tensor(inner[:, slot, :, :], blend[:, :, :], h1[:, slot % 2, :, :], ALU.add).then_inc(s_inner, 1)

            def inner_stats(g, slot, turn):
                v.wait_ge(s_inner, g + 1)
                if after(g, 1):
                    v.wait_ge(s_var3, g)
                moment3.stats(g, inner[:, slot], stats[2])

            def inner_sums(g, slot, turn):
                moment3.sums(g, stats[2], tmp[2])

            def inner_means(g, slot, turn):
                if after(g, 2):
                    v.wait_ge(s_shift3, g - 1)
                moment3.mean(g, tmp[2], lessmean3[:, slot % 2, :], -0.5)

            def inner_variances(g, slot, turn):
                v.wait_ge(s_moment3, 4 * g + 3)
                moment3.variance(tmp[2], var3[:, slot % 2, :]).then_inc(s_moment3, 1)

            def inner_spreads(g, slot, turn):
                v.wait_ge(s_moment3, 4 * g + 4)
                v.tensor_scalar(var3[:, slot % 2, :], var3[:, slot % 2, :], EPS, None, ALU.add).then_inc(s_var3, 1)

            skewed(v, GN, (own_logits, 2), (row_stats, 0), (logits, 2), (row_sums, 0), (inner_stats, 3), (row_means, 0),
                   (rectify, 0), (inner_sums, 3), (rectified_stats, 0), (inner_means, 3), (betas, 2), (rectified_sums, 0), (inverted, 2),
                   (inner_variances, 3), (rectified_means, 0), (blends, 2), (rectified_variances, 0), (inner_spreads, 3), (finish, 6), (inners, 2),
                   (both_spreads, 0), width=4)

        @block.tensor
        def _(pe):
            ident = keep["ident"]
            pe.wait_ge(s_weights, 16 * (9 + CH + 3))
            pe.matmul(p_turn[0:1, 0:C], norm[:, 1:2], skip_raw[:, :], start=True, stop=True)
            for k in range(CH):
                last = pe.matmul(p_hid[0][:, k:k + 1], w1_raw[:, k * P:(k + 1) * P], norm[:, 3:4], start=True, stop=True)
            last.then_inc(s_prep, 1)
            pe.wait_ge(s_consts, 2)
            pe.wait_ge(s_three, 96)

            def turns3(g, slot, turn):
                pe.wait_ge(s_norm3, g + 1)
                if after(g, 1):
                    pe.wait_ge(s_x3T, g)
                for k in range(TILES):
                    last = pe.transpose(p_turn3[:, k * P:(k + 1) * P], normed3[:, slot % 2, k, :], ident[:, :])
                last.then_inc(s_turn3, 1)

            def up(g, slot, k):
                if after(g, 1) or k >= 2:
                    pe.wait_ge(s_hidden, CH * g + k - 1)
                pe.matmul(p_hid[k % 2][:, :], w1[:, k * P:(k + 1) * P], x3T[:, slot % 2, :], start=True, stop=True).then_inc(s_up, 1)

            def down(g, slot, k):
                pe.wait_ge(s_hidden, CH * g + k + 1)
                for j in range(TILES):
                    last = pe.matmul(p_y[slot % 2][:, j, :], hidden[:, k, j * P:(j + 1) * P], w2[:, k, :], start=False, stop=(k == CH - 1 and j == TILES - 1))
                last.then_inc(s_down, 1)

            def ups_first(g, slot, turn):
                if after(g, 2):
                    pe.wait_ge(s_result, g - 1)
                pe.matmul(fold(p_y[slot % 2][:, :, :]), ones[:, :], b2_three[:, :], start=True, stop=False)
                pe.wait_ge(s_x3T, g + 1)
                up(g, slot, 0)
                up(g, slot, 1)

            def down_first(g, slot, turn):
                down(g, slot, 0)
                up(g, slot, 2)

            def down_second(g, slot, turn):
                down(g, slot, 1)

            def turns(g, slot, turn):
                pe.wait_ge(s_norm, g + 1)
                if after(g, 1):
                    pe.wait_ge(s_xT, g)
                for k in range(TILES):
                    last = pe.transpose(p_turn[:, k * P:(k + 1) * P], normed[:, slot % 2, k, :], ident[:, :])
                last.then_inc(s_turn, 1)

            def mlp_last(g, slot, turn):
                up(g, slot, 3)
                down(g, slot, 2)
                down(g, slot, 3)

            def skips(g, slot, turn):
                if after(g, 1):
                    pe.wait_ge(s_blend, 2 * g - 1)
                    pe.wait_ge(s_logit, 2 * g)
                for b in range(2):
                    pe.matmul(p_skip[:, b, 0:2 * (C + 1)], ones[:, :], skip_three[:, :], start=True, stop=False)
                pe.wait_ge(s_xT, g + 1)
                for j in range(TILES):
                    last = pe.matmul(p_skip[:, j // 2, (j % 2) * (C + 1):(j % 2 + 1) * (C + 1)], xT[:, slot % 2, j * P:(j + 1) * P], w_skip[:, :],
                                     start=False, stop=(j % 2 == 1))
                last.then_inc(s_skip, 1)

            skewed(pe, GN, (ups_first, 5), (turns, 1), (down_first, 5), (skips, 1), (down_second, 5), (turns3, 4), (mlp_last, 5), width=4)


def build(nc, a, out):
    N, E = a["x"].shape[0], a["src"].shape[0]
    GE, GN = -(-E // GROUP), -(-N // GROUP)
    assert N % TILES == 0 and GE % 2 == 0 and GN % 2 == 0 and GE <= P and GN <= 2 * P
    shape = (N, E, GE, GN)
    dram = {name: nc.dram_tensor(name, dims, F32).ap() for name, dims in (
        ("mixed", (GN * GROUP, C)), ("attended", (GN * GROUP, C)), ("x1", (GN * GROUP, C)),
        ("same", (GE, GROUP)), ("factor", (GE, 2, GROUP)), ("dinv", (GN * GROUP, 1)))}
    with ExitStack() as ctx:
        def sb(name, dims, dt=F32):
            return ctx.enter_context(nc.sbuf_tensor(name, dims, dt))

        keep = dict(ident=sb("ident", [P, P]), eps=sb("eps", [P, 1]), one=sb("one", [P, 1]),
                    index=sb("index", [P, 3, TILES * GE], I32),
                    selfw=sb("selfw", [P, TILES, GN]), lonew=sb("lonew", [P, TILES, GN]))
        prepare(nc, shape, keep, dram, a["src"], a["dst"])
        edges0(nc, shape, keep, dram, a["x"], a["L0_gnn_bases_W"], a["L0_gnn_comb_W"], a["L0_gnn_comb_b"])
        nodes0(nc, shape, keep, dram, a["x"], a["L0_gnn_bases_W"], a["L0_gnn_comb_W"], a["L0_gnn_comb_b"], a["L0_gnn_bias"])
        prm = {n[len("L1_gnn_"):]: v for n, v in a.items() if n.startswith("L1_gnn_")}
        edges1(nc, shape, keep, dram, a["edge_attr_4"], prm["ln1_g"], prm["ln1_b"],
               {"k": prm["Wk"], "v": prm["Wv"], "q": prm["Wq"]}, {"k": prm["bk"], "v": prm["bv"], "q": prm["bq"]}, prm["We"])
        nodes1(nc, shape, keep, dram, prm, out)


def kernel(**inputs):
    import numpy as np
    import concourse.bacc as bacc
    from concourse.bass_utils import run_bass_kernel_spmd

    nc = bacc.Bacc("TRN2", target_bir_lowering=False, num_devices=1)
    arrays, views = {}, {}
    for name, value in inputs.items():
        array = np.ascontiguousarray(value)
        arrays[f"in_{name}"] = array
        views[name] = nc.dram_tensor(f"in_{name}", array.shape, mybir.dt.from_np(array.dtype), kind="ExternalInput").ap()
    out = nc.dram_tensor("out_x", tuple(inputs["x"].shape), F32, kind="ExternalOutput").ap()
    build(nc, views, out)
    result = run_bass_kernel_spmd(nc, [arrays], core_ids=[0])
    return result.results[0]["out_x"]
```
